# Optimizing a Trainium2 kernel written in Bass

```python
import numpy as np
import jax
import jax.numpy as jnp

def _softmax(x, axis=-1):
    return jax.nn.softmax(x, axis=axis)

def _gelu(x):
    return jax.nn.gelu(x, approximate=True)

def _silu(x):
    return jax.nn.silu(x)

def _sigmoid(x):
    return jax.nn.sigmoid(x)

def _layernorm(x, axis=-1, eps=1e-05):
    m = jnp.mean(x, axis=axis, keepdims=True)
    v = jnp.var(x, axis=axis, keepdims=True)
    return (x - m) / jnp.sqrt(v + eps)

def _scatter_add(tgt, idx, src, axis=0):
    return tgt.at[idx].add(src)

def _segment_sum(src, seg, n):
    return jax.ops.segment_sum(src, seg, n)
kernel_name = 'mk_perceiver_d2_seqx_r4_b8f390'

def setup_inputs(seed: int=0):
    np.random.seed(seed)
    _w = jnp.asarray

    def _rec_inputs():
        import jax
        import jax.numpy as jnp
        _rk = jax.random.key(seed)
        x = -0.0003929 + 0.9999 * jax.random.normal(jax.random.fold_in(_rk, 1), (16, 64, 256), jnp.float32)
        _lenS = 64 - jax.random.randint(jax.random.fold_in(_rk, 7), (16,), 0, max(1, 64 // 4) + 1, jnp.int32)
        _lenS2 = 1601 - jax.random.randint(jax.random.fold_in(_rk, 8), (16,), 0, max(1, 1601 // 4) + 1, jnp.int32)
        _ctx_1024P = jax.random.normal(jax.random.fold_in(_rk, 11), (16, 16, 256), jnp.float32)
        _ctx_1024c = jax.random.dirichlet(jax.random.fold_in(_rk, 511), 0.3 * jnp.ones((16,), jnp.float32), (16, 1601))
        _ctx_1024t = jnp.einsum('bsk,bkd->bsd', _ctx_1024c, _ctx_1024P)
        _ctx_1024t = _ctx_1024t * jax.lax.rsqrt(jnp.mean(jnp.square(_ctx_1024t)) + 1e-12) * 0.953939
        ctx_1024 = 2.81802e-05 + 1.00001 * (_ctx_1024t + 0.3 * jax.random.normal(jax.random.fold_in(_rk, 611), (16, 1601, 256), jnp.float32))
        _validS = jnp.arange(64)[None, :] < _lenS[:, None]
        _validS2 = jnp.arange(1601)[None, :] < _lenS2[:, None]
        _causal = jnp.tril(jnp.ones((64, 64), dtype=bool))
        mask_BxS_ik1 = jnp.where(jnp.broadcast_to(_validS[:, :], (16, 64)), 1, 0).astype(jnp.int32)
        return (x, ctx_1024, mask_BxS_ik1)
    x, ctx_1024, mask_BxS_ik1 = _rec_inputs()

    def _L0_xattn_setup():
        import jax, jax.numpy as jnp
        import numpy as np
        HID_DIM = 256
        B, S = (8, 512)
        SCALE = float(np.sqrt(HID_DIM))
        NEG = -10000000000.0
        key = jax.random.key(seed)
        ks = jax.random.split(key, 13)
        d = HID_DIM
        std = 1.0 / np.sqrt(d)
        return {'query': jax.random.normal(ks[0], (B, S, d), jnp.float32), 'key_': jax.random.normal(ks[1], (B, S, d), jnp.float32), 'value': jax.random.normal(ks[2], (B, S, d), jnp.float32), 'mask': jax.random.randint(ks[3], (B, S), 0, 2, jnp.int32), 'Wq': jax.random.uniform(ks[4], (d, d), jnp.float32, -std, std), 'bq': jax.random.uniform(ks[5], (d,), jnp.float32, -std, std), 'Wk': jax.random.uniform(ks[6], (d, d), jnp.float32, -std, std), 'bk': jax.random.uniform(ks[7], (d,), jnp.float32, -std, std), 'Wv': jax.random.uniform(ks[8], (d, d), jnp.float32, -std, std), 'bv': jax.random.uniform(ks[9], (d,), jnp.float32, -std, std), 'Wfc': jax.random.uniform(ks[10], (d, d), jnp.float32, -std, std), 'bfc': jax.random.uniform(ks[11], (d,), jnp.float32, -std, std)}
    _L0_xattn_all = _L0_xattn_setup()
    _L0_xattn_in = {k: v for k, v in _L0_xattn_all.items() if k in ('Wq', 'bq', 'Wk', 'bk', 'Wv', 'bv', 'Wfc', 'bfc')}
    del _L0_xattn_all

    def _L0_attn_setup():
        import jax, jax.numpy as jnp
        import numpy as np
        B, T, D = (2, 512, 256)
        H = 16
        HD = D // H
        DL = 128
        NR = 64
        EPS = 1.1920929e-07

        def _rms_norm(x, w):
            ms = jnp.mean(jnp.square(x), axis=-1, keepdims=True)
            return x * jax.lax.rsqrt(ms + EPS) * w
        key = jax.random.key(seed)
        ks = jax.random.split(key, 10)
        s = 0.02
        return {'x': jax.random.normal(ks[0], (B, T, D), dtype=jnp.float32), 'W_DQ': jax.random.normal(ks[1], (DL, HD), dtype=jnp.float32) * s, 'W_UQ': jax.random.normal(ks[2], (HD, DL), dtype=jnp.float32) * s, 'W_DKV': jax.random.normal(ks[3], (2 * DL, HD), dtype=jnp.float32) * s, 'W_UKV': jax.random.normal(ks[4], (2 * HD, 2 * DL), dtype=jnp.float32) * s, 'W_QR': jax.random.normal(ks[5], (NR, HD), dtype=jnp.float32) * s, 'W_KR': jax.random.normal(ks[6], (NR, HD), dtype=jnp.float32) * s, 'W_O': jax.random.normal(ks[7], (HD, HD), dtype=jnp.float32) * s, 'q_norm_w': jnp.ones((HD,), dtype=jnp.float32), 'k_norm_w': jnp.ones((HD,), dtype=jnp.float32)}
    _L0_attn_all = _L0_attn_setup()
    _L0_attn_in = {k: v for k, v in _L0_attn_all.items() if k in ('W_DQ', 'W_UQ', 'W_DKV', 'W_UKV', 'W_QR', 'W_KR', 'W_O', 'q_norm_w', 'k_norm_w')}
    del _L0_attn_all

    def _L0_ffn_setup():
        import math
        import jax, jax.numpy as jnp
        import numpy as np
        D_CONTENT = 256
        D_POSITION = 32
        NUM_TILES = 8
        BATCH = 8
        SEQ = 512

        def make_pe(seq_len, d_pos):
            pos = jnp.arange(seq_len, dtype=jnp.float32)[:, None]
            div = jnp.exp(jnp.arange(0, d_pos, 2, dtype=jnp.float32) * (-math.log(10000.0) / d_pos))
            ang = pos * div
            pe = jnp.zeros((seq_len, d_pos), dtype=jnp.float32)
            pe = pe.at[:, 0::2].set(jnp.sin(ang))
            pe = pe.at[:, 1::2].set(jnp.cos(ang))
            return pe
        key = jax.random.key(seed)
        k1, k2, k3, k4 = jax.random.split(key, 4)
        x = jax.random.normal(k1, (BATCH, SEQ, D_CONTENT), dtype=jnp.float32)
        tile_sigs = jax.random.normal(k2, (NUM_TILES, D_POSITION), dtype=jnp.float32)
        lim = 1.0 / math.sqrt(D_CONTENT)
        W = jax.random.uniform(k3, (NUM_TILES, D_CONTENT, D_CONTENT), minval=-lim, maxval=lim, dtype=jnp.float32)
        b = jax.random.uniform(k4, (NUM_TILES, D_CONTENT), minval=-lim, maxval=lim, dtype=jnp.float32)
        return {'x': x, 'tile_sigs': tile_sigs, 'W': W, 'b': b}
    _L0_ffn_all = _L0_ffn_setup()
    _L0_ffn_in = {k: v for k, v in _L0_ffn_all.items() if k in ('tile_sigs', 'W', 'b')}
    del _L0_ffn_all

    def _L1_xattn_setup():
        import jax, jax.numpy as jnp
        import numpy as np
        B, S, D_IN, D_MODEL = (4, 512, 256, 256)
        key = jax.random.key(seed)
        ks = jax.random.split(key, 9)
        return {'q': jax.random.normal(ks[0], (B, S, D_IN), jnp.float32), 'k': jax.random.normal(ks[1], (B, S, D_IN), jnp.float32), 'v': jax.random.normal(ks[2], (B, S, D_IN), jnp.float32), 'Wq': jax.random.normal(ks[3], (D_IN, D_MODEL), jnp.float32) * 0.02, 'bq': jax.random.normal(ks[4], (D_MODEL,), jnp.float32) * 0.02, 'Wk': jax.random.normal(ks[5], (D_IN, D_MODEL), jnp.float32) * 0.02, 'bk': jax.random.normal(ks[6], (D_MODEL,), jnp.float32) * 0.02, 'Wv': jax.random.normal(ks[7], (D_IN, D_MODEL), jnp.float32) * 0.02, 'bv': jax.random.normal(ks[8], (D_MODEL,), jnp.float32) * 0.02}
    _L1_xattn_all = _L1_xattn_setup()
    _L1_xattn_in = {k: v for k, v in _L1_xattn_all.items() if k in ('Wq', 'bq', 'Wk', 'bk', 'Wv', 'bv')}
    del _L1_xattn_all

    def _L1_attn_setup():
        import jax, jax.numpy as jnp
        import numpy as np
        import math
        D_MODEL = 256
        D_STATE = 64
        EXPAND = 2
        D_CONV = 4
        D_INNER = D_MODEL * EXPAND
        NHEADS = D_INNER // D_STATE
        HEADDIM = D_INNER // NHEADS
        D_PROJ = 2 * D_INNER + NHEADS * (2 * D_STATE + 1)
        BATCH, SEQLEN = (2, 256)

        def _ssm_forward(x, W_in, conv_w, conv_b, A_log, D, dt_bias, W_out):
            B, L, _ = x.shape
            d, n, s = (D_INNER, NHEADS, D_STATE)
            proj = x @ W_in.T
            x_inner = proj[..., :d]
            z = proj[..., d:2 * d]
            bc_dt = proj[..., 2 * d:].reshape(B, L, n, 2 * s + 1)
            B_proj = bc_dt[..., :s]
            C_proj = bc_dt[..., s:2 * s]
            dt_proj = bc_dt[..., 2 * s]
            xc = jax.lax.conv_general_dilated(jnp.transpose(x_inner, (0, 2, 1)), conv_w, window_strides=(1,), padding=[(D_CONV - 1, 0)], feature_group_count=d, dimension_numbers=('NCH', 'OIH', 'NCH'))
            xc = xc + conv_b[None, :, None]
            x_conv = jax.nn.silu(jnp.transpose(xc, (0, 2, 1)))
            x_heads = x_conv.reshape(B, L, n, HEADDIM)
            A = -jnp.exp(A_log)
            dt = jax.nn.softplus(dt_proj + dt_bias)
            dA = jnp.exp(A[None, None] * dt[..., None])
            dB = B_proj * dt[..., None]

            def step(h, inp):
                dA_t, dB_t, C_t, x_t = inp
                h = dA_t[..., None] * h + dB_t[..., None] * x_t[:, :, None, :]
                y_t = jnp.einsum('bns,bnsd->bnd', C_t, h)
                return (h, y_t)
            h0 = jnp.zeros((B, n, s, HEADDIM), dtype=x.dtype)
            xs = (jnp.moveaxis(dA, 1, 0), jnp.moveaxis(dB, 1, 0), jnp.moveaxis(C_proj, 1, 0), jnp.moveaxis(x_heads, 1, 0))
            _, y_scan = jax.lax.scan(step, h0, xs)
            y_heads = jnp.moveaxis(y_scan, 0, 1)
            y_heads = y_heads + D[None, None, :, None] * x_heads
            y = y_heads.reshape(B, L, d) * jax.nn.silu(z)
            return y @ W_out.T
        key = jax.random.key(seed)
        ks = jax.random.split(key, 6)
        x = jax.random.normal(ks[0], (BATCH, SEQLEN, D_MODEL), dtype=jnp.float32)
        W_in = jax.random.normal(ks[1], (D_PROJ, D_MODEL), dtype=jnp.float32) * 0.02
        conv_w = jax.random.normal(ks[2], (D_INNER, 1, D_CONV), dtype=jnp.float32) * (1.0 / math.sqrt(D_CONV))
        conv_b = jnp.zeros((D_INNER,), dtype=jnp.float32)
        A_log = jnp.tile(jnp.log(jnp.arange(1, D_STATE + 1, dtype=jnp.float32))[None, :], (NHEADS, 1))
        D = jnp.ones((NHEADS,), dtype=jnp.float32)
        u = jax.random.uniform(ks[3], (NHEADS,), dtype=jnp.float32)
        dt_bias = u * (math.log(0.1) - math.log(0.001)) + math.log(0.001)
        W_out = jax.random.normal(ks[4], (D_MODEL, D_INNER), dtype=jnp.float32) * (0.02 / math.sqrt(2))
        return {'x': x, 'W_in': W_in, 'conv_w': conv_w, 'conv_b': conv_b, 'A_log': A_log, 'D': D, 'dt_bias': dt_bias, 'W_out': W_out}
    _L1_attn_all = _L1_attn_setup()
    _L1_attn_in = {k: v for k, v in _L1_attn_all.items() if k in ('W_in', 'conv_w', 'conv_b', 'A_log', 'D', 'dt_bias', 'W_out')}
    del _L1_attn_all

    def _L1_ffn_setup():
        import jax, jax.numpy as jnp
        import numpy as np
        B, S, H = (2, 512, 256)
        E, F, K = (64, 128, 8)
        G, TG = (8, 4)
        SCALE = 2.5
        F_SH = 128

        def _gate(x, gate_w, gate_bias):
            scores = jax.nn.sigmoid(x @ gate_w.T)
            sc = scores + gate_bias[None, :]
            T = x.shape[0]
            group_scores = jax.lax.top_k(sc.reshape(T, G, E // G), 2)[0].sum(-1)
            _, gidx = jax.lax.top_k(group_scores, TG)
            gmask = jnp.zeros((T, G), sc.dtype).at[jnp.arange(T)[:, None], gidx].set(1.0)
            smask = jnp.repeat(gmask, E // G, axis=1)
            masked = jnp.where(smask > 0, sc, -jnp.inf)
            _, tidx = jax.lax.top_k(masked, K)
            tw = jnp.take_along_axis(scores, tidx, axis=1)
            tw = tw / (tw.sum(-1, keepdims=True) + 1e-20)
            return (tidx, tw * SCALE)
        key = jax.random.key(seed)
        ks = jax.random.split(key, 9)

        def w(k, shape, fan_in):
            return jax.random.normal(k, shape, jnp.float32) / np.float32(np.sqrt(fan_in))
        return {'hidden_states': jax.random.normal(ks[0], (B, S, H), jnp.float32), 'gate_w': w(ks[1], (E, H), H), 'gate_bias': jax.random.normal(ks[2], (E,), jnp.float32) * 0.01, 'We_gate': w(ks[3], (E, H, F), H), 'We_up': w(ks[4], (E, H, F), H), 'We_down': w(ks[5], (E, F, H), F), 'Ws_gate': w(ks[6], (H, F_SH), H), 'Ws_up': w(ks[7], (H, F_SH), H), 'Ws_down': w(ks[8], (F_SH, H), F_SH)}
    _L1_ffn_all = _L1_ffn_setup()
    _L1_ffn_in = {k: v for k, v in _L1_ffn_all.items() if k in ('gate_w', 'gate_bias', 'We_gate', 'We_up', 'We_down', 'Ws_gate', 'Ws_up', 'Ws_down')}
    del _L1_ffn_all
    return {'x': x, 'ctx_1024': ctx_1024, 'mask_BxS_ik1': mask_BxS_ik1, 'L0_xattn_Wq': _L0_xattn_in['Wq'], 'L0_xattn_bq': _L0_xattn_in['bq'], 'L0_xattn_Wk': _L0_xattn_in['Wk'], 'L0_xattn_bk': _L0_xattn_in['bk'], 'L0_xattn_Wv': _L0_xattn_in['Wv'], 'L0_xattn_bv': _L0_xattn_in['bv'], 'L0_xattn_Wfc': _L0_xattn_in['Wfc'], 'L0_xattn_bfc': _L0_xattn_in['bfc'], 'L0_attn_W_DQ': _L0_attn_in['W_DQ'], 'L0_attn_W_UQ': _L0_attn_in['W_UQ'], 'L0_attn_W_DKV': _L0_attn_in['W_DKV'], 'L0_attn_W_UKV': _L0_attn_in['W_UKV'], 'L0_attn_W_QR': _L0_attn_in['W_QR'], 'L0_attn_W_KR': _L0_attn_in['W_KR'], 'L0_attn_W_O': _L0_attn_in['W_O'], 'L0_attn_q_norm_w': _L0_attn_in['q_norm_w'], 'L0_attn_k_norm_w': _L0_attn_in['k_norm_w'], 'L0_ffn_tile_sigs': _L0_ffn_in['tile_sigs'], 'L0_ffn_W': _L0_ffn_in['W'], 'L0_ffn_b': _L0_ffn_in['b'], 'L1_xattn_Wq': _L1_xattn_in['Wq'], 'L1_xattn_bq': _L1_xattn_in['bq'], 'L1_xattn_Wk': _L1_xattn_in['Wk'], 'L1_xattn_bk': _L1_xattn_in['bk'], 'L1_xattn_Wv': _L1_xattn_in['Wv'], 'L1_xattn_bv': _L1_xattn_in['bv'], 'L1_attn_W_in': _L1_attn_in['W_in'], 'L1_attn_conv_w': _L1_attn_in['conv_w'], 'L1_attn_conv_b': _L1_attn_in['conv_b'], 'L1_attn_A_log': _L1_attn_in['A_log'], 'L1_attn_D': _L1_attn_in['D'], 'L1_attn_dt_bias': _L1_attn_in['dt_bias'], 'L1_attn_W_out': _L1_attn_in['W_out'], 'L1_ffn_gate_w': _L1_ffn_in['gate_w'], 'L1_ffn_gate_bias': _L1_ffn_in['gate_bias'], 'L1_ffn_We_gate': _L1_ffn_in['We_gate'], 'L1_ffn_We_up': _L1_ffn_in['We_up'], 'L1_ffn_We_down': _L1_ffn_in['We_down'], 'L1_ffn_Ws_gate': _L1_ffn_in['Ws_gate'], 'L1_ffn_Ws_up': _L1_ffn_in['Ws_up'], 'L1_ffn_Ws_down': _L1_ffn_in['Ws_down']}

def reference(x, ctx_1024, mask_BxS_ik1, L0_xattn_Wq, L0_xattn_bq, L0_xattn_Wk, L0_xattn_bk, L0_xattn_Wv, L0_xattn_bv, L0_xattn_Wfc, L0_xattn_bfc, L0_attn_W_DQ, L0_attn_W_UQ, L0_attn_W_DKV, L0_attn_W_UKV, L0_attn_W_QR, L0_attn_W_KR, L0_attn_W_O, L0_attn_q_norm_w, L0_attn_k_norm_w, L0_ffn_tile_sigs, L0_ffn_W, L0_ffn_b, L1_xattn_Wq, L1_xattn_bq, L1_xattn_Wk, L1_xattn_bk, L1_xattn_Wv, L1_xattn_bv, L1_attn_W_in, L1_attn_conv_w, L1_attn_conv_b, L1_attn_A_log, L1_attn_D, L1_attn_dt_bias, L1_attn_W_out, L1_ffn_gate_w, L1_ffn_gate_bias, L1_ffn_We_gate, L1_ffn_We_up, L1_ffn_We_down, L1_ffn_Ws_gate, L1_ffn_Ws_up, L1_ffn_Ws_down):
    import jax
    import jax.numpy as jnp

    def _L0_xattn_ref(query, key_, value, mask, Wq, bq, Wk, bk, Wv, bv, Wfc, bfc):
        import jax, jax.numpy as jnp
        import numpy as np
        HID_DIM = 256
        B, S = (8, 512)
        SCALE = float(np.sqrt(HID_DIM))
        NEG = -10000000000.0
        Q = jnp.einsum('bsd,ed->bse', query, Wq) + bq
        K = jnp.einsum('bsd,ed->bse', key_, Wk) + bk
        V = jnp.einsum('bsd,ed->bse', value, Wv) + bv
        energy = jnp.einsum('bqd,bkd->bqk', Q, K) / SCALE
        energy = jnp.where(mask[:, :, None] == 0, NEG, energy)
        attention = jax.nn.softmax(energy, axis=-1)
        x = jnp.einsum('bqk,bkd->bqd', attention, V)
        out = jnp.einsum('bsd,ed->bse', x, Wfc) + bfc
        return out

    def _L0_attn_ref(x, W_DQ, W_UQ, W_DKV, W_UKV, W_QR, W_KR, W_O, q_norm_w, k_norm_w):
        import jax, jax.numpy as jnp
        import numpy as np
        B, T, D = (2, 512, 256)
        H = 16
        HD = D // H
        DL = 128
        NR = 64
        EPS = 1.1920929e-07

        def _rms_norm(x, w):
            ms = jnp.mean(jnp.square(x), axis=-1, keepdims=True)
            return x * jax.lax.rsqrt(ms + EPS) * w
        b, t, d = x.shape
        scale = HD ** (-0.5)
        xh = x.reshape(b, t, H, HD).transpose(0, 2, 1, 3)
        c_q = jnp.einsum('bhtd,ld->bhtl', xh, W_DQ)
        q_c = jnp.einsum('bhtl,dl->bhtd', c_q, W_UQ)
        q_c_norm = _rms_norm(q_c, q_norm_w)
        q_r = jnp.einsum('bhtd,rd->bhtr', q_c_norm, W_QR)
        q = jnp.concatenate([q_c_norm, q_r], axis=-1)
        c_kv = jnp.einsum('bhtd,ld->bhtl', xh, W_DKV)
        kv = jnp.einsum('bhtl,dl->bhtd', c_kv, W_UKV)
        k_c, v_c = (kv[..., :HD], kv[..., HD:])
        k_c_norm = _rms_norm(k_c, k_norm_w)
        k_r = jnp.einsum('bhtd,rd->bhtr', xh, W_KR)
        k = jnp.concatenate([k_c_norm, k_r], axis=-1)
        scores = jnp.einsum('bhqd,bhkd->bhqk', q, k) * scale
        causal = jnp.triu(jnp.full((t, t), -jnp.inf, dtype=scores.dtype), k=1)
        attn = jax.nn.softmax(scores + causal, axis=-1)
        ctx = jnp.einsum('bhqk,bhkd->bhqd', attn, v_c)
        out = jnp.einsum('bhtd,od->bhto', ctx, W_O)
        return out.transpose(0, 2, 1, 3).reshape(b, t, d)

    def _L0_ffn_ref(x, tile_sigs, W, b):
        import math
        import jax, jax.numpy as jnp
        import numpy as np
        D_CONTENT = 256
        D_POSITION = 32
        NUM_TILES = 8
        BATCH = 8
        SEQ = 512

        def make_pe(seq_len, d_pos):
            pos = jnp.arange(seq_len, dtype=jnp.float32)[:, None]
            div = jnp.exp(jnp.arange(0, d_pos, 2, dtype=jnp.float32) * (-math.log(10000.0) / d_pos))
            ang = pos * div
            pe = jnp.zeros((seq_len, d_pos), dtype=jnp.float32)
            pe = pe.at[:, 0::2].set(jnp.sin(ang))
            pe = pe.at[:, 1::2].set(jnp.cos(ang))
            return pe
        B, S, D = x.shape
        P = tile_sigs.shape[1]
        pe = make_pe(S, P)
        scores = jnp.einsum('sp,tp->st', pe, jnp.sign(tile_sigs))
        idx = jnp.argmax(scores, axis=-1)
        y_all = jnp.einsum('bsd,tod->bsto', x, W) + b
        idx4 = jnp.broadcast_to(idx[None, :, None, None], (B, S, 1, D))
        out = jnp.take_along_axis(y_all, idx4, axis=2)[:, :, 0]
        return out

    def _L1_xattn_ref(q, k, v, Wq, bq, Wk, bk, Wv, bv):
        import jax, jax.numpy as jnp
        import numpy as np
        B, S, D_IN, D_MODEL = (4, 512, 256, 256)
        qp = jnp.einsum('bsd,de->bse', q, Wq) + bq
        kp = jnp.einsum('bsd,de->bse', k, Wk) + bk
        vp = jnp.einsum('bsd,de->bse', v, Wv) + bv
        scale = 1.0 / jnp.sqrt(jnp.asarray(kp.shape[-1], jnp.float32))
        logits = jnp.einsum('bqe,bke->bqk', qp, kp) * scale
        attn = jax.nn.softmax(logits, axis=-1)
        return jnp.einsum('bqk,bke->bqe', attn, vp)

    def _L1_attn_ref(x, W_in, conv_w, conv_b, A_log, D, dt_bias, W_out):
        import jax, jax.numpy as jnp
        import numpy as np
        import math
        D_MODEL = 256
        D_STATE = 64
        EXPAND = 2
        D_CONV = 4
        D_INNER = D_MODEL * EXPAND
        NHEADS = D_INNER // D_STATE
        HEADDIM = D_INNER // NHEADS
        D_PROJ = 2 * D_INNER + NHEADS * (2 * D_STATE + 1)
        BATCH, SEQLEN = (2, 256)

        def _ssm_forward(x, W_in, conv_w, conv_b, A_log, D, dt_bias, W_out):
            B, L, _ = x.shape
            d, n, s = (D_INNER, NHEADS, D_STATE)
            proj = x @ W_in.T
            x_inner = proj[..., :d]
            z = proj[..., d:2 * d]
            bc_dt = proj[..., 2 * d:].reshape(B, L, n, 2 * s + 1)
            B_proj = bc_dt[..., :s]
            C_proj = bc_dt[..., s:2 * s]
            dt_proj = bc_dt[..., 2 * s]
            xc = jax.lax.conv_general_dilated(jnp.transpose(x_inner, (0, 2, 1)), conv_w, window_strides=(1,), padding=[(D_CONV - 1, 0)], feature_group_count=d, dimension_numbers=('NCH', 'OIH', 'NCH'))
            xc = xc + conv_b[None, :, None]
            x_conv = jax.nn.silu(jnp.transpose(xc, (0, 2, 1)))
            x_heads = x_conv.reshape(B, L, n, HEADDIM)
            A = -jnp.exp(A_log)
            dt = jax.nn.softplus(dt_proj + dt_bias)
            dA = jnp.exp(A[None, None] * dt[..., None])
            dB = B_proj * dt[..., None]

            def step(h, inp):
                dA_t, dB_t, C_t, x_t = inp
                h = dA_t[..., None] * h + dB_t[..., None] * x_t[:, :, None, :]
                y_t = jnp.einsum('bns,bnsd->bnd', C_t, h)
                return (h, y_t)
            h0 = jnp.zeros((B, n, s, HEADDIM), dtype=x.dtype)
            xs = (jnp.moveaxis(dA, 1, 0), jnp.moveaxis(dB, 1, 0), jnp.moveaxis(C_proj, 1, 0), jnp.moveaxis(x_heads, 1, 0))
            _, y_scan = jax.lax.scan(step, h0, xs)
            y_heads = jnp.moveaxis(y_scan, 0, 1)
            y_heads = y_heads + D[None, None, :, None] * x_heads
            y = y_heads.reshape(B, L, d) * jax.nn.silu(z)
            return y @ W_out.T
        return _ssm_forward(x, W_in, conv_w, conv_b, A_log, D, dt_bias, W_out)

    def _L1_ffn_ref(hidden_states, gate_w, gate_bias, We_gate, We_up, We_down, Ws_gate, Ws_up, Ws_down):
        import jax, jax.numpy as jnp
        import numpy as np
        B, S, H = (2, 512, 256)
        E, F, K = (64, 128, 8)
        G, TG = (8, 4)
        SCALE = 2.5
        F_SH = 128

        def _gate(x, gate_w, gate_bias):
            scores = jax.nn.sigmoid(x @ gate_w.T)
            sc = scores + gate_bias[None, :]
            T = x.shape[0]
            group_scores = jax.lax.top_k(sc.reshape(T, G, E // G), 2)[0].sum(-1)
            _, gidx = jax.lax.top_k(group_scores, TG)
            gmask = jnp.zeros((T, G), sc.dtype).at[jnp.arange(T)[:, None], gidx].set(1.0)
            smask = jnp.repeat(gmask, E // G, axis=1)
            masked = jnp.where(smask > 0, sc, -jnp.inf)
            _, tidx = jax.lax.top_k(masked, K)
            tw = jnp.take_along_axis(scores, tidx, axis=1)
            tw = tw / (tw.sum(-1, keepdims=True) + 1e-20)
            return (tidx, tw * SCALE)
        b, s, h = hidden_states.shape
        x = hidden_states.reshape(-1, h).astype(jnp.float32)
        tidx, tw = _gate(x, gate_w, gate_bias)
        T = x.shape[0]
        w_dense = jnp.zeros((T, E), tw.dtype).at[jnp.arange(T)[:, None], tidx].add(tw)

        def body(acc, ws):
            wg, wu, wdn, cw = ws
            hmid = jax.nn.silu(x @ wg) * (x @ wu)
            return (acc + cw[:, None] * (hmid @ wdn), None)
        y, _ = jax.lax.scan(body, jnp.zeros_like(x), (We_gate, We_up, We_down, w_dense.T))
        y = y.reshape(b, s, h)
        shared = jax.nn.silu(hidden_states @ Ws_gate) * (hidden_states @ Ws_up) @ Ws_down
        return y + shared
    x = x + _L0_xattn_ref(_layernorm(x, axis=-1), ctx_1024, ctx_1024, mask_BxS_ik1, L0_xattn_Wq, L0_xattn_bq, L0_xattn_Wk, L0_xattn_bk, L0_xattn_Wv, L0_xattn_bv, L0_xattn_Wfc, L0_xattn_bfc)
    x = x + _L0_attn_ref(_layernorm(x, axis=-1), L0_attn_W_DQ, L0_attn_W_UQ, L0_attn_W_DKV, L0_attn_W_UKV, L0_attn_W_QR, L0_attn_W_KR, L0_attn_W_O, L0_attn_q_norm_w, L0_attn_k_norm_w)
    x = x + _L0_ffn_ref(_layernorm(x, axis=-1), L0_ffn_tile_sigs, L0_ffn_W, L0_ffn_b)
    x = x + _L1_xattn_ref(_layernorm(x, axis=-1), ctx_1024, ctx_1024, L1_xattn_Wq, L1_xattn_bq, L1_xattn_Wk, L1_xattn_bk, L1_xattn_Wv, L1_xattn_bv)
    x = x + _L1_attn_ref(_layernorm(x, axis=-1), L1_attn_W_in, L1_attn_conv_w, L1_attn_conv_b, L1_attn_A_log, L1_attn_D, L1_attn_dt_bias, L1_attn_W_out)
    x = x + _L1_ffn_ref(_layernorm(x, axis=-1), L1_ffn_gate_w, L1_ffn_gate_bias, L1_ffn_We_gate, L1_ffn_We_up, L1_ffn_We_down, L1_ffn_Ws_gate, L1_ffn_Ws_up, L1_ffn_Ws_down)
    return x

_drawn_inputs = setup_inputs


def setup_inputs(seed=0):
    import zlib

    import numpy as np

    out = dict(_drawn_inputs(seed))
    spreads = {'L0_attn_q_norm_w': (1.0, 0.6),
     'L0_attn_k_norm_w': (1.0, 0.6),
     'L1_attn_conv_b': (0.0, 0.1),
     'L1_attn_D': (1.0, 0.6)}
    factors = {'L0_xattn_bq': 5.291,
     'L0_xattn_bk': 8.0,
     'L0_attn_W_DQ': 4.519,
     'L0_attn_W_UQ': 4.799,
     'L0_attn_W_DKV': 5.345,
     'L0_attn_W_UKV': 4.131,
     'L0_attn_W_QR': 8.0,
     'L0_attn_W_KR': 8.0,
     'L0_attn_W_O': 3.995,
     'L1_xattn_bq': 6.734,
     'L1_xattn_bk': 8.0,
     'L1_attn_A_log': 6.495,
     'L1_attn_dt_bias': 6.937}
    for name, (base, spread) in spreads.items():
        noise = np.random.default_rng([zlib.crc32(name.encode()), seed]).standard_normal(out[name].shape)
        drawn = base * np.exp(spread * noise) if base else spread * noise
        out[name] = jnp.asarray(drawn.astype(out[name].dtype))
    for name, factor in factors.items():
        out[name] = (out[name] * factor).astype(out[name].dtype)
    return out
```

```python
import math
from contextlib import ExitStack

import numpy as np

import concourse.bass as bass
from concourse import mybir

F32 = mybir.dt.float32
I32 = mybir.dt.int32
ALU = mybir.AluOpType
ACT = mybir.ActivationFunctionType
AX = mybir.AxisListType.X
ds = bass.ds

P = 128
B, S, D = 16, 64, 256
T = B * S
NT = T // P
DH = D // P
NK = 1601
KC = NK // P
KR = NK - KC * P
NC_ = KC + 1
H0, HD0 = 16, 16
NPAIR = H0 // 2
NTILE = 8
NH, DS = 8, 64
CI = NH * DS // P
LV = 6
E, FE, TOPK = 64, 128, 8
G = 8
TG = 4
BIG = 1.0e30
NEG = -10000000000.0


def bc(ap, axis, n):
    shape = list(ap.shape)
    shape.insert(axis, n)
    return ap.unsqueeze(axis).broadcast_to(shape)


def wait(eng, sem, value):
    if isinstance(value, int) and value <= 0:
        return
    eng.wait_ge(sem, value)


def perceiver(nc, a, out, start=0, upto=6):
    with ExitStack() as ctx:
        def sb(name, shape, dt=F32, own=ctx):
            return own.enter_context(nc.sbuf_tensor(name, shape, dt))

        def sem(name):
            return ctx.enter_context(nc.semaphore(name))

        ps = ctx.enter_context(nc.psum_tensor("ps", [P, 8, 512], F32))

        first_ln = "ln%d" % start
        xt = sb("xt", [P, NT, D])
        xn = sb("xn", [P, NT, D])
        xnT = sb("xnT", [P, DH, T])
        ident = sb("ident", [P, P])
        stats = sb("stats", [P, NT, 6])
        mv = sb("mv", [P, NT, 2])
        vare = sb("vare", [P, NT])
        rstd = sb("rstd", [P, NT])
        neghalf = sb("neghalf", [P, 32])

        s_x = sem("x_loaded")
        s_const = sem("const_loaded")
        s_out = sem("out_stored")

        def layer_norm(tag, starts):
            s_stat = sem(tag + "_var_ready")
            s_rstd = sem(tag + "_rstd_ready")
            s_xn = sem(tag + "_xn_ready")
            s_tr = sem(tag + "_tile_transposed")
            s_cp = sem(tag + "_xnT_ready")
            with nc.Block(no_gpsimd_drain=True) as block:
                @block.sync
                def _(sp):
                    starts(sp)

                @block.vector
                def _(dve):
                    if tag == first_ln:
                        dve.wait_ge(s_x, 16)
                    for j in range(NT):
                        nc.vector.bn_stats(stats[:, j, :], xt[:, j, :])
                    dve.drain()
                    for j in range(NT):
                        nc.vector.bn_aggr(mv[:, j, :], stats[:, j, :])
                    dve.drain()
                    nc.vector.tensor_scalar_add(vare[:], mv[:, :, 1], 1e-5).then_inc(s_stat, 1)
                    dve.wait_ge(s_rstd, 1)
                    for j in range(NT):
                        nc.vector.tensor_scalar(xn[:, j, :], xt[:, j, :], mv[:, j, 0:1], rstd[:, j:j + 1],
                                                ALU.subtract, ALU.mult).then_inc(s_xn, 1)

                @block.gpsimd
                def _(pool):
                    pool.wait_ge(s_stat, 1)
                    nc.gpsimd.tensor_tensor(rstd[:], vare[:], neghalf[:, 0:NT], ALU.pow).then_inc(s_rstd, 1)

                @block.tensor
                def _(pe):
                    for j in range(NT):
                        pe.wait_ge(s_xn, j + 1)
                        wait(pe, s_cp, j - 3)
                        for h in range(DH):
                            mm = pe.transpose(ps[:, j % 4, h * P:(h + 1) * P], xn[:, j, h * P:(h + 1) * P], ident[:])
                        mm.then_inc(s_tr, 1)

                @block.scalar
                def _(act):
                    for j in range(NT):
                        act.wait_ge(s_tr, j + 1)
                        nc.scalar.copy(xnT[:, :, j * P:(j + 1) * P],
                                       ps[:, j % 4, 0:D].rearrange("p (h t) -> p h t", h=DH)).then_inc(s_cp, 1)

        class Weights:

            def __init__(self, own, s):
                self.own, self.s, self.loads = own, s, []

            def put(self, name, shape, src, dt=F32):
                t = sb("w_" + name, shape, dt, own=self.own)
                self.loads.append((t[:], src, self.s))
                return t

            def plain(self, name, src, dt=F32):
                return self.put(name, list(a[src].shape), a[src], dt)

            def rows(self, name, src):
                n = a[src].shape[0] // P
                return self.put(name, [P, n, a[src].shape[1]], a[src].rearrange("(h p) e -> p h e", h=n))

            def on_all(self, name, src):
                return self.put(name, [P, a[src].shape[0]], a[src].partition_broadcast(P))

        def issue(eng, loads):
            for dst, src, s in loads:
                eng.dma_start(dst, src).then_inc(s, 16)

        def weights_x0(st):
            W = Weights(st, sem("x0_weights_loaded"))
            w = dict(wq=W.rows("x0_wqT", "L0_xattn_WqT"), wk=W.rows("x0_wk", "L0_xattn_Wk"),
                     wv=W.rows("x0_wvT", "L0_xattn_WvT"), wfc=W.rows("x0_wfcT", "L0_xattn_WfcT"),
                     bq=W.plain("x0_bq", "L0_xattn_bq"), bk=W.plain("x0_bk", "L0_xattn_bk"),
                     bv=W.plain("x0_bv", "L0_xattn_bv"), bout=W.on_all("x0_bfc", "L0_xattn_bfc"),
                     maski=W.put("maski", [P, T], a["mask_BxS_ik1"].rearrange("b s -> (b s)").partition_broadcast(P), I32),
                     maskci=W.plain("maskci", "mask_col", I32))
            w["maskf"] = w["maski"][:].bitcast(F32)
            w["maskcf"] = w["maskci"][:].bitcast(F32)
            w["negc"] = sb("negc", [P, NT], own=st)
            w["loaded"], w["loads"] = W.s, 16 * len(W.loads)
            return w, W.loads

        def weights_x1(st):
            W = Weights(st, sem("x1_weights_loaded"))
            w = dict(wq=W.rows("x1_wq", "L1_xattn_Wq"), wk=W.rows("x1_wkT", "L1_xattn_WkT"), wv=W.rows("x1_wv", "L1_xattn_Wv"),
                     bq=W.plain("x1_bq", "L1_xattn_bq"), bk=W.plain("x1_bk", "L1_xattn_bk"), bv=None,
                     bout=W.on_all("x1_bv", "L1_xattn_bv"))
            w["loaded"], w["loads"] = W.s, 16 * len(W.loads)
            return w, W.loads

        def load_pair(eng, q, u, ctxN, ctxT, s_ctx, s_ctxT):
            eng.dma_start(ctxT[:, u, :, :, :].rearrange("p b h k -> p (b h) k"),
                          a["ctx_T"][ds(q * 4, 4), :, :].rearrange("x p k -> p x k")).then_inc(s_ctxT[u], 16)
            eng.dma_start(ctxN[:, u, :, 0:KC, :].rearrange("p b c d -> p b (c d)"),
                          a["ctx_1024"][ds(q * 2, 2), 0:KC * P, :].rearrange("b (p c) d -> p b (c d)", c=KC)
                          ).then_inc(s_ctx[u], 16)
            eng.dma_start(ctxN[0:KR, u, :, KC, :],
                          a["ctx_1024"][ds(q * 2, 2), KC * P:NK, :].rearrange("b p d -> p b d")).then_inc(s_ctx[u], 16)

        s_ctx = {l: [sem(f"{l}_ctx_rows_loaded{u}") for u in range(2)] for l in ("x0", "x1")}
        s_ctxT = {l: [sem(f"{l}_ctx_cols_loaded{u}") for u in range(2)] for l in ("x0", "x1")}

        def cross_attention(l, ln, make_weights, masked):
            st = ExitStack()
            ctxN = sb(l + "ctxN", [P, 2, 2, NC_, D], own=st)
            ctxT = sb(l + "ctxT", [P, 2, 2, DH, NK], own=st)
            w, loads = make_weights(st)

            def starts(sp):
                issue(sp, loads)
                for q in range(2):
                    load_pair(sp, q, q, ctxN, ctxT, s_ctx[l], s_ctxT[l])
            layer_norm(ln, starts)
            own = lambda name, shape, dt=F32: sb(l + name, shape, dt, own=st)
            wq, wk, wv, bq, bk, bv = (w[k] for k in ("wq", "wk", "wv", "bq", "bk", "bv"))
            s_w = w["loaded"]
            QT = own("QT", [P, DH, T])
            Q2T = own("Q2T", [P, DH, T])
            UT = QT
            rowc = own("rowc", [P, NT])
            s_qmm = sem(l + "_q_product")
            s_q = sem(l + "_q_ready")
            s_q2mm = sem(l + "_qk_product")
            s_q2 = sem(l + "_qk_ready")
            s_qb = sem(l + "_q_dot_bk")
            with nc.Block(no_gpsimd_drain=True) as block:
                @block.tensor
                def _(pe):
                    pe.wait_ge(s_w, w["loads"])
                    for e in range(DH):
                        for n in range(2):
                            for h in range(DH):
                                mm = pe.matmul(ps[:, 2 * e + n, :], wq[:, h, e * P:(e + 1) * P], xnT[:, h, n * 512:(n + 1) * 512],
                                               start=h == 0, stop=h == DH - 1)
                            mm.then_inc(s_qmm, 1)
                    pe.wait_ge(s_q, 4)
                    for e in range(DH):
                        for n in range(2):
                            for h in range(DH):
                                mm = pe.matmul(ps[:, 4 + 2 * e + n, :], wk[:, h, e * P:(e + 1) * P], QT[:, h, n * 512:(n + 1) * 512],
                                               start=h == 0, stop=h == DH - 1)
                            mm.then_inc(s_q2mm, 1)
                    for j in range(NT):
                        for h in range(DH):
                            mm = pe.matmul(ps[:, 0, j:j + 1], QT[:, h, j * P:(j + 1) * P], bk[:, h:h + 1],
                                           start=h == 0, stop=h == DH - 1)
                    mm.then_inc(s_qb, 1)

                @block.scalar
                def _(act):
                    act.wait_ge(s_w, w["loads"])
                    for i in range(4):
                        act.wait_ge(s_qmm, i + 1)
                        e, n = i // 2, i % 2
                        nc.scalar.activation(QT[:, e, n * 512:(n + 1) * 512], ps[:, i, :], ACT.Identity,
                                             bias=bq[:, e:e + 1]).then_inc(s_q, 1)

                @block.vector
                def _(dve):
                    dve.wait_ge(s_w, w["loads"])
                    if masked:
                        maskf = w["maskf"]
                        nc.vector.tensor_copy(maskf, w["maski"][:])
                        nc.vector.tensor_copy(w["maskcf"], w["maskci"][:])
                        dve.drain()
                    for i in range(4):
                        e, n = i // 2, i % 2
                        dve.wait_ge(s_q2mm, i + 1)
                        if masked:
                            nc.vector.tensor_tensor(Q2T[:, e, n * 512:(n + 1) * 512], ps[:, 4 + i, :],
                                                    maskf[:, n * 512:(n + 1) * 512], ALU.mult)
                        else:
                            nc.vector.tensor_copy(Q2T[:, e, n * 512:(n + 1) * 512], ps[:, 4 + i, :])
                    dve.wait_ge(s_qb, 1)
                    if masked:
                        nc.vector.scalar_tensor_tensor(rowc[:], ps[:, 0, 0:NT], 1.0 / 16, w["maskcf"], ALU.mult, ALU.mult)
                        nc.vector.tensor_scalar(w["negc"][:], w["maskcf"], -NEG, NEG, ALU.mult, ALU.add)
                        dve.drain()
                        nc.vector.tensor_tensor(rowc[:], rowc[:], w["negc"][:], ALU.add)
                    else:
                        nc.vector.tensor_scalar(rowc[:], ps[:, 0, 0:NT], 1.0 / 16, None, ALU.mult)

            qcur = own("qcur", [P, 2, DH, P])
            prob = own("prob", [P, 2, NK])
            pT = own("pT", [P, 2, NC_, P])
            un = own("un", [P, 2, D])
            mx = own("mx", [P, 2])
            en = own("en", [P, 2])
            nb = own("nb", [P, 2])
            ssum = own("ssum", [P, 2])
            rsum = own("rsum", [P, 2])
            s_qc = sem(l + "_qcur_ready")
            s_sc = sem(l + "_scores_done")
            s_mx = sem(l + "_max_taken")
            s_ex = sem(l + "_exp_done")
            s_pt = sem(l + "_probs_transposed")
            s_pca = sem(l + "_probsT_copied_act")
            s_pcv = sem(l + "_probsT_copied_dve")
            s_pv = sem(l + "_pv_done")
            s_un = sem(l + "_u_normalised")
            s_ut = sem(l + "_u_transposed")
            s_uc = sem(l + "_uT_copied")
            groups = [(0, 4), (4, 8), (8, 12), (12, 13)]
            with nc.Block(no_gpsimd_drain=True) as block:
                def pe_scores(pe, p, u, q):
                    wait(pe, s_qc, p + 1)
                    pe.wait_ge(s_ctxT[l][u], q * 16 + 16)
                    wait(pe, s_ex, p)
                    for n in range(4):
                        k0, k1 = n * 512, min(NK, n * 512 + 512)
                        for h in range(DH):
                            for b in range(2):
                                mm = pe.matmul(ps[64 * b:64 * b + 64, n, 0:k1 - k0], qcur[:, u, h, 64 * b:64 * b + 64],
                                               ctxT[:, u, b, h, k0:k1], start=h == 0, stop=h == DH - 1)
                    mm.then_inc(s_sc, 1)

                def pe_transposes(pe, p, u):
                    pe.wait_ge(s_ex, p + 1)
                    for g, (c0, c1) in enumerate(groups):
                        if g < 2:
                            wait(pe, s_pca if g == 0 else s_pcv, 2 * p)
                        else:
                            pe.wait_ge(s_pca if g == 2 else s_pcv, 2 * p + 1)
                        for c in range(c0, c1):
                            k = P if c < KC else KR
                            src = prob[:, u, c:KC * P:KC] if c < KC else prob[:, u, KC * P:NK]
                            mm = pe.transpose(ps[0:k, 4 + g % 2, (c - c0) * P:(c - c0 + 1) * P], src, ident[:])
                        mm.then_inc(s_pt, 1)

                def pe_pv(pe, p, u, q):
                    pe.wait_ge(s_pca, 2 * p + 2)
                    pe.wait_ge(s_pcv, 2 * p + 2)
                    pe.wait_ge(s_ctx[l][u], q * 32 + 32)
                    wait(pe, s_un, p)
                    for c in range(NC_):
                        k = P if c < KC else KR
                        for b in range(2):
                            mm = pe.matmul(ps[64 * b:64 * b + 64, 6, 0:D], pT[0:k, u, c, 64 * b:64 * b + 64],
                                           ctxN[0:k, u, b, c, :], start=c == 0, stop=c == NC_ - 1)
                    mm.then_inc(s_pv, 1)

                def pe_ut(pe, p, u):
                    pe.wait_ge(s_un, p + 1)
                    wait(pe, s_uc, p)
                    for h in range(DH):
                        mm = pe.transpose(ps[:, 7, h * P:(h + 1) * P], un[:, u, h * P:(h + 1) * P], ident[:])
                    mm.then_inc(s_ut, 1)

                @block.tensor
                def _(pe):
                    pe_scores(pe, 0, 0, 0)
                    pe_transposes(pe, 0, 0)

                    def step(p, u, q, qb):
                        pe_scores(pe, p, u, q)
                        pe_pv(pe, p - 1, 1 - u, qb)
                        pe_transposes(pe, p, u)
                        pe_ut(pe, p - 1, 1 - u)
                    with pe.Fori(0, NT // 2 - 1) as i:
                        step(i * 2 + 1, 1, i, i)
                        step(i * 2 + 2, 0, i + 1, i)
                    step(NT - 1, 1, NT // 2 - 1, NT // 2 - 1)
                    pe_pv(pe, NT - 1, 1, NT // 2 - 1)
                    pe_ut(pe, NT - 1, 1)

                def vec_max(dve, p, u):
                    dve.wait_ge(s_sc, p + 1)
                    nc.vector.tensor_reduce(mx[:, u:u + 1], ps[:, 0:4, :].rearrange("p a n -> p (a n)")[:, 0:NK], AX, ALU.max)
                    dve.drain()
                    nc.vector.scalar_tensor_tensor(en[:, u:u + 1], mx[:, u:u + 1], 1.0 / 16, rowc[:, ds(p, 1)], ALU.mult, ALU.add)
                    dve.drain()
                    nc.vector.tensor_tensor(nb[:, u:u + 1], rowc[:, ds(p, 1)], en[:, u:u + 1], ALU.subtract).then_inc(s_mx, 1)

                def copy_group(eng, op, p, u, g, s):
                    c0, c1 = groups[g]
                    eng.wait_ge(s_pt, 4 * p + g + 1)
                    if not (isinstance(p, int) and p < 2):
                        wait(eng, s_pv, p - 1)
                    k = P if c0 < KC else KR
                    op(pT[0:k, u, c0:c1, :], ps[0:k, 4 + g % 2, 0:(c1 - c0) * P].rearrange("p (c t) -> p c t", c=c1 - c0)
                       ).then_inc(s, 1)

                def vec_norm(dve, p, u):
                    dve.wait_ge(s_pv, p + 1)
                    if not (isinstance(p, int) and p < 2):
                        wait(dve, s_ut, p - 1)
                    nc.vector.reciprocal(rsum[:, u:u + 1], ssum[:, u:u + 1])
                    dve.drain()
                    nc.vector.tensor_scalar(un[:, u, :], ps[:, 6, 0:D], rsum[:, u:u + 1], None, ALU.mult).then_inc(s_un, 1)

                @block.vector
                def _(dve):
                    vec_max(dve, 0, 0)
                    copy_group(dve, nc.vector.tensor_copy, 0, 0, 1, s_pcv)
                    copy_group(dve, nc.vector.tensor_copy, 0, 0, 3, s_pcv)

                    def step(p, u):
                        vec_max(dve, p, u)
                        vec_norm(dve, p - 1, 1 - u)
                        copy_group(dve, nc.vector.tensor_copy, p, u, 1, s_pcv)
                        copy_group(dve, nc.vector.tensor_copy, p, u, 3, s_pcv)
                    step(1, 1)
                    step(2, 0)
                    with dve.Fori(1, NT // 2 - 1) as i:
                        step(i * 2 + 1, 1)
                        step(i * 2 + 2, 0)
                    step(NT - 1, 1)
                    vec_norm(dve, NT - 1, 1)

                def act_exp(act, p, u):
                    act.wait_ge(s_mx, p + 1)
                    if not (isinstance(p, int) and p < 2):
                        wait(act, s_pt, 4 * p - 4)
                        wait(act, s_un, p - 1)
                    nc.scalar.activation(prob[:, u, :], ps[:, 0:4, :].rearrange("p a n -> p (a n)")[:, 0:NK], ACT.Exp,
                                         bias=nb[:, u:u + 1], scale=1.0 / 16, accum_out=ssum[:, u:u + 1]).then_inc(s_ex, 1)

                def act_ut(act, p):
                    act.wait_ge(s_ut, p + 1)
                    nc.scalar.copy(UT[:, :, ds(p * P, P)], ps[:, 7, 0:D].rearrange("p (h t) -> p h t", h=DH)).then_inc(s_uc, 1)

                @block.scalar
                def _(act):
                    act_exp(act, 0, 0)
                    copy_group(act, nc.scalar.copy, 0, 0, 0, s_pca)
                    copy_group(act, nc.scalar.copy, 0, 0, 2, s_pca)

                    def step(p, u):
                        act_exp(act, p, u)
                        copy_group(act, nc.scalar.copy, p, u, 0, s_pca)
                        copy_group(act, nc.scalar.copy, p, u, 2, s_pca)
                        act_ut(act, p - 1)
                    step(1, 1)
                    step(2, 0)
                    with act.Fori(1, NT // 2 - 1) as i:
                        step(i * 2 + 1, 1)
                        step(i * 2 + 2, 0)
                    step(NT - 1, 1)
                    act_ut(act, NT - 1)

                @block.gpsimd
                def _(pool):
                    def load_q(p, u):
                        if not (isinstance(p, int) and p < 2):
                            wait(pool, s_sc, p - 1)
                        nc.gpsimd.tensor_copy(qcur[:, u, :, :], Q2T[:, :, ds(p * P, P)]).then_inc(s_qc, 1)
                    load_q(0, 0)
                    load_q(1, 1)
                    with pool.Fori(1, NT // 2) as i:
                        load_q(i * 2, 0)
                        load_q(i * 2 + 1, 1)

                @block.sync
                def _(sp):
                    with sp.Fori(1, NT // 2) as i:
                        for u in range(2):
                            sp.wait_ge(s_pv, i * 2 + u - 1)
                            load_pair(sp, i * 2 + u, u, ctxN, ctxT, s_ctx[l], s_ctxT[l])

            s_vmm = sem(l + "_v_product")
            s_v = sem(l + "_v_ready")
            s_omm = sem(l + "_out_product")
            s_res = sem(l + "_residual_added")
            s_bias = sem(l + "_out_bias_added")
            x1T = Q2T
            with nc.Block(no_gpsimd_drain=True) as block:
                @block.tensor
                def _(pe):
                    if masked:
                        for e in range(DH):
                            for n in range(2):
                                for h in range(DH):
                                    mm = pe.matmul(ps[:, 2 * e + n, :], wv[:, h, e * P:(e + 1) * P], UT[:, h, n * 512:(n + 1) * 512],
                                                   start=h == 0, stop=h == DH - 1)
                                mm.then_inc(s_vmm, 1)
                        pe.wait_ge(s_v, 4)
                    src, ww = (x1T, w["wfc"]) if masked else (UT, wv)
                    for j in range(NT):
                        wait(pe, s_res, j - 3)
                        for h in range(DH):
                            mm = pe.matmul(ps[:, 4 + j % 4, 0:D], src[:, h, j * P:(j + 1) * P], ww[:, h, :],
                                           start=h == 0, stop=h == DH - 1)
                        mm.then_inc(s_omm, 1)

                if masked:
                    @block.scalar
                    def _(act):
                        for i in range(4):
                            act.wait_ge(s_vmm, i + 1)
                            e, n = i // 2, i % 2
                            nc.scalar.activation(x1T[:, e, n * 512:(n + 1) * 512], ps[:, i, :], ACT.Identity,
                                                 bias=bv[:, e:e + 1]).then_inc(s_v, 1)

                @block.gpsimd
                def _(pool):
                    for j in range(NT):
                        nc.gpsimd.tensor_tensor(xt[:, j, :], xt[:, j, :], w["bout"][:], ALU.add).then_inc(s_bias, 1)

                @block.vector
                def _(dve):
                    for j in range(NT):
                        dve.wait_ge(s_omm, j + 1)
                        dve.wait_ge(s_bias, j + 1)
                        nc.vector.tensor_tensor(xt[:, j, :], xt[:, j, :], ps[:, 4 + j % 4, 0:D], ALU.add).then_inc(s_res, 1)
            st.close()

        def latent_and_ffn():
            st = ExitStack()
            W = Weights(st, sem("latent_weights_loaded"))
            wdq = W.plain("wdq", "L0_attn_W_DQ8")
            wuq = W.plain("wuq", "L0_attn_W_UQT")
            wdkv = W.rows("wdkv", "L0_attn_W_DKV8")
            wukv = W.rows("wukv", "L0_attn_W_UKVT")
            wkr = W.plain("wkr", "L0_attn_W_KR8")
            wqr = W.plain("wqr", "L0_attn_W_QR")
            wo = W.plain("wo", "L0_attn_W_OT")
            c_bd = W.plain("c_bd", "c_blockdiag")
            c_head = W.plain("c_head", "c_head")
            c_causal = W.plain("c_causal", "c_causal")
            pe_t = W.plain("pe_t", "c_positions")
            sig = W.plain("sig", "L0_ffn_sigsT")
            fb = W.put("fb", [1, NTILE, D], a["L0_ffn_b"].rearrange("(o t) d -> o t d", o=1))
            qkw = sb("qkw", [P, 32, 16], own=st)
            for i, n in enumerate(("q", "k")):
                wsrc = a[f"L0_attn_{n}_norm_w"].partition_broadcast(P)
                for h in range(2):
                    o = h * 16 + i * 8
                    W.loads.append((qkw[:, o:o + 8, :], wsrc.unsqueeze(1).broadcast_to([P, 8, 16]), W.s))
            s_lw, n_lw = W.s, 16 * len(W.loads)
            bd = sb("bd", [P, 3, P], own=st)
            bdv = sb("bdv", [P, P], own=st)
            sel = sb("sel", [P, NTILE, S], own=st)
            fbias = sb("fbias", [P, D], own=st)
            WF = Weights(st, sem("ffn_weights_loaded"))
            wf = WF.put("wf", [P, NTILE * DH, D], a["L0_ffn_WT"].rearrange("(t p) e -> p t e", p=P))
            s_fw, n_fw = WF.s, 16

            def latent_setup():
                with ExitStack() as st:
                    own = lambda name, shape, dt=F32: sb("la_" + name, shape, dt, own=st)
                    wvc = own("wvc", [HD0, 8, HD0])
                    sgn = own("sgn", [32, NTILE])
                    neg = own("neg", [32, NTILE])
                    top = own("top", [P, S])
                    taken = own("taken", [P, S])
                    sel2 = own("sel2", [1, NTILE, 2, S])
                    s_mm = sem("la_composite_product")
                    s_bd = sem("la_composite_ready")
                    s_vc = sem("la_value_product")
                    s_vcc = sem("la_value_copied")
                    s_sg = sem("router_signs_ready")
                    s_rs = sem("router_scores")
                    s_sel = sem("router_chosen")
                    s_fb = sem("ffn_bias_product")
                    with nc.Block(no_gpsimd_drain=True) as block:
                        @block.tensor
                        def _(pe):
                            pe.wait_ge(s_lw, n_lw)

                            def tiled(x):
                                return bc(x, 1, 8)
                            mm = pe.matmul(ps[:, 0, 0:P], wdq[:], tiled(wuq[:]), start=True, stop=True)
                            for h in range(2):
                                mm = pe.matmul(ps[:, 1, 0:P], wdkv[:, h, :], tiled(wukv[:, h, 0:HD0]), start=h == 0, stop=h == 1)
                            mm = pe.matmul(ps[:, 2, 0:P], wkr[:], tiled(wqr[:]), start=True, stop=True)
                            for h in range(2):
                                mm = pe.matmul(ps[0:HD0, 4, 0:HD0], wukv[:, h, HD0:2 * HD0], wdkv[:, h, 0:HD0], start=h == 0, stop=h == 1)
                            mm.then_inc(s_vc, 1)
                            pe.wait_ge(s_vcc, 1)
                            pe.matmul(ps[:, 3, 0:P], wvc[:].rearrange("p x d -> p (x d)"), tiled(wo[:]), start=True, stop=True).then_inc(s_mm, 1)
                            pe.wait_ge(s_sg, 1)
                            for t in range(NTILE):
                                mm = pe.matmul(ps[:, 5, t * S:(t + 1) * S], sgn[:, t:t + 1].broadcast_to([32, P]), pe_t[:],
                                               start=True, stop=True)
                            mm.then_inc(s_rs, 1)
                            pe.wait_ge(s_sel, 1)
                            for t in range(NTILE):
                                mm = pe.matmul(ps[:, 6, 0:D], sel2[0:1, t, :, :].rearrange("p b s -> p (b s)"), fb[0:1, t, :],
                                               start=t == 0, stop=t == NTILE - 1)
                            mm.then_inc(s_fb, 1)

                        @block.vector
                        def _(dve):
                            dve.wait_ge(s_lw, n_lw)
                            nc.vector.tensor_scalar(neg[:], sig[:], 0.0, None, ALU.is_lt)
                            nc.vector.tensor_scalar(sgn[:], sig[:], 0.0, None, ALU.is_gt)
                            dve.drain()
                            nc.vector.tensor_tensor(sgn[:], sgn[:], neg[:], ALU.subtract).then_inc(s_sg, 1)
                            dve.wait_ge(s_vc, 1)
                            nc.vector.tensor_copy(wvc[:], bc(ps[0:HD0, 4, 0:HD0], 1, 8)).then_inc(s_vcc, 1)
                            dve.wait_ge(s_mm, 1)
                            for i in range(3):
                                nc.vector.tensor_tensor(bd[:, i, :], ps[:, i, 0:P], c_bd[:], ALU.mult)
                            nc.vector.tensor_tensor(bdv[:], ps[:, 3, 0:P], c_bd[:], ALU.mult)
                            dve.wait_ge(s_rs, 1)
                            sc = ps[:, 5, :].rearrange("p (t s) -> p t s", t=NTILE)
                            nc.vector.tensor_reduce(top[:], sc.rearrange("p t s -> p s t"), AX, ALU.max)
                            nc.vector.memset(taken[:], 0.0)
                            dve.drain()
                            nc.vector.tensor_tensor(sel[:], sc, bc(top[:], 1, NTILE), ALU.is_equal)
                            dve.drain()
                            for t in range(NTILE):
                                nc.vector.tensor_tensor(sel[:, t, :], sel[:, t, :], taken[:], ALU.is_gt)
                                dve.drain()
                                last = nc.vector.tensor_tensor(taken[:], taken[:], sel[:, t, :], ALU.max)
                                dve.drain()
                            nc.vector.tensor_copy(sel2[:], bc(sel[0:1, :, :], 2, 2)).then_inc(s_sel, 1)
                            dve.wait_ge(s_fb, 1)
                            nc.vector.tensor_copy(fbias[:], ps[:, 6, 0:D])

            def latent_attention():
                st = ExitStack()
                own = lambda name, shape, dt=F32: sb("la_" + name, shape, dt, own=st)
                sq = own("sq", [P, 2, 2, 2 * P])
                ms = own("ms", [P, 2, 32])
                rs = own("rs", [P, 2, 32])
                qk = own("qk", [P, 2, 2, 2, P])
                qkT = own("qkT", [P, 4, T])
                vz = own("vz", [P, B, NPAIR, 34])
                s_pj = sem("la_projected")
                s_sq = sem("la_squared")
                s_ms = sem("la_meansq")
                s_rs = sem("la_rms")
                s_rn = sem("la_scaled")
                s_wn = sem("la_weighted")
                s_kx = sem("la_qk_ready")
                s_tr = sem("la_qk_transposed")
                s_tc = sem("la_qkT_copied")
                s_v = sem("la_v_product")
                s_vz = sem("la_v_filled")
                s_vz0 = sem("la_v_cleared")
                with nc.Block(no_gpsimd_drain=True) as block:
                    @block.tensor
                    def _(pe):
                        def project(j):
                            wait(pe, s_kx, j - 1)
                            u = j % 2
                            for h in range(DH):
                                mm = pe.matmul(ps[:, 2 * u + h, 0:3 * P], xnT[:, h, j * P:(j + 1) * P],
                                               bd[:].rearrange("p i e -> p (i e)"), start=True, stop=True)
                            mm.then_inc(s_pj, 1)

                        def values(j):
                            wait(pe, s_vz, 2 * (j - 1))
                            for b in range(2):
                                for h in range(DH):
                                    for par in range(2):
                                        mm = pe.matmul(ps[64 * par:64 * par + 64, 6 + j % 2, (b * DH + h) * 64:(b * DH + h + 1) * 64],
                                                       xnT[:, h, (2 * j + b) * S:(2 * j + b + 1) * S],
                                                       bdv[:].rearrange("p (x r d) -> p x r d", r=2, d=16)[:, :, par, :], start=True, stop=True)
                            mm.then_inc(s_v, 1)

                        def turn(j):
                            pe.wait_ge(s_kx, j + 1)
                            wait(pe, s_tc, j - 1)
                            for i in range(4):
                                mm = pe.transpose(ps[:, 4 + j % 2, i * P:(i + 1) * P], qk[:, j % 2, i // 2, i % 2, :], ident[:])
                            mm.then_inc(s_tr, 1)
                        project(0)
                        for j in range(NT):
                            values(j)
                            if j + 1 < NT:
                                project(j + 1)
                            turn(j)

                    @block.scalar
                    def _(act):
                        for j in range(NT + 1):
                            if j < NT:
                                u = j % 2
                                act.wait_ge(s_pj, j + 1)
                                wait(act, s_ms, j - 1)
                                nc.scalar.activation(sq[:, u, :, :], ps[:, 2 * u:2 * u + 2, 0:2 * P], ACT.Square).then_inc(s_sq, 1)
                            if j >= 1:
                                act.wait_ge(s_tr, j)
                                nc.scalar.copy(qkT[:, :, (j - 1) * P:j * P],
                                               ps[:, 4 + (j - 1) % 2, :].rearrange("p (i t) -> p i t", i=4)).then_inc(s_tc, 1)

                    @block.vector
                    def _(dve):
                        def value_blocks(j):
                            dve.wait_ge(s_v, j + 1)
                            dve.wait_ge(s_vz0, 3)
                            for par in range(2):
                                r = slice(64 * par, 64 * par + 64)
                                nc.vector.tensor_copy(vz[r, 2 * j:2 * j + 2, :, 17 * par:17 * par + 16].rearrange("p b h d -> p (b h) d"),
                                                      ps[r, 6 + j % 2, 0:D].rearrange("p (x d) -> p x d", d=16)
                                                      ).then_inc(s_vz, 1)
                        for j in range(NT):
                            u = j % 2
                            dve.wait_ge(s_sq, j + 1)
                            wait(dve, s_rs, j - 1)
                            nc.vector.tensor_reduce(ms[:, u, :], sq[:, u, :, :].rearrange("p h (x d) -> p (h x) d", d=16), AX, ALU.add)
                            dve.drain()
                            nc.vector.tensor_scalar(ms[:, u, :], ms[:, u, :], 1.0 / HD0, 1.1920929e-07, ALU.mult, ALU.add).then_inc(s_ms, 1)
                            value_blocks(j)
                            dve.wait_ge(s_rs, j + 1)
                            wait(dve, s_tr, j - 1)
                            nc.vector.tensor_tensor(qk[:, u, :, :, :].rearrange("p h i (x d) -> p h (i x) d", d=16),
                                                    ps[:, 2 * u:2 * u + 2, 0:2 * P].rearrange("p h (x d) -> p h x d", d=16),
                                                    bc(rs[:, u, :].rearrange("p (h x) -> p h x", h=2), 3, 16), ALU.mult).then_inc(s_rn, 1)
                            dve.wait_ge(s_wn, j + 1)
                            nc.vector.tensor_tensor(qk[:, u, :, 1, :], qk[:, u, :, 1, :], ps[:, 2 * u:2 * u + 2, 2 * P:3 * P],
                                                    ALU.add).then_inc(s_kx, 1)

                    @block.gpsimd
                    def _(pool):
                        nc.gpsimd.memset(vz[:].rearrange("p b x d -> p (b x d)"), 0.0).then_inc(s_vz0, 1)
                        pool.wait_ge(s_vz0, 1)
                        nc.gpsimd.memset(vz[0:64, :, :, 16:17], 1.0).then_inc(s_vz0, 1)
                        pool.wait_ge(s_vz0, 2)
                        nc.gpsimd.memset(vz[64:128, :, :, 33:34], 1.0).then_inc(s_vz0, 1)
                        pool.wait_ge(s_vz0, 3)
                        for j in range(NT):
                            u = j % 2
                            pool.wait_ge(s_ms, j + 1)
                            wait(pool, s_rn, j - 1)
                            nc.gpsimd.tensor_tensor(rs[:, u, :], ms[:, u, :], neghalf[:], ALU.pow).then_inc(s_rs, 1)
                            pool.wait_ge(s_rn, j + 1)
                            nc.gpsimd.tensor_tensor(qk[:, u, :, :, :].rearrange("p h i (x d) -> p (h i x) d", d=16),
                                                    qk[:, u, :, :, :].rearrange("p h i (x d) -> p (h i x) d", d=16),
                                                    qkw[:], ALU.mult).then_inc(s_wn, 1)

                kz = own("kz", [P, 2, 2, 2, 8, S])
                sm = own("sm", [P, 2, H0, S])
                mx = own("mx", [P, 2, H0])
                pT = own("pT", [P, 2, NPAIR, P])
                rden = own("rden", [P, 2, H0])
                av = own("av", [P, 2, H0, HD0])
                s_kz = sem("la_keys_spread_dve")
                s_kp = sem("la_keys_spread_pool")
                s_sc = sem("la_scores_done")
                s_mk = sem("la_scores_masked")
                s_sb = sem("la_max_subtracted")
                s_ex = sem("la_exp_done")
                s_pt = sem("la_probs_transposed")
                s_pc = sem("la_probsT_copied")
                s_av = sem("la_av_done")
                s_nm = sem("la_normalised")
                s_ad = sem("la_added")
                with nc.Block(no_gpsimd_drain=True) as block:
                    def spread(eng, e, j, b, s):
                        u = j % 2
                        wait(eng, s_sc, j - 1)
                        for h in range(2):
                            ins = e.tensor_tensor(kz[:, u, b, h, :, :], bc(qkT[:, 2 * h + 1, (2 * j + b) * S:(2 * j + b + 1) * S], 1, 8),
                                                  bc(c_head[:], 2, S), ALU.mult)
                        ins.then_inc(s, 1)

                    @block.gpsimd
                    def _(pool):
                        spread(pool, nc.gpsimd, 0, 1, s_kp)
                        for j in range(NT):
                            u = j % 2
                            if j + 1 < NT:
                                spread(pool, nc.gpsimd, j + 1, 1, s_kp)
                            pool.wait_ge(s_nm, j + 1)
                            nc.gpsimd.tensor_tensor(xt[:, j, :], xt[:, j, :], av[:, u, :, :].rearrange("p h d -> p (h d)"),
                                                    ALU.add).then_inc(s_ad, 1)
                        pool.wait_ge(s_ad, NT)

                    @block.tensor
                    def _(pe):
                        def scores(j):
                            u = j % 2
                            pe.wait_ge(s_kz, j + 1)
                            pe.wait_ge(s_kp, j + 1)
                            wait(pe, s_mk, j - 1)
                            for h in range(2):
                                for b in range(2):
                                    mm = pe.matmul(ps[64 * b:64 * b + 64, 2 * u + h, :], qkT[:, 2 * h, (2 * j + b) * S:(2 * j + b + 1) * S],
                                                   kz[:, u, b, h, :, :].rearrange("p x k -> p (x k)"), start=True, stop=True)
                            mm.then_inc(s_sc, 1)

                        def turn(j):
                            u = j % 2
                            pe.wait_ge(s_ex, j + 1)
                            for g in range(2):
                                wait(pe, s_pc, 2 * j + g - 1)
                                for i in range(4):
                                    hp = 4 * g + i
                                    mm = pe.transpose(ps[:, 4 + g, i * P:(i + 1) * P],
                                                      sm[:, u, 2 * hp:2 * hp + 2, :].rearrange("p h k -> p (h k)"), ident[:])
                                mm.then_inc(s_pt, 1)

                        def mix(j):
                            u = j % 2
                            pe.wait_ge(s_pc, 2 * j + 2)
                            wait(pe, s_nm, j - 1)
                            for hp in range(NPAIR):
                                for b in range(2):
                                    mm = pe.matmul(ps[64 * b:64 * b + 64, 6 + u, hp * 34:hp * 34 + 34], pT[:, u, hp, 64 * b:64 * b + 64],
                                                   vz[:, 2 * j + b, hp, :], start=True, stop=True)
                            mm.then_inc(s_av, 1)
                        scores(0)
                        for j in range(NT):
                            if j + 1 < NT:
                                scores(j + 1)
                            turn(j)
                            mix(j)

                    @block.vector
                    def _(dve):
                        def soft(j):
                            u = j % 2
                            dve.wait_ge(s_sc, j + 1)
                            wait(dve, s_pt, 2 * (j - 1))
                            nc.vector.scalar_tensor_tensor(sm[:, u, :, :], ps[:, 2 * u:2 * u + 2, :].rearrange("p h (x k) -> p (h x) k", k=S),
                                                           float(HD0) ** -0.5, bc(c_causal[:], 1, H0), ALU.mult, ALU.add).then_inc(s_mk, 1)
                            dve.drain()
                            nc.vector.tensor_reduce(mx[:, u, :], sm[:, u, :, :], AX, ALU.max)
                            dve.drain()
                            nc.vector.tensor_tensor(sm[:, u, :, :], sm[:, u, :, :], bc(mx[:, u, :], 2, S), ALU.subtract).then_inc(s_sb, 1)

                        def norm(j):
                            u = j % 2
                            dve.wait_ge(s_av, j + 1)
                            wait(dve, s_ad, j - 1)
                            o = ps[:, 6 + u, 0:NPAIR * 34].rearrange("p (x d) -> p x d", d=17)
                            nc.vector.reciprocal(rden[:, u, :], o[:, :, 16])
                            dve.drain()
                            nc.vector.tensor_tensor(av[:, u, :, :], o[:, :, 0:HD0], bc(rden[:, u, :], 2, HD0), ALU.mult).then_inc(s_nm, 1)
                        spread(dve, nc.vector, 0, 0, s_kz)
                        for j in range(NT):
                            if j + 1 < NT:
                                spread(dve, nc.vector, j + 1, 0, s_kz)
                            soft(j)
                            if j >= 1:
                                norm(j - 1)
                        norm(NT - 1)

                    @block.scalar
                    def _(act):
                        for j in range(NT):
                            u = j % 2
                            act.wait_ge(s_sb, j + 1)
                            nc.scalar.activation(sm[:, u, :, :], sm[:, u, :, :], ACT.Exp).then_inc(s_ex, 1)
                            wait(act, s_av, j - 1)
                            for g in range(2):
                                act.wait_ge(s_pt, 2 * j + g + 1)
                                nc.scalar.copy(pT[:, u, 4 * g:4 * g + 4, :],
                                               ps[:, 4 + g, :].rearrange("p (i t) -> p i t", i=4)).then_inc(s_pc, 1)
                st.close()

            def routed_ffn():
                st = ExitStack()
                xm = sb("ffn_masked", [P, 2, DH, T], F32, own=st)
                s_m = [sem("ffn_masked_dve"), sem("ffn_masked_pool")]
                s_mm = sem("ffn_product")
                s_bias = sem("ffn_bias_added")
                with nc.Block(no_gpsimd_drain=True) as block:
                    def mask(eng, e, h, t):
                        wait(eng, s_mm, t - 1)
                        e.tensor_tensor(xm[:, t % 2, h, :].rearrange("p (b s) -> p b s", s=S), xnT[:, h, :].rearrange("p (b s) -> p b s", s=S),
                                        bc(sel[:, t, :], 1, B), ALU.mult).then_inc(s_m[h], 1)

                    @block.gpsimd
                    def _(pool):
                        for t in range(NTILE):
                            mask(pool, nc.gpsimd, 1, t)
                        for j in range(NT):
                            nc.gpsimd.tensor_tensor(xt[:, j, :], xt[:, j, :], fbias[:], ALU.add).then_inc(s_bias, 1)

                    @block.tensor
                    def _(pe):
                        pe.wait_ge(s_fw, n_fw)
                        for t in range(NTILE):
                            pe.wait_ge(s_m[0], t + 1)
                            pe.wait_ge(s_m[1], t + 1)
                            for j in range(NT):
                                for h in range(DH):
                                    mm = pe.matmul(ps[:, j, 0:D], xm[:, t % 2, h, j * P:(j + 1) * P], wf[:, DH * t + h, :],
                                                   start=t == 0 and h == 0, stop=t == NTILE - 1 and h == 1)
                                if j == NT - 1 or t == NTILE - 1:
                                    mm.then_inc(s_mm, 1)

                    @block.vector
                    def _(dve):
                        for t in range(NTILE):
                            mask(dve, nc.vector, 0, t)
                        for j in range(NT):
                            dve.wait_ge(s_mm, NTILE + j)
                            dve.wait_ge(s_bias, j + 1)
                            nc.vector.tensor_tensor(xt[:, j, :], xt[:, j, :], ps[:, j, 0:D], ALU.add)
                st.close()

            if start < 2:
                layer_norm("ln1", lambda sp: issue(sp, W.loads + WF.loads))
                latent_setup()
                latent_attention()
            if upto >= 3:
                layer_norm("ln2", lambda sp: issue(sp, W.loads + WF.loads) if start == 2 else None)
                if start == 2:
                    latent_setup()
                routed_ffn()
            st.close()

        def state_space():
            st = ExitStack()
            own = lambda name, shape, dt=F32: sb("ss_" + name, shape, dt, own=st)
            W = Weights(st, sem("mixer_weights_loaded"))
            win = W.rows("win", "L1_attn_W_inT")
            wdt = W.rows("wdt", "L1_attn_W_dtT")
            wout = W.rows("wout", "L1_attn_W_outT")
            cw = W.plain("cw", "L1_attn_conv")
            cb = W.plain("cb", "L1_attn_conv_b")
            al = W.plain("al", "L1_attn_A_log")
            dcol = W.put("dcol", [P, CI], a["L1_attn_D2"][0].partition_broadcast(P))
            dcol2 = W.put("dcol2", [P, CI], a["L1_attn_D2"][1].partition_broadcast(P))
            dtb = W.on_all("dtb", "L1_attn_dt_bias")
            c_sel = W.plain("c_sel", "c_segments")
            c_lvl = W.plain("c_lvl", "c_levels")
            s_w, n_w = W.s, 16 * len(W.loads)
            layer_norm("ln4", lambda sp: issue(sp, W.loads))

            xi = own("xi", [P, CI, B, S + 3])
            xc = own("xc", [P, CI, T])
            sz = own("sz", [P, CI, T])
            bT = own("bT", [P, CI, T])
            cT = own("cT", [P, CI, T])
            dt = own("dt", [P, NT * NH])
            tmp = own("tmp", [P, 8, NT * NH])
            aneg = own("aneg", [P, CI])
            xdt = own("xdt", [P, NT, NH * DS])
            s_pm = sem("ss_projected")
            s_ev = sem("ss_projection_copied")
            s_dtp = sem("ss_dt_product")
            s_dv = sem("ss_dt_vector_step")
            s_da = sem("ss_dt_scalar_step")
            s_a = sem("ss_A_exp")
            s_cv = sem("ss_convolved")
            s_cs = sem("ss_conv_gated")
            s_xt = sem("ss_x_transposed")
            s_xd = sem("ss_x_scaled")
            with nc.Block(no_gpsimd_drain=True) as block:
                @block.tensor
                def _(pe):
                    pe.wait_ge(s_w, n_w)
                    for m in range(4 * CI):
                        wait(pe, s_ev, m - 3)
                        for n in range(2):
                            for h in range(DH):
                                mm = pe.matmul(ps[:, 2 * (m % 4) + n, :], win[:, h, m * P:(m + 1) * P], xnT[:, h, n * 512:(n + 1) * 512],
                                               start=h == 0, stop=h == DH - 1)
                        mm.then_inc(s_pm, 1)
                    pe.wait_ge(s_ev, 4 * CI)
                    for j in range(NT):
                        for h in range(DH):
                            mm = pe.matmul(ps[:, 0, j * NH:(j + 1) * NH], xnT[:, h, j * P:(j + 1) * P], wdt[:, h, :],
                                           start=h == 0, stop=h == DH - 1)
                    mm.then_inc(s_dtp, 1)
                    pe.wait_ge(s_cs, CI)
                    for j in range(NT):
                        wait(pe, s_xd, j - 3)
                        for c in range(CI):
                            mm = pe.transpose(ps[:, 4 + j % 4, c * P:(c + 1) * P], xc[:, c, j * P:(j + 1) * P], ident[:])
                        mm.then_inc(s_xt, 1)

                @block.scalar
                def _(act):
                    act.wait_ge(s_w, n_w)
                    nc.scalar.activation(aneg[:], al[:], ACT.Exp).then_inc(s_a, 1)

                    def gate(c):
                        act.wait_ge(s_cv, c + 1)
                        nc.scalar.activation(xc[:, c, :], xc[:, c, :], ACT.Silu).then_inc(s_cs, 1)
                    for m in range(4 * CI):
                        act.wait_ge(s_pm, m + 1)
                        src = ps[:, 2 * (m % 4):2 * (m % 4) + 2, :].rearrange("p a n -> p (a n)")
                        c = m % CI
                        if m < CI:
                            nc.scalar.copy(xi[:, c, :, 3:S + 3], src.rearrange("p (b s) -> p b s", s=S)).then_inc(s_ev, 1)
                        elif m < 2 * CI:
                            nc.scalar.activation(sz[:, c, :], src, ACT.Silu).then_inc(s_ev, 1)
                        else:
                            nc.scalar.copy((bT if m < 3 * CI else cT)[:, c, :], src).then_inc(s_ev, 1)
                        if m >= 3 * CI:
                            gate(c)
                    act.wait_ge(s_dv, 1)
                    nc.scalar.activation(tmp[:, 2, :], tmp[:, 1, :], ACT.Exp, scale=-1.0).then_inc(s_da, 1)
                    act.wait_ge(s_dv, 2)
                    nc.scalar.activation(tmp[:, 4, :], tmp[:, 3, :], ACT.Ln).then_inc(s_da, 1)

                @block.vector
                def _(dve):
                    nc.vector.memset(xi[:, :, :, 0:3].rearrange("p c b k -> p (c b) k"), 0.0)
                    dve.wait_ge(s_w, n_w)
                    nc.vector.tensor_copy(dcol[64:128, :], dcol2[64:128, :])
                    dve.wait_ge(s_a, 1)
                    nc.vector.tensor_scalar(aneg[:], aneg[:], -1.0, None, ALU.mult)
                    for c in range(CI):
                        dve.wait_ge(s_ev, c + 1)
                        acc = xc[:, c, :].rearrange("p (b s) -> p b s", s=S)
                        nc.vector.tensor_scalar(acc, xi[:, c, :, 3:S + 3], cw[:, 4 * c + 3:4 * c + 4], cb[:, c:c + 1], ALU.mult, ALU.add)
                        for k in range(3):
                            dve.drain()
                            last = nc.vector.scalar_tensor_tensor(acc, xi[:, c, :, k:k + S], cw[:, 4 * c + k:4 * c + k + 1], acc,
                                                                  ALU.mult, ALU.add)
                        last.then_inc(s_cv, 1)
                    dve.wait_ge(s_dtp, 1)
                    v, av, e, u, lnu, d, z, q = (tmp[:, i, :] for i in range(8))
                    nc.vector.tensor_tensor(v.rearrange("p (j n) -> p j n", n=NH), ps[:, 0, 0:NT * NH].rearrange("p (j n) -> p j n", n=NH),
                                            bc(dtb[:], 1, NT), ALU.add)
                    dve.drain()
                    nc.vector.scalar_tensor_tensor(av, v, -1.0, v, ALU.mult, ALU.max).then_inc(s_dv, 1)
                    dve.wait_ge(s_da, 1)
                    nc.vector.tensor_scalar(u, e, 1.0, None, ALU.add).then_inc(s_dv, 1)
                    dve.drain()
                    nc.vector.tensor_scalar(d, u, -1.0, None, ALU.add)
                    dve.drain()
                    nc.vector.tensor_scalar(z, d, 0.0, None, ALU.is_equal)
                    dve.drain()
                    nc.vector.tensor_tensor(d, d, z, ALU.add)
                    dve.drain()
                    nc.vector.reciprocal(q, d)
                    dve.drain()
                    nc.vector.tensor_tensor(q, q, e, ALU.mult)
                    nc.vector.tensor_tensor(z, z, e, ALU.mult)
                    dve.wait_ge(s_da, 2)
                    dve.drain()
                    nc.vector.tensor_tensor(q, q, lnu, ALU.mult)
                    dve.drain()
                    nc.vector.tensor_tensor(q, q, z, ALU.add)
                    nc.vector.tensor_scalar(v, v, 0.0, None, ALU.max)
                    dve.drain()
                    nc.vector.tensor_tensor(dt[:], q, v, ALU.add)
                    dve.drain()
                    for j in range(NT):
                        dve.wait_ge(s_xt, j + 1)
                        nc.vector.tensor_tensor(xdt[:, j, :].rearrange("p (n d) -> p n d", d=DS),
                                                ps[:, 4 + j % 4, :].rearrange("p (n d) -> p n d", d=DS),
                                                bc(dt[:, j * NH:(j + 1) * NH], 2, DS), ALU.mult).then_inc(s_xd, 1)

            dec = own("dec", [P, 2, LV, T])
            pr = own("pr", [P, 2, 2, (LV + 1) * S])
            gm = own("gm", [P, 2, 2, S])
            yT = xi[:].rearrange("p c b s -> p (c b s)")[:, 0:CI * T].rearrange("p (c t) -> p c t", c=CI)
            s_sg = sem("ss_segments_summed")
            s_e = sem("ss_decay_ready")
            s_fl = sem("ss_left_factors")
            s_fr = sem("ss_right_factors")
            s_g = sem("ss_pair_products")
            s_gk = sem("ss_products_masked")
            s_gr = sem("ss_G_ready")
            s_y = sem("ss_y_product")
            s_yd = sem("ss_y_plus_Dx")
            s_yz = sem("ss_y_gated")
            with nc.Block(no_gpsimd_drain=True) as block:
                @block.tensor
                def _(pe):
                    def segments(c, j):
                        wait(pe, s_e, c * NT + j)
                        for a_ in range(2):
                            for par in range(2):
                                n = j * NH + 2 * c + par
                                mm = pe.matmul(ps[64 * par:64 * par + 64, a_, 0:3 * P], dt[:, n:n + 1].broadcast_to([P, 64]),
                                               c_sel[:, a_ * 3 * P:(a_ + 1) * 3 * P], start=True, stop=True)
                        mm.then_inc(s_sg, 1)

                    def pairs(c, j):
                        k, u = c * NT + j, j % 2
                        pe.wait_ge(s_fl, LV * (c + 1))
                        pe.wait_ge(s_fr, LV * (c + 1))
                        wait(pe, s_gk, k - 1)
                        for l in range(LV + 1):
                            for b in range(2):
                                t0 = (2 * j + b) * S
                                for par in range(2):
                                    r = slice(64 * par, 64 * par + 64)
                                    f, g = (dec[r, c % 2, l, t0:t0 + S],) * 2 if l < LV else (bT[r, c, t0:t0 + S], cT[r, c, t0:t0 + S])
                                    mm = pe.matmul(ps[64 * b:64 * b + 64, 4 + 2 * u + par, l * S:(l + 1) * S], f, g, start=True, stop=True)
                        mm.then_inc(s_g, 1)

                    def apply(c, j):
                        k, u = c * NT + j, j % 2
                        pe.wait_ge(s_gr, k + 1)
                        wait(pe, s_yd, 2 * c)
                        for b in range(2):
                            for par in range(2):
                                n = 2 * c + par
                                r = slice(64 * b, 64 * b + 64)
                                mm = pe.matmul(ps[64 * par:64 * par + 64, 2 + b, j * S:(j + 1) * S], xdt[r, j, n * DS:(n + 1) * DS],
                                               gm[r, u, par, :], start=True, stop=True)
                        mm.then_inc(s_y, 1)
                    for j in range(NT):
                        segments(0, j)
                    for c in range(CI):
                        for j in range(NT):
                            if c + 1 < CI:
                                segments(c + 1, j)
                            pairs(c, j)
                            if j >= 1:
                                apply(c, j - 1)
                        apply(c, NT - 1)

                @block.scalar
                def _(act):
                    for c in range(CI):
                        for j in range(NT):
                            act.wait_ge(s_sg, c * NT + j + 1)
                            wait(act, s_g, (c - 1) * NT)
                            nc.scalar.activation(dec[:, c % 2, :, j * P:(j + 1) * P].rearrange("p (a l) t -> p a l t", a=2),
                                                 ps[:, 0:2, 0:3 * P].rearrange("p a (l t) -> p a l t", l=3), ACT.Exp,
                                                 scale=aneg[:, c:c + 1]).then_inc(s_e, 1)

                def factors(eng, e, c, side, src, s):
                    eng.wait_ge(s_e, NT * (c + 1))
                    for l in range(LV):
                        w = 32 >> l
                        f = dec[:, c % 2, l, :].rearrange("p (k r w) -> p k r w", r=2, w=w)[:, :, side, :]
                        g = src[:, c, :].rearrange("p (k r w) -> p k r w", r=2, w=w)[:, :, side, :]
                        e.tensor_tensor(f, f, g, ALU.mult).then_inc(s, 1)

                @block.gpsimd
                def _(pool):
                    for c in range(CI):
                        factors(pool, nc.gpsimd, c, 1, cT, s_fr)
                        if c >= 1:
                            pool.wait_ge(s_yd, 2 * c)
                            nc.gpsimd.tensor_tensor(yT[:, c - 1, :], yT[:, c - 1, :], sz[:, c - 1, :], ALU.mult).then_inc(s_yz, 1)
                    pool.wait_ge(s_yd, 2 * CI)
                    nc.gpsimd.tensor_tensor(yT[:, CI - 1, :], yT[:, CI - 1, :], sz[:, CI - 1, :], ALU.mult).then_inc(s_yz, 1)
                    pool.wait_ge(s_yz, CI)

                @block.vector
                def _(dve):
                    factors(dve, nc.vector, 0, 0, bT, s_fl)
                    for c in range(CI):
                        for j in range(NT):
                            k, u = c * NT + j, j % 2
                            dve.wait_ge(s_g, k + 1)
                            nc.vector.tensor_tensor(pr[:, u, :, :], ps[:, 4 + 2 * u:6 + 2 * u, 0:(LV + 1) * S], bc(c_lvl[:], 1, 2),
                                                    ALU.mult).then_inc(s_gk, 1)
                            wait(dve, s_y, k - 1)
                            dve.drain()
                            nc.vector.tensor_reduce(gm[:, u, :, :], pr[:, u, :, :].rearrange("p r (l t) -> p r t l", t=S), AX,
                                                    ALU.add).then_inc(s_gr, 1)
                        if c + 1 < CI:
                            factors(dve, nc.vector, c + 1, 0, bT, s_fl)
                        dve.wait_ge(s_y, NT * (c + 1))
                        for b in range(2):
                            def half(t):
                                return t.rearrange("p (j b s) -> p j b s", b=2, s=S)[:, :, b, :]
                            nc.vector.scalar_tensor_tensor(half(yT[:, c, :]), half(xc[:, c, :]), dcol[:, c:c + 1],
                                                           ps[:, 2 + b, :].rearrange("p (j s) -> p j s", s=S), ALU.mult, ALU.add
                                                           ).then_inc(s_yd, 1)

            s_o = sem("ss_out_product")
            with nc.Block(no_gpsimd_drain=True) as block:
                @block.tensor
                def _(pe):
                    for j in range(NT):
                        for c in range(CI):
                            mm = pe.matmul(ps[:, j, 0:D], yT[:, c, j * P:(j + 1) * P], wout[:, c, :], start=c == 0, stop=c == CI - 1)
                        mm.then_inc(s_o, 1)

                @block.vector
                def _(dve):
                    for j in range(NT):
                        dve.wait_ge(s_o, j + 1)
                        nc.vector.tensor_tensor(xt[:, j, :], xt[:, j, :], ps[:, j, 0:D], ALU.add)
            st.close()

        def experts():
            st = ExitStack()
            own = lambda name, shape, dt=F32: sb("moe_" + name, shape, dt, own=st)
            W = Weights(st, sem("moe_weights_loaded"))
            gw = W.rows("gw", "L1_ffn_gate_wT")
            gb = W.on_all("gb", "L1_ffn_gate_bias")
            wsgu = W.rows("wsgu", "moe_shared_gu")
            wsd = W.plain("wsd", "L1_ffn_Ws_down")
            c_lt = W.plain("c_lt", "c_lower")
            s_w, n_w = W.s, 16 * len(W.loads)
            wgu = own("wgu", [P, 2, DH, 2 * FE])
            wdn = own("wdn", [P, 2, D])
            s_wl = [sem("moe_expert_loaded0"), sem("moe_expert_loaded1")]

            def load_expert(sp, e, u):
                sp.dma_start(wgu[:, u, :, :], a["moe_gu"][ds(e * DH, DH), :, :].rearrange("h p f -> p h f")).then_inc(s_wl[u], 16)
                sp.dma_start(wdn[:, u, :], a["L1_ffn_We_down"][ds(e, 1), :, :].rearrange("o p d -> p (o d)")).then_inc(s_wl[u], 16)

            def starts(sp):
                issue(sp, W.loads)
                for u in range(2):
                    load_expert(sp, u, u)
            layer_norm("ln5", starts)

            sg = own("sg", [P, NT, E])
            sc = own("sc", [P, NT, E])
            m8 = own("m8", [P, NT, G, 8])
            gs = own("gs", [P, NT, G])
            cmp = own("cmp", [P, NT, G, G])
            eq = own("eq", [P, NT, G, G])
            gmask = own("gmask", [P, NT * G])
            goff = own("goff", [P, NT * G])
            top = own("top", [P, NT, 8])
            rep = own("rep", [P, NT, E])
            cwt = own("cwt", [P, NT, E])
            tot = own("tot", [P, NT])
            s_gp = sem("moe_gate_product")
            s_ge = sem("moe_gate_exp")
            with nc.Block(no_gpsimd_drain=True) as block:
                @block.tensor
                def _(pe):
                    pe.wait_ge(s_w, n_w)
                    for j in range(NT):
                        for h in range(DH):
                            mm = pe.matmul(ps[:, 0, j * E:(j + 1) * E], xnT[:, h, j * P:(j + 1) * P], gw[:, h, :],
                                           start=h == 0, stop=h == DH - 1)
                    mm.then_inc(s_gp, 1)

                @block.scalar
                def _(act):
                    act.wait_ge(s_gp, 1)
                    nc.scalar.activation(sg[:].rearrange("p j e -> p (j e)"), ps[:, 0, :], ACT.Exp, scale=-1.0).then_inc(s_ge, 1)

                @block.vector
                def _(dve):
                    dve.wait_ge(s_ge, 1)
                    nc.vector.tensor_scalar(sg[:], sg[:], 1.0, None, ALU.add)
                    dve.drain()
                    nc.vector.reciprocal(sg[:], sg[:])
                    dve.drain()
                    nc.vector.tensor_tensor(sc[:], sg[:], bc(gb[:], 1, NT), ALU.add)
                    dve.drain()
                    for j in range(NT):
                        for g in range(G):
                            nc.vector.max(m8[:, j, g, :], sc[:, j, g * 8:(g + 1) * 8])
                    dve.drain()
                    nc.vector.tensor_tensor(gs[:], m8[:, :, :, 0], m8[:, :, :, 1], ALU.add)
                    dve.drain()
                    nc.vector.tensor_tensor(cmp[:], bc(gs[:], 2, G), bc(gs[:], 3, G), ALU.is_gt)
                    nc.vector.tensor_tensor(eq[:], bc(gs[:], 2, G), bc(gs[:], 3, G), ALU.is_equal)
                    dve.drain()
                    nc.vector.tensor_tensor(eq[:].rearrange("p j g h -> p j (g h)"), eq[:].rearrange("p j g h -> p j (g h)"),
                                            bc(c_lt[:], 1, NT), ALU.mult)
                    dve.drain()
                    nc.vector.tensor_tensor(cmp[:], cmp[:], eq[:], ALU.add)
                    dve.drain()
                    nc.vector.tensor_reduce(gmask[:], cmp[:].rearrange("p j g h -> p (j g) h"), AX, ALU.add)
                    dve.drain()
                    nc.vector.tensor_scalar(gmask[:], gmask[:], float(TG), None, ALU.is_lt)
                    dve.drain()
                    nc.vector.tensor_scalar(goff[:], gmask[:], BIG, -BIG, ALU.mult, ALU.add)
                    sc8 = sc[:].rearrange("p j (g x) -> p (j g) x", x=8)
                    nc.vector.tensor_tensor(sc8, sc8, bc(gmask[:], 2, 8), ALU.mult)
                    dve.drain()
                    nc.vector.tensor_tensor(sc8, sc8, bc(goff[:], 2, 8), ALU.add)
                    dve.drain()
                    for j in range(NT):
                        nc.vector.max(top[:, j, :], sc[:, j, :])
                    dve.drain()
                    for j in range(NT):
                        nc.vector.match_replace(out=rep[:, j, :], in_to_replace=top[:, j, :], in_values=sc[:, j, :], imm_value=-3.0 * BIG)
                    dve.drain()
                    nc.vector.tensor_tensor(rep[:], rep[:], sc[:], ALU.not_equal)
                    dve.drain()
                    nc.vector.tensor_tensor(cwt[:], sg[:], rep[:], ALU.mult)
                    dve.drain()
                    nc.vector.tensor_reduce(tot[:], cwt[:], AX, ALU.add)
                    dve.drain()
                    nc.vector.tensor_scalar(tot[:], tot[:], 1e-20, None, ALU.add)
                    dve.drain()
                    nc.vector.reciprocal(tot[:], tot[:])
                    dve.drain()
                    nc.vector.tensor_scalar(tot[:], tot[:], 2.5, None, ALU.mult)
                    dve.drain()
                    nc.vector.tensor_tensor(cwt[:], cwt[:], bc(tot[:], 2, E), ALU.mult)

            hs = own("hs", [P, 2, FE])
            hh = own("hh", [P, 2, FE])
            hT = own("hT", [P, 2, FE])
            s_gu = sem("moe_gate_up")
            s_si = sem("moe_silu")
            s_hh = sem("moe_hidden")
            s_ht = sem("moe_hidden_transposed")
            s_hc = sem("moe_hiddenT_copied")
            s_dn = sem("moe_down")
            s_fin = sem("moe_added")
            with nc.Block(no_gpsimd_drain=True) as block:
                @block.tensor
                def _(pe):
                    def gate_up(k, m, j, w):
                        wait(pe, s_hh, k - 1)
                        for h in range(DH):
                            mm = pe.matmul(ps[:, 4 + m % 2, 0:2 * FE], xnT[:, h, j * P:(j + 1) * P], w[:, h, :],
                                           start=h == 0, stop=h == DH - 1)
                        mm.then_inc(s_gu, 1)

                    def turn(k, m):
                        pe.wait_ge(s_hh, k + 1)
                        wait(pe, s_hc, k - 1)
                        pe.transpose(ps[:, 6 + m % 2, 0:P], hh[:, m % 2, :], ident[:]).then_inc(s_ht, 1)

                    def down(k, m, j, w, first=False):
                        pe.wait_ge(s_hc, k + 1)
                        pe.matmul(ps[:, j // 2, (j % 2) * D:(j % 2 + 1) * D], hT[:, m % 2, :], w,
                                  start=first and j % 2 == 0, stop=True, skip_group_check=True).then_inc(s_dn, 1)
                    for j in range(NT):
                        gate_up(j, j, j, wsgu[:])
                        if j >= 2:
                            turn(j - 2, j)
                        if j >= 3:
                            down(j - 3, j - 3, j - 3, wsd[:], True)

                    def expert_pair(i, first):
                        for m in range(2 * NT):
                            k = i * 16 + (NT + m)
                            if m % NT == 0:
                                pe.wait_ge(s_wl[m // NT], i * 32 + 32)
                            gate_up(k, m, m % NT, wgu[:, m // NT, :, :])
                            turn(k - 2, m)
                            if first and m < 3:
                                down(k - 3, m - 3, NT - 3 + m, wsd[:], True)
                            else:
                                down(k - 3, m - 3, (m - 3) % NT, wdn[:, ((m - 3) // NT) % 2, :])
                    expert_pair(0, True)
                    with pe.Fori(1, E // 2) as i:
                        expert_pair(i, False)
                    K = NT + E * NT
                    down(K - 3, 1, 5, wdn[:, 1, :])
                    for k in (K - 2, K - 1):
                        turn(k, k)
                        down(k, k, k % NT, wdn[:, 1, :])

                def hidden(dve, k, m, cw):
                    dve.wait_ge(s_si, k + 1)
                    wait(dve, s_ht, k - 1)
                    up = ps[:, 4 + m % 2, FE:2 * FE]
                    if cw is None:
                        nc.vector.tensor_tensor(hh[:, m % 2, :], hs[:, m % 2, :], up, ALU.mult).then_inc(s_hh, 1)
                    else:
                        nc.vector.scalar_tensor_tensor(hh[:, m % 2, :], hs[:, m % 2, :], cw, up, ALU.mult, ALU.mult).then_inc(s_hh, 1)

                @block.vector
                def _(dve):
                    for j in range(NT):
                        hidden(dve, j, j, None)

                    def expert_pair(i):
                        for m in range(2 * NT):
                            hidden(dve, i * 16 + (NT + m), m, cwt[:, m % NT, ds(i * 2 + m // NT, 1)])
                    expert_pair(0)
                    with dve.Fori(1, E // 2) as i:
                        expert_pair(i)
                    dve.wait_ge(s_dn, NT + E * NT)
                    for j in range(NT):
                        nc.vector.tensor_tensor(xt[:, j, :], xt[:, j, :], ps[:, j // 2, (j % 2) * D:(j % 2 + 1) * D], ALU.add)

                @block.scalar
                def _(act):
                    def silu(k, m):
                        act.wait_ge(s_gu, k + 1)
                        wait(act, s_hh, k - 1)
                        nc.scalar.activation(hs[:, m % 2, :], ps[:, 4 + m % 2, 0:FE], ACT.Silu).then_inc(s_si, 1)

                    def copy(k, m):
                        act.wait_ge(s_ht, k + 1)
                        wait(act, s_dn, k - 1)
                        nc.scalar.copy(hT[:, m % 2, :], ps[:, 6 + m % 2, 0:P]).then_inc(s_hc, 1)
                    for k in range(NT):
                        silu(k, k)
                        if k >= 2:
                            copy(k - 2, k)

                    def expert_pair(i):
                        for m in range(2 * NT):
                            k = i * 16 + (NT + m)
                            silu(k, m)
                            copy(k - 2, m)
                    expert_pair(0)
                    with act.Fori(1, E // 2) as i:
                        expert_pair(i)
                    for k in (NT + E * NT - 2, NT + E * NT - 1):
                        copy(k, k)

                @block.sync
                def _(sp):
                    with sp.Fori(1, E // 2) as i:
                        for u in range(2):
                            sp.wait_ge(s_dn, i * 16 + NT * u)
                            load_expert(sp, i * 2 + u, u)
            st.close()

        with nc.Block(no_gpsimd_drain=True) as block:
            @block.sync
            def _(sp):
                sp.dma_start(xt[:], a["x"].rearrange("(j b) s d -> (b s) j d", b=2)).then_inc(s_x, 16)
                sp.dma_start(ident[:], a["c_ident"]).then_inc(s_const, 16)

            @block.vector
            def _(dve):
                nc.vector.memset(neghalf[:], -0.5)

            @block.tensor
            def _(pe):
                pe.wait_ge(s_const, 16)

        if start < 1 <= upto:
            cross_attention("x0", "ln0", weights_x0, True)
        if start < 3 and upto >= 2:
            latent_and_ffn()
        if start < 4 <= upto:
            cross_attention("x1", "ln3", weights_x1, False)
        if start < 5 <= upto:
            state_space()
        if start < 6 <= upto:
            experts()

        with nc.Block(no_gpsimd_drain=True) as block:
            @block.sync
            def _(sp):
                sp.dma_start(out.rearrange("(j b) s d -> (b s) j d", b=2), xt[:]).then_inc(s_out, 16)
                sp.wait_ge(s_out, 16)


def _constants():
    f = np.float32
    c = {"c_ident": np.eye(P, dtype=f)}
    r = np.arange(P)
    c["c_blockdiag"] = (r[:, None] // HD0 == r[None, :] // HD0).astype(f)
    c["c_head"] = (r[:, None] // HD0 == np.arange(8)[None, :]).astype(f)
    c["c_causal"] = np.where(np.arange(S)[None, :] <= (r % S)[:, None], 0.0, -BIG).astype(f)
    pos = np.arange(S, dtype=f)[:, None]
    ang = pos * np.exp(np.arange(0, 32, 2, dtype=f) * f(-math.log(10000.0) / 32))
    table = np.zeros((S, 32), f)
    table[:, 0::2], table[:, 1::2] = np.sin(ang), np.cos(ang)
    same = r[:, None] // S == r[None, :] // S
    tr, tc = (r % S)[:, None], (r % S)[None, :]
    seg, lvl = [], []
    for l in range(LV):
        w = 32 >> l
        mid = tc // (2 * w) * 2 * w + w - 1
        right = tc > mid
        seg.append(same & np.where(right, (tr > mid) & (tr <= tc), (tr > tc) & (tr <= mid)))
        lvl.append((tr // (2 * w) == tc // (2 * w)) & (tr % (2 * w) < w) & (tc % (2 * w) >= w))
    lvl.append(tr == tc)
    c["c_segments"] = np.concatenate(seg, 1).astype(f)
    c["c_levels"] = np.concatenate([v[:, :S] for v in lvl], 1).astype(f)
    c["c_lower"] = np.tile((np.arange(G)[None, :] < np.arange(G)[:, None]).astype(f).reshape(1, -1), (P, 1))
    c["c_positions"] = np.ascontiguousarray(table.T)
    return c


def _arrays(inputs):
    t = {k: np.ascontiguousarray(v) for k, v in inputs.items()}
    lay = {}

    def column(v):
        return np.ascontiguousarray(v.reshape(-1, P).T)

    def T_(name, new):
        lay[new] = np.ascontiguousarray(np.swapaxes(t[name], -1, -2))

    for n in ("x", "ctx_1024", "mask_BxS_ik1", "L0_xattn_Wk", "L0_xattn_bfc"):
        lay[n] = t[n]
    for n in ("L0_xattn_bq", "L0_xattn_bk", "L0_xattn_bv"):
        lay[n] = column(t[n])
    lay["mask_col"] = column(t["mask_BxS_ik1"])
    for n in ("L0_attn_W_QR", "L0_attn_q_norm_w", "L0_attn_k_norm_w", "L0_ffn_b",
              "L1_xattn_Wq", "L1_xattn_Wv", "L1_xattn_bv"):
        lay[n] = t[n]
    T_("L0_ffn_tile_sigs", "L0_ffn_sigsT")
    for n in ("L0_attn_W_DQ", "L0_attn_W_DKV", "L0_attn_W_KR"):
        lay[n + "8"] = np.tile(t[n], (1, 8))
    lay["L0_ffn_WT"] = np.ascontiguousarray(np.swapaxes(t["L0_ffn_W"], 1, 2)).reshape(NTILE * D, D)
    for n in ("L1_xattn_bq", "L1_xattn_bk"):
        lay[n] = column(t[n])
    for n in ("L0_xattn_Wq", "L0_xattn_Wv", "L0_xattn_Wfc", "L0_attn_W_UQ", "L0_attn_W_UKV", "L0_attn_W_O", "L1_xattn_Wk"):
        T_(n, n + "T")
    w_in = t["L1_attn_W_in"].T
    heads = w_in[:, 2 * NH * DS:].reshape(D, NH, 2 * DS + 1)
    lay["L1_attn_W_inT"] = np.ascontiguousarray(np.concatenate(
        [w_in[:, :2 * NH * DS], heads[:, :, :DS].reshape(D, -1), heads[:, :, DS:2 * DS].reshape(D, -1)], 1))
    lay["L1_attn_W_dtT"] = np.ascontiguousarray(heads[:, :, 2 * DS])
    lay["L1_attn_conv"] = np.ascontiguousarray(t["L1_attn_conv_w"].reshape(CI, P, 4).transpose(1, 0, 2)).reshape(P, CI * 4)
    lay["L1_attn_conv_b"] = column(t["L1_attn_conv_b"])
    lay["L1_attn_A_log"] = column(t["L1_attn_A_log"].reshape(-1))
    lay["L1_attn_D2"] = np.ascontiguousarray(t["L1_attn_D"].reshape(CI, 2).T)
    lay["L1_attn_dt_bias"] = t["L1_attn_dt_bias"]
    T_("L1_attn_W_out", "L1_attn_W_outT")
    T_("L1_ffn_gate_w", "L1_ffn_gate_wT")
    lay["L1_ffn_gate_bias"] = t["L1_ffn_gate_bias"]
    lay["moe_gu"] = np.concatenate([t["L1_ffn_We_gate"], t["L1_ffn_We_up"]], 2).reshape(E * DH, P, 2 * FE)
    lay["L1_ffn_We_down"] = t["L1_ffn_We_down"]
    lay["moe_shared_gu"] = np.concatenate([t["L1_ffn_Ws_gate"], t["L1_ffn_Ws_up"]], 1)
    lay["L1_ffn_Ws_down"] = t["L1_ffn_Ws_down"]
    lay["ctx_T"] = np.ascontiguousarray(np.swapaxes(t["ctx_1024"], 1, 2)).reshape(B * DH, P, NK)
    lay.update(_constants())
    return lay


def kernel(**inputs):
    from concourse import bacc
    from concourse.bass_utils import run_bass_kernel_spmd

    nc = bacc.Bacc("TRN2", target_bir_lowering=False, num_devices=1)
    arrays = _arrays(inputs)
    args = {k: nc.dram_tensor(k, v.shape, mybir.dt.from_np(v.dtype), kind="ExternalInput").ap() for k, v in arrays.items()}
    out = nc.dram_tensor("out", (B, S, D), F32, kind="ExternalOutput").ap()
    perceiver(nc, args, out)
    r = run_bass_kernel_spmd(nc, [arrays], core_ids=[0])
    return r.results[0]["out"]
```

```python
import math
from contextlib import ExitStack

import numpy as np

import concourse.bass as bass
from concourse import mybir

F32 = mybir.dt.float32
I32 = mybir.dt.int32
BF16 = mybir.dt.bfloat16
ALU = mybir.AluOpType
ACT = mybir.ActivationFunctionType
AX = mybir.AxisListType.X
ds = bass.ds

P = 128
B, S, D = 16, 64, 256
T = B * S
NT = T // P
DH = D // P
NK = 1601
KC = NK // P
KR = NK - KC * P
NC_ = KC + 1
H0, HD0 = 16, 16
NPAIR = H0 // 2
NTILE = 8
NH, DS = 8, 64
CI = NH * DS // P
LV = 6
E, FE = 64, 128
G = 8
TG = 4
BIG = 1.0e30
NEG = -10000000000.0


def bc(ap, axis, n):
    shape = list(ap.shape)
    shape.insert(axis, n)
    return ap.unsqueeze(axis).broadcast_to(shape)


def wait(eng, sem, value):
    if isinstance(value, int) and value <= 0:
        return
    eng.wait_ge(sem, value)


def perceiver(nc, a, out):
    with ExitStack() as ctx:
        def sb(name, shape, dt=F32, own=ctx):
            return own.enter_context(nc.sbuf_tensor(name, shape, dt))

        def sem(name):
            return ctx.enter_context(nc.semaphore(name))

        ps = ctx.enter_context(nc.psum_tensor("ps", [P, 8, 512], F32))

        xt = sb("xt", [P, NT, D])
        xn = sb("xn", [P, NT, D])
        xnT = sb("xnT", [P, DH, T])
        ident = sb("ident", [P, P])
        stats = sb("stats", [P, NT, 6])
        mv = sb("mv", [P, NT, 2])
        vare = sb("vare", [P, NT])
        rstd = sb("rstd", [P, NT])
        neghalf = sb("neghalf", [P, 32])

        xn_rows = nc.dram_tensor("xn_rows", (T, D), F32).ap()
        y_rows = nc.dram_tensor("y_rows", (P * P + T * 8, D), F32).ap()
        s_x = sem("x_loaded")
        s_const = sem("const_loaded")
        s_out = sem("out_stored")

        s_stat = sem("ln_var_ready")
        s_rstd = sem("ln_rstd_ready")
        s_xn = sem("ln_tile_normalised")
        s_tr = sem("ln_tile_transposed")
        s_cp = sem("ln_xnT_copied")
        ln_done = [0]

        def layer_norm(starts):
            r = ln_done[0]
            ln_done[0] += 1
            with nc.Block(no_gpsimd_drain=True) as block:
                @block.sync
                def _(sp):
                    starts(sp)

                @block.vector
                def _(dve):
                    if r == 0:
                        dve.wait_ge(s_x, 16)
                    for j in range(NT):
                        nc.vector.bn_stats(stats[:, j, :], xt[:, j, :])
                    dve.drain()
                    for j in range(NT):
                        nc.vector.bn_aggr(mv[:, j, :], stats[:, j, :])
                    dve.drain()
                    nc.vector.tensor_scalar_add(vare[:], mv[:, :, 1], 1e-5).then_inc(s_stat, 1)
                    dve.wait_ge(s_rstd, r + 1)
                    for j in range(NT):
                        nc.vector.tensor_scalar(xn[:, j, :], xt[:, j, :], mv[:, j, 0:1], rstd[:, j:j + 1],
                                                ALU.subtract, ALU.mult).then_inc(s_xn, 1)

                @block.gpsimd
                def _(pool):
                    pool.wait_ge(s_stat, r + 1)
                    nc.gpsimd.tensor_tensor(rstd[:], vare[:], neghalf[:, 0:NT], ALU.pow).then_inc(s_rstd, 1)

                @block.tensor
                def _(pe):
                    for j in range(NT):
                        pe.wait_ge(s_xn, r * NT + j + 1)
                        wait(pe, s_cp, r * NT + j - 3 if j > 3 else 0)
                        for h in range(DH):
                            mm = pe.transpose(ps[:, j % 4, h * P:(h + 1) * P], xn[:, j, h * P:(h + 1) * P], ident[:])
                        mm.then_inc(s_tr, 1)

                @block.scalar
                def _(act):
                    for j in range(NT):
                        act.wait_ge(s_tr, r * NT + j + 1)
                        nc.scalar.copy(xnT[:, :, j * P:(j + 1) * P],
                                       ps[:, j % 4, 0:D].rearrange("p (h t) -> p h t", h=DH)).then_inc(s_cp, 1)

        class Weights:

            def __init__(self, own, s):
                self.own, self.s, self.loads = own, s, []

            def put(self, name, shape, src, dt=F32):
                t = sb("w_" + name, shape, dt, own=self.own)
                self.loads.append((t[:], src, self.s))
                return t

            def plain(self, name, src, dt=F32):
                return self.put(name, list(a[src].shape), a[src], dt)

            def rows(self, name, src):
                n = a[src].shape[0] // P
                return self.put(name, [P, n, a[src].shape[1]], a[src].rearrange("(h p) e -> p h e", h=n))

            def on_all(self, name, src):
                return self.put(name, [P, a[src].shape[0]], a[src].partition_broadcast(P))

        def issue(eng, loads):
            for dst, src, s in loads:
                eng.dma_start(dst, src).then_inc(s, 16)

        def weights_x0(st):
            W = Weights(st, sem("x0_weights_loaded"))
            w = dict(wq=W.rows("x0_wqT", "L0_xattn_WqT"), wk=W.rows("x0_wk", "L0_xattn_Wk"),
                     wv=W.rows("x0_wvT", "L0_xattn_WvT"), wfc=W.rows("x0_wfcT", "L0_xattn_WfcT"),
                     bq=W.plain("x0_bq", "L0_xattn_bq"), bk=W.plain("x0_bk", "L0_xattn_bk"),
                     bv=W.plain("x0_bv", "L0_xattn_bv"), bout=W.on_all("x0_bfc", "L0_xattn_bfc"),
                     maski=W.put("maski", [P, T], a["mask_BxS_ik1"].rearrange("b s -> (b s)").partition_broadcast(P), I32),
                     maskci=W.plain("maskci", "mask_col", I32))
            w["maskf"] = w["maski"][:].bitcast(F32)
            w["maskcf"] = w["maskci"][:].bitcast(F32)
            w["negc"] = sb("negc", [P, NT], own=st)
            w["loaded"], w["loads"] = W.s, 16 * len(W.loads)
            return w, W.loads

        def weights_x1(st):
            W = Weights(st, sem("x1_weights_loaded"))
            w = dict(wq=W.rows("x1_wq", "L1_xattn_Wq"), wk=W.rows("x1_wkT", "L1_xattn_WkT"), wv=W.rows("x1_wv", "L1_xattn_Wv"),
                     bq=W.plain("x1_bq", "L1_xattn_bq"), bk=W.plain("x1_bk", "L1_xattn_bk"), bv=None,
                     bout=W.on_all("x1_bv", "L1_xattn_bv"))
            w["loaded"], w["loads"] = W.s, 16 * len(W.loads)
            return w, W.loads

        def load_columns(eng, q, u, ctxT, s):
            eng.dma_start(ctxT[:, u, :, :, :].rearrange("p b h k -> p (b h) k"),
                          a["ctx_T"][ds(q * 4, 4), :, :].rearrange("x p k -> p x k")).then_inc(s[u], 16)

        def load_rows(eng, q, u, ctxN, s):
            eng.dma_start(ctxN[:, u, :, 0:KC, :].rearrange("p b c d -> p b (c d)"),
                          a["ctx_1024"][ds(q * 2, 2), 0:KC * P, :].rearrange("b (p c) d -> p b (c d)", c=KC)
                          ).then_inc(s[u], 16)
            eng.dma_start(ctxN[0:KR, u, :, KC, :],
                          a["ctx_1024"][ds(q * 2, 2), KC * P:NK, :].rearrange("b p d -> p b d")).then_inc(s[u], 16)

        s_ctx = [sem(f"ctx_rows_loaded{u}") for u in range(2)]
        s_ctxT = [sem(f"ctx_cols_loaded{u}") for u in range(2)]
        x_done = [0]
        s_qmm = sem("x_q_product")
        s_q = sem("x_q_ready")
        s_q2mm = sem("x_qk_product")
        s_qb = sem("x_q_dot_bk")
        s_q2 = sem("x_qk_ready")
        s_rc = sem("x_constants_ready")
        s_qc = sem("x_qcur_ready")
        s_sc = sem("x_scores_done")
        s_mx = sem("x_max_taken")
        s_ex = sem("x_exp_done")
        s_pt = sem("x_probs_transposed")
        s_pca = sem("x_probsT_copied_act")
        s_pcv = sem("x_probsT_copied_dve")
        s_pv = sem("x_pv_done")
        s_un = sem("x_u_normalised")
        s_ut = sem("x_u_transposed")
        s_uc = sem("x_uT_copied")
        s_vmm = sem("x_v_product")
        s_v = sem("x_v_ready")
        s_omm = sem("x_out_product")
        s_res = sem("x_residual_added")
        s_bias = sem("x_out_bias_added")

        def cross_attention(l, make_weights, masked):
            st = ExitStack()
            rt = x_done[0] * 16 * (NT // 2)
            rr = x_done[0] * 32 * (NT // 2)
            r = x_done[0]
            p0 = r * NT
            x_done[0] += 1
            ctxN = sb(l + "ctxN", [P, 2, 2, NC_, D], own=st)
            ctxT = sb(l + "ctxT", [P, 2, 2, DH, NK], own=st)
            w, loads = make_weights(st)

            def starts(sp):
                issue(sp, loads)
                load_columns(sp, 0, 0, ctxT, s_ctxT)
                load_columns(sp, 1, 1, ctxT, s_ctxT)
                load_rows(sp, 0, 0, ctxN, s_ctx)
                load_rows(sp, 1, 1, ctxN, s_ctx)
            layer_norm(starts)
            own = lambda name, shape, dt=F32: sb(l + name, shape, dt, own=st)
            wq, wk, wv, bq, bk, bv = (w[k] for k in ("wq", "wk", "wv", "bq", "bk", "bv"))
            s_w = w["loaded"]
            QT = own("QT", [P, DH, T])
            Q2T = own("Q2T", [P, DH, T])
            rowc = own("rowc", [P, NT])
            def pe_queries(pe, n, banks):
                for e in range(DH):
                    for h in range(DH):
                        mm = pe.matmul(ps[:, banks[e], :], wq[:, h, e * P:(e + 1) * P], xnT[:, h, n * 512:(n + 1) * 512],
                                       start=h == 0, stop=h == DH - 1)
                    mm.then_inc(s_qmm, 1)

            def pe_carried(pe, n, banks):
                pe.wait_ge(s_q, 4 * r + 2 * n + 2)
                for e in range(DH):
                    for h in range(DH):
                        mm = pe.matmul(ps[:, banks[e], :], wk[:, h, e * P:(e + 1) * P], QT[:, h, n * 512:(n + 1) * 512],
                                       start=h == 0, stop=h == DH - 1)
                    mm.then_inc(s_q2mm, 1)

            def pe_constants(pe, n, bank):
                for j in range(4):
                    for h in range(DH):
                        mm = pe.matmul(ps[:, bank, j:j + 1], QT[:, h, (4 * n + j) * P:(4 * n + j + 1) * P], bk[:, h:h + 1],
                                       start=h == 0, stop=h == DH - 1)
                mm.then_inc(s_qb, 1)

            def act_queries(act, n, banks):
                for e in range(DH):
                    act.wait_ge(s_qmm, 4 * r + 2 * n + e + 1)
                    nc.scalar.activation(QT[:, e, n * 512:(n + 1) * 512], ps[:, banks[e], :], ACT.Identity,
                                         bias=bq[:, e:e + 1]).then_inc(s_q, 1)

            def vec_carried(dve, n, banks):
                for e in range(DH):
                    dve.wait_ge(s_q2mm, 4 * r + 2 * n + e + 1)
                    dst = Q2T[:, e, n * 512:(n + 1) * 512]
                    if masked:
                        ins = nc.vector.tensor_tensor(dst, ps[:, banks[e], :], w["maskf"][:, n * 512:(n + 1) * 512], ALU.mult)
                    else:
                        ins = nc.vector.tensor_copy(dst, ps[:, banks[e], :])
                    ins.then_inc(s_q2, 1)

            def vec_constants(dve, n, bank):
                dve.wait_ge(s_qb, 2 * r + n + 1)
                tiles = slice(4 * n, 4 * n + 4)
                if masked:
                    nc.vector.scalar_tensor_tensor(rowc[:, tiles], ps[:, bank, 0:4], 1.0 / 16, w["maskcf"][:, tiles],
                                                   ALU.mult, ALU.mult).then_inc(s_rc, 1)
                    dve.drain()
                    nc.vector.tensor_tensor(rowc[:, tiles], rowc[:, tiles], w["negc"][:, tiles], ALU.add)
                else:
                    nc.vector.tensor_scalar(rowc[:, tiles], ps[:, bank, 0:4], 1.0 / 16, None, ALU.mult).then_inc(s_rc, 1)

            with nc.Block(no_gpsimd_drain=True) as block:
                @block.tensor
                def _(pe):
                    pe.wait_ge(s_w, w["loads"])
                    pe_queries(pe, 0, (0, 1))
                    pe_carried(pe, 0, (4, 5))
                    pe_constants(pe, 0, 2)

                @block.scalar
                def _(act):
                    act.wait_ge(s_w, w["loads"])
                    act_queries(act, 0, (0, 1))

                @block.vector
                def _(dve):
                    dve.wait_ge(s_w, w["loads"])
                    if masked:
                        nc.vector.tensor_copy(w["maskf"], w["maski"][:])
                        nc.vector.tensor_copy(w["maskcf"], w["maskci"][:])
                        dve.drain()
                        nc.vector.tensor_scalar(w["negc"][:], w["maskcf"], -NEG, NEG, ALU.mult, ALU.add)
                        dve.drain()
                    vec_carried(dve, 0, (4, 5))
                    vec_constants(dve, 0, 2)

            qcur = own("qcur", [P, 2, DH, P])
            prob = own("prob", [P, 2, NK])
            pT = own("pT", [P, 2, NC_, P])
            un = own("un", [P, 2, D])
            UT = own("UT", [P, 2, DH, P])
            vT = own("vT", [P, 2, DH, P])
            mx = own("mx", [P, 2])
            en = own("en", [P, 2])
            nb = own("nb", [P, 2])
            ssum = own("ssum", [P, 2])
            rsum = own("rsum", [P, 2])
            groups = [(0, 4), (4, 8), (8, 12), (12, 13)]
            with nc.Block(no_gpsimd_drain=True) as block:
                def pe_scores(pe, p, u, q):
                    wait(pe, s_qc, (p + p0) + 1)
                    pe.wait_ge(s_ctxT[u], q * 16 + rt + 16)
                    wait(pe, s_ex, (p + p0))
                    for n in range(4):
                        k0, k1 = n * 512, min(NK, n * 512 + 512)
                        for h in range(DH):
                            for b in range(2):
                                mm = pe.matmul(ps[64 * b:64 * b + 64, n, 0:k1 - k0], qcur[:, u, h, 64 * b:64 * b + 64],
                                               ctxT[:, u, b, h, k0:k1], start=h == 0, stop=h == DH - 1)
                    mm.then_inc(s_sc, 1)

                def pe_transposes(pe, p, u):
                    pe.wait_ge(s_ex, (p + p0) + 1)
                    for g, (c0, c1) in enumerate(groups):
                        if g < 2:
                            wait(pe, s_pca if g == 0 else s_pcv, 2 * (p + p0))
                        else:
                            pe.wait_ge(s_pca if g == 2 else s_pcv, 2 * (p + p0) + 1)
                        for c in range(c0, c1):
                            k = P if c < KC else KR
                            src = prob[:, u, c:KC * P:KC] if c < KC else prob[:, u, KC * P:NK]
                            mm = pe.transpose(ps[0:k, 4 + g % 2, (c - c0) * P:(c - c0 + 1) * P], src, ident[:])
                        mm.then_inc(s_pt, 1)

                def pe_pv(pe, p, u, q):
                    pe.wait_ge(s_pca, 2 * (p + p0) + 2)
                    pe.wait_ge(s_pcv, 2 * (p + p0) + 2)
                    pe.wait_ge(s_ctx[u], q * 32 + rr + 32)
                    wait(pe, s_un, (p + p0))
                    if not (isinstance(p, int) and p < 2):
                        pe.wait_ge(s_res, p + p0 - 1)
                    for c in range(NC_):
                        k = P if c < KC else KR
                        for b in range(2):
                            mm = pe.matmul(ps[64 * b:64 * b + 64, 6, 0:D], pT[0:k, u, c, 64 * b:64 * b + 64],
                                           ctxN[0:k, u, b, c, :], start=c == 0, stop=c == NC_ - 1)
                    mm.then_inc(s_pv, 1)

                def pe_ut(pe, p, u):
                    pe.wait_ge(s_un, (p + p0) + 1)
                    wait(pe, s_uc, (p + p0))
                    if masked:
                        wait(pe, s_v, p)
                    for h in range(DH):
                        mm = pe.transpose(ps[:, 7, h * P:(h + 1) * P], un[:, u, h * P:(h + 1) * P], ident[:])
                    mm.then_inc(s_ut, 1)

                def pe_v(pe, p, u):
                    if masked:
                        pe.wait_ge(s_uc, p + 1)
                        for e in range(DH):
                            for h in range(DH):
                                mm = pe.matmul(ps[:, 7, D + e * P:D + (e + 1) * P], wv[:, h, e * P:(e + 1) * P], UT[:, u, h, :],
                                               start=h == 0, stop=h == DH - 1)
                        mm.then_inc(s_vmm, 1)

                def pe_out(pe, p, u):
                    if masked:
                        pe.wait_ge(s_v, p + 1)
                    else:
                        pe.wait_ge(s_uc, p + p0 + 1)
                    src, ww = (vT, w["wfc"]) if masked else (UT, wv)
                    for h in range(DH):
                        mm = pe.matmul(ps[:, 6, D:2 * D], src[:, u, h, :], ww[:, h, :], start=h == 0, stop=h == DH - 1)
                    mm.then_inc(s_omm, 1)

                @block.tensor
                def _(pe):
                    pe_scores(pe, 0, 0, 0)
                    pe_queries(pe, 1, (6, 7))
                    pe_transposes(pe, 0, 0)
                    pe_carried(pe, 1, (6, 7))
                    pe.wait_ge(s_q2, 4 * r + 4)
                    pe_constants(pe, 1, 7)

                    def step(p, u, q, qb):
                        pe_scores(pe, p, u, q)
                        if not (isinstance(p, int) and p < 2):
                            pe_v(pe, p - 2, u)
                        pe_pv(pe, p - 1, 1 - u, qb)
                        pe_transposes(pe, p, u)
                        if isinstance(p, int) and p == 1:
                            pe.wait_ge(s_rc, 2 * r + 2)
                        pe_ut(pe, p - 1, 1 - u)
                        if not (isinstance(p, int) and p < 2):
                            pe_out(pe, p - 2, u)
                    step(1, 1, 0, 0)
                    step(2, 0, 1, 0)
                    with pe.Fori(1, NT // 2 - 1) as i:
                        step(i * 2 + 1, 1, i, i)
                        step(i * 2 + 2, 0, i + 1, i)
                    step(NT - 1, 1, NT // 2 - 1, NT // 2 - 1)
                    pe_v(pe, NT - 2, 0)
                    pe_pv(pe, NT - 1, 1, NT // 2 - 1)
                    pe_ut(pe, NT - 1, 1)
                    pe_out(pe, NT - 2, 0)
                    pe_v(pe, NT - 1, 1)
                    pe.wait_ge(s_res, p0 + NT - 1)
                    pe_out(pe, NT - 1, 1)

                def vec_max(dve, p, u):
                    dve.wait_ge(s_sc, (p + p0) + 1)
                    nc.vector.tensor_reduce(mx[:, u:u + 1], ps[:, 0:4, :].rearrange("p a n -> p (a n)")[:, 0:NK], AX, ALU.max)
                    dve.drain()
                    nc.vector.scalar_tensor_tensor(en[:, u:u + 1], mx[:, u:u + 1], 1.0 / 16, rowc[:, ds(p, 1)], ALU.mult, ALU.add)
                    dve.drain()
                    nc.vector.tensor_tensor(nb[:, u:u + 1], rowc[:, ds(p, 1)], en[:, u:u + 1], ALU.subtract).then_inc(s_mx, 1)

                def copy_group(eng, op, p, u, g, s):
                    c0, c1 = groups[g]
                    eng.wait_ge(s_pt, 4 * (p + p0) + g + 1)
                    if not (isinstance(p, int) and p < 2):
                        wait(eng, s_pv, (p + p0) - 1)
                    k = P if c0 < KC else KR
                    op(pT[0:k, u, c0:c1, :], ps[0:k, 4 + g % 2, 0:(c1 - c0) * P].rearrange("p (c t) -> p c t", c=c1 - c0)
                       ).then_inc(s, 1)

                def vec_norm(dve, p, u):
                    dve.wait_ge(s_pv, (p + p0) + 1)
                    if not (isinstance(p, int) and p < 2):
                        wait(dve, s_ut, (p + p0) - 1)
                    nc.vector.reciprocal(rsum[:, u:u + 1], ssum[:, u:u + 1])
                    dve.drain()
                    nc.vector.tensor_scalar(un[:, u, :], ps[:, 6, 0:D], rsum[:, u:u + 1], None, ALU.mult).then_inc(s_un, 1)

                def vec_residual(dve, p):
                    dve.wait_ge(s_omm, p + p0 + 1)
                    nc.vector.tensor_tensor(xt[:, ds(p, 1), :], xt[:, ds(p, 1), :], ps[:, 6:7, D:2 * D], ALU.add).then_inc(s_res, 1)

                @block.vector
                def _(dve):
                    vec_max(dve, 0, 0)
                    copy_group(dve, nc.vector.tensor_copy, 0, 0, 1, s_pcv)
                    copy_group(dve, nc.vector.tensor_copy, 0, 0, 3, s_pcv)
                    vec_carried(dve, 1, (6, 7))
                    vec_constants(dve, 1, 7)

                    def step(p, u):
                        vec_max(dve, p, u)
                        vec_norm(dve, p - 1, 1 - u)
                        copy_group(dve, nc.vector.tensor_copy, p, u, 1, s_pcv)
                        copy_group(dve, nc.vector.tensor_copy, p, u, 3, s_pcv)
                        if not (isinstance(p, int) and p < 2):
                            vec_residual(dve, p - 2)
                    step(1, 1)
                    dve.wait_ge(s_bias, NT * r + NT)
                    step(2, 0)
                    with dve.Fori(1, NT // 2 - 1) as i:
                        step(i * 2 + 1, 1)
                        step(i * 2 + 2, 0)
                    step(NT - 1, 1)
                    vec_norm(dve, NT - 1, 1)
                    vec_residual(dve, NT - 2)
                    vec_residual(dve, NT - 1)

                def act_exp(act, p, u):
                    act.wait_ge(s_mx, (p + p0) + 1)
                    if not (isinstance(p, int) and p < 2):
                        wait(act, s_pt, 4 * (p + p0) - 4)
                        wait(act, s_un, (p + p0) - 1)
                    nc.scalar.activation(prob[:, u, :], ps[:, 0:4, :].rearrange("p a n -> p (a n)")[:, 0:NK], ACT.Exp,
                                         bias=nb[:, u:u + 1], scale=1.0 / 16, accum_out=ssum[:, u:u + 1]).then_inc(s_ex, 1)

                def act_ut(act, p, u):
                    act.wait_ge(s_ut, p + p0 + 1)
                    nc.scalar.copy(UT[:, u, :, :], ps[:, 7, 0:D].rearrange("p (h t) -> p h t", h=DH)).then_inc(s_uc, 1)

                def act_v(act, p, u):
                    if masked:
                        act.wait_ge(s_vmm, p + 1)
                        for e in range(DH):
                            ins = nc.scalar.activation(vT[:, u, e, :], ps[:, 7, D + e * P:D + (e + 1) * P], ACT.Identity,
                                                       bias=bv[:, e:e + 1])
                        ins.then_inc(s_v, 1)

                @block.scalar
                def _(act):
                    act_exp(act, 0, 0)
                    act_queries(act, 1, (6, 7))
                    copy_group(act, nc.scalar.copy, 0, 0, 0, s_pca)
                    copy_group(act, nc.scalar.copy, 0, 0, 2, s_pca)

                    def step(p, u):
                        act_exp(act, p, u)
                        if not (isinstance(p, int) and p < 2):
                            act_v(act, p - 2, u)
                        copy_group(act, nc.scalar.copy, p, u, 0, s_pca)
                        copy_group(act, nc.scalar.copy, p, u, 2, s_pca)
                        act_ut(act, p - 1, 1 - u)
                    step(1, 1)
                    step(2, 0)
                    with act.Fori(1, NT // 2 - 1) as i:
                        step(i * 2 + 1, 1)
                        step(i * 2 + 2, 0)
                    step(NT - 1, 1)
                    act_v(act, NT - 2, 0)
                    act_ut(act, NT - 1, 1)
                    act_v(act, NT - 1, 1)

                @block.gpsimd
                def _(pool):
                    def load_q(p, u):
                        if not (isinstance(p, int) and p < 2):
                            wait(pool, s_sc, (p + p0) - 1)
                        nc.gpsimd.tensor_copy(qcur[:, u, :, :], Q2T[:, :, ds(p * P, P)]).then_inc(s_qc, 1)
                    load_q(0, 0)
                    load_q(1, 1)
                    for j in range(NT):
                        nc.gpsimd.tensor_tensor(xt[:, j, :], xt[:, j, :], w["bout"][:], ALU.add).then_inc(s_bias, 1)
                    pool.wait_ge(s_q2, 4 * r + 4)
                    with pool.Fori(1, NT // 2) as i:
                        load_q(i * 2, 0)
                        load_q(i * 2 + 1, 1)

                @block.sync
                def _(sp):
                    def step(p, u, last=False):
                        if not last:
                            sp.wait_ge(s_sc, (p + p0) + 1)
                            load_columns(sp, p + 2, u, ctxT, s_ctxT)
                        if not (isinstance(p, int) and p < 1):
                            sp.wait_ge(s_pv, (p + p0))
                            load_rows(sp, p + 1, 1 - u, ctxN, s_ctx)
                    step(0, 0)
                    step(1, 1)
                    with sp.Fori(1, NT // 2 - 1) as i:
                        step(i * 2, 0)
                        step(i * 2 + 1, 1)
                    step(NT - 2, 0, True)

            st.close()

        def latent_and_ffn():
            st = ExitStack()
            W = Weights(st, sem("latent_weights_loaded"))
            wdq = W.plain("wdq", "L0_attn_W_DQ8")
            wuq = W.plain("wuq", "L0_attn_W_UQT")
            wdkv = W.rows("wdkv", "L0_attn_W_DKV8")
            wukv = W.rows("wukv", "L0_attn_W_UKVT")
            wkr = W.plain("wkr", "L0_attn_W_KR8")
            wqr = W.plain("wqr", "L0_attn_W_QR")
            wo = W.plain("wo", "L0_attn_W_OT")
            c_bd = W.plain("c_bd", "c_blockdiag")
            c_head = W.plain("c_head", "c_head")
            c_causal = W.plain("c_causal", "c_causal")
            pe_t = W.plain("pe_t", "c_positions")
            sig = W.plain("sig", "L0_ffn_sigsT")
            fb = W.put("fb", [1, NTILE, D], a["L0_ffn_b"].rearrange("(o t) d -> o t d", o=1))
            qkw = sb("qkw", [P, 32, 16], own=st)
            for i, n in enumerate(("q", "k")):
                wsrc = a[f"L0_attn_{n}_norm_w"].partition_broadcast(P)
                for h in range(2):
                    o = h * 16 + i * 8
                    W.loads.append((qkw[:, o:o + 8, :], wsrc.unsqueeze(1).broadcast_to([P, 8, 16]), W.s))
            s_lw, n_lw = W.s, 16 * len(W.loads)
            bd = sb("bd", [P, 3, P], own=st)
            bdv = sb("bdv", [P, P], own=st)
            sel = sb("sel", [P, NTILE, S], own=st)
            fbias = sb("fbias", [P, D], own=st)
            WF = Weights(st, sem("ffn_weights_loaded"))
            wf = WF.put("wf", [P, NTILE * DH, D], a["L0_ffn_WT"].rearrange("(t p) e -> p t e", p=P))
            s_fw, n_fw = WF.s, 16

            def latent_setup():
                with ExitStack() as st:
                    own = lambda name, shape, dt=F32: sb("la_" + name, shape, dt, own=st)
                    wvc = own("wvc", [HD0, 8, HD0])
                    sgn = own("sgn", [32, NTILE])
                    neg = own("neg", [32, NTILE])
                    top = own("top", [P, S])
                    taken = own("taken", [P, S])
                    sel2 = own("sel2", [1, NTILE, 2, S])
                    s_mm = sem("la_composite_product")
                    s_bd = sem("la_composite_ready")
                    s_vc = sem("la_value_product")
                    s_vcc = sem("la_value_copied")
                    s_sg = sem("router_signs_ready")
                    s_rs = sem("router_scores")
                    s_sel = sem("router_chosen")
                    s_fb = sem("ffn_bias_product")
                    with nc.Block(no_gpsimd_drain=True) as block:
                        @block.tensor
                        def _(pe):
                            pe.wait_ge(s_lw, n_lw)

                            def tiled(x):
                                return bc(x, 1, 8)
                            mm = pe.matmul(ps[:, 0, 0:P], wdq[:], tiled(wuq[:]), start=True, stop=True)
                            for h in range(2):
                                mm = pe.matmul(ps[:, 1, 0:P], wdkv[:, h, :], tiled(wukv[:, h, 0:HD0]), start=h == 0, stop=h == 1)
                            mm = pe.matmul(ps[:, 2, 0:P], wkr[:], tiled(wqr[:]), start=True, stop=True)
                            for h in range(2):
                                mm = pe.matmul(ps[0:HD0, 4, 0:HD0], wukv[:, h, HD0:2 * HD0], wdkv[:, h, 0:HD0], start=h == 0, stop=h == 1)
                            mm.then_inc(s_vc, 1)
                            pe.wait_ge(s_vcc, 1)
                            pe.matmul(ps[:, 3, 0:P], wvc[:].rearrange("p x d -> p (x d)"), tiled(wo[:]), start=True, stop=True).then_inc(s_mm, 1)
                            pe.wait_ge(s_sg, 1)
                            for t in range(NTILE):
                                mm = pe.matmul(ps[:, 5, t * S:(t + 1) * S], sgn[:, t:t + 1].broadcast_to([32, P]), pe_t[:],
                                               start=True, stop=True)
                            mm.then_inc(s_rs, 1)
                            pe.wait_ge(s_sel, 1)
                            for t in range(NTILE):
                                mm = pe.matmul(ps[:, 6, 0:D], sel2[0:1, t, :, :].rearrange("p b s -> p (b s)"), fb[0:1, t, :],
                                               start=t == 0, stop=t == NTILE - 1)
                            mm.then_inc(s_fb, 1)

                        @block.vector
                        def _(dve):
                            dve.wait_ge(s_lw, n_lw)
                            nc.vector.tensor_scalar(neg[:], sig[:], 0.0, None, ALU.is_lt)
                            nc.vector.tensor_scalar(sgn[:], sig[:], 0.0, None, ALU.is_gt)
                            dve.drain()
                            nc.vector.tensor_tensor(sgn[:], sgn[:], neg[:], ALU.subtract).then_inc(s_sg, 1)
                            dve.wait_ge(s_vc, 1)
                            nc.vector.tensor_copy(wvc[:], bc(ps[0:HD0, 4, 0:HD0], 1, 8)).then_inc(s_vcc, 1)
                            dve.wait_ge(s_mm, 1)
                            for i in range(3):
                                nc.vector.tensor_tensor(bd[:, i, :], ps[:, i, 0:P], c_bd[:], ALU.mult)
                            nc.vector.tensor_tensor(bdv[:], ps[:, 3, 0:P], c_bd[:], ALU.mult)
                            dve.wait_ge(s_rs, 1)
                            sc = ps[:, 5, :].rearrange("p (t s) -> p t s", t=NTILE)
                            nc.vector.tensor_reduce(top[:], sc.rearrange("p t s -> p s t"), AX, ALU.max)
                            nc.vector.memset(taken[:], 0.0)
                            dve.drain()
                            nc.vector.tensor_tensor(sel[:], sc, bc(top[:], 1, NTILE), ALU.is_equal)
                            dve.drain()
                            for t in range(NTILE):
                                nc.vector.tensor_tensor(sel[:, t, :], sel[:, t, :], taken[:], ALU.is_gt)
                                dve.drain()
                                last = nc.vector.tensor_tensor(taken[:], taken[:], sel[:, t, :], ALU.max)
                                dve.drain()
                            nc.vector.tensor_copy(sel2[:], bc(sel[0:1, :, :], 2, 2)).then_inc(s_sel, 1)
                            dve.wait_ge(s_fb, 1)
                            nc.vector.tensor_copy(fbias[:], ps[:, 6, 0:D])

            def latent_attention():
                st = ExitStack()
                own = lambda name, shape, dt=F32: sb("la_" + name, shape, dt, own=st)
                sq = own("sq", [P, 2, 2, 2 * P])
                ms = own("ms", [P, 2, 32])
                rs = own("rs", [P, 2, 32])
                qk = own("qk", [P, 2, 2, 2, P])
                qkT = own("qkT", [P, 4, T])
                vz = own("vz", [P, B, NPAIR, 34])
                s_pj = sem("la_projected")
                s_sq = sem("la_squared")
                s_ms = sem("la_meansq")
                s_rs = sem("la_rms")
                s_rn = sem("la_scaled")
                s_wn = sem("la_weighted")
                s_kx = sem("la_qk_ready")
                s_tr = sem("la_qk_transposed")
                s_tc = sem("la_qkT_copied")
                s_v = sem("la_v_product")
                s_vz = sem("la_v_filled")
                s_vz0 = sem("la_v_cleared")
                with nc.Block(no_gpsimd_drain=True) as block:
                    @block.tensor
                    def _(pe):
                        def project(j):
                            wait(pe, s_kx, j - 1)
                            u = j % 2
                            for h in range(DH):
                                mm = pe.matmul(ps[:, 2 * u + h, 0:3 * P], xnT[:, h, j * P:(j + 1) * P],
                                               bd[:].rearrange("p i e -> p (i e)"), start=True, stop=True)
                            mm.then_inc(s_pj, 1)

                        def values(j):
                            wait(pe, s_vz, 2 * (j - 1))
                            for b in range(2):
                                for h in range(DH):
                                    for par in range(2):
                                        mm = pe.matmul(ps[64 * par:64 * par + 64, 6 + j % 2, (b * DH + h) * 64:(b * DH + h + 1) * 64],
                                                       xnT[:, h, (2 * j + b) * S:(2 * j + b + 1) * S],
                                                       bdv[:].rearrange("p (x r d) -> p x r d", r=2, d=16)[:, :, par, :], start=True, stop=True)
                            mm.then_inc(s_v, 1)

                        def turn(j):
                            pe.wait_ge(s_kx, j + 1)
                            wait(pe, s_tc, j - 1)
                            for i in range(4):
                                mm = pe.transpose(ps[:, 4 + j % 2, i * P:(i + 1) * P], qk[:, j % 2, i // 2, i % 2, :], ident[:])
                            mm.then_inc(s_tr, 1)
                        project(0)
                        for j in range(NT):
                            values(j)
                            if j + 1 < NT:
                                project(j + 1)
                            turn(j)

                    @block.scalar
                    def _(act):
                        for j in range(NT + 1):
                            if j < NT:
                                u = j % 2
                                act.wait_ge(s_pj, j + 1)
                                wait(act, s_ms, j - 1)
                                nc.scalar.activation(sq[:, u, :, :], ps[:, 2 * u:2 * u + 2, 0:2 * P], ACT.Square).then_inc(s_sq, 1)
                                act.wait_ge(s_ms, j + 1)
                                wait(act, s_rn, j - 1)
                                nc.scalar.activation(rs[:, u, :], ms[:, u, :], ACT.Sqrt).then_inc(s_rs, 1)
                            if j >= 1:
                                act.wait_ge(s_tr, j)
                                nc.scalar.copy(qkT[:, :, (j - 1) * P:j * P],
                                               ps[:, 4 + (j - 1) % 2, :].rearrange("p (i t) -> p i t", i=4)).then_inc(s_tc, 1)

                    @block.vector
                    def _(dve):
                        def value_blocks(j):
                            dve.wait_ge(s_v, j + 1)
                            dve.wait_ge(s_vz0, 3)
                            for par in range(2):
                                r = slice(64 * par, 64 * par + 64)
                                nc.vector.tensor_copy(vz[r, 2 * j:2 * j + 2, :, 17 * par:17 * par + 16].rearrange("p b h d -> p (b h) d"),
                                                      ps[r, 6 + j % 2, 0:D].rearrange("p (x d) -> p x d", d=16)
                                                      ).then_inc(s_vz, 1)
                        def rotary_part(j):
                            u = j % 2
                            dve.wait_ge(s_wn, j + 1)
                            nc.vector.tensor_tensor(qk[:, u, :, 1, :], qk[:, u, :, 1, :], ps[:, 2 * u:2 * u + 2, 2 * P:3 * P],
                                                    ALU.add).then_inc(s_kx, 1)

                        for j in range(NT):
                            u = j % 2
                            dve.wait_ge(s_sq, j + 1)
                            wait(dve, s_rs, j - 1)
                            nc.vector.tensor_reduce(ms[:, u, :], sq[:, u, :, :].rearrange("p h (x d) -> p (h x) d", d=16), AX, ALU.add)
                            dve.drain()
                            nc.vector.tensor_scalar(ms[:, u, :], ms[:, u, :], 1.0 / HD0, 1.1920929e-07, ALU.mult, ALU.add).then_inc(s_ms, 1)
                            if j >= 1:
                                rotary_part(j - 1)
                            value_blocks(j)
                            dve.wait_ge(s_rs, j + 1)
                            nc.vector.reciprocal(rs[:, u, :], rs[:, u, :])
                            wait(dve, s_tr, j - 1)
                            dve.drain()
                            nc.vector.tensor_tensor(qk[:, u, :, :, :].rearrange("p h i (x d) -> p h (i x) d", d=16),
                                                    ps[:, 2 * u:2 * u + 2, 0:2 * P].rearrange("p h (x d) -> p h x d", d=16),
                                                    bc(rs[:, u, :].rearrange("p (h x) -> p h x", h=2), 3, 16), ALU.mult).then_inc(s_rn, 1)
                        rotary_part(NT - 1)

                    @block.gpsimd
                    def _(pool):
                        nc.gpsimd.memset(vz[:].rearrange("p b x d -> p (b x d)"), 0.0).then_inc(s_vz0, 1)
                        pool.wait_ge(s_vz0, 1)
                        nc.gpsimd.memset(vz[0:64, :, :, 16:17], 1.0).then_inc(s_vz0, 1)
                        pool.wait_ge(s_vz0, 2)
                        nc.gpsimd.memset(vz[64:128, :, :, 33:34], 1.0).then_inc(s_vz0, 1)
                        pool.wait_ge(s_vz0, 3)
                        for j in range(NT):
                            u = j % 2
                            pool.wait_ge(s_rn, j + 1)
                            nc.gpsimd.tensor_tensor(qk[:, u, :, :, :].rearrange("p h i (x d) -> p (h i x) d", d=16),
                                                    qk[:, u, :, :, :].rearrange("p h i (x d) -> p (h i x) d", d=16),
                                                    qkw[:], ALU.mult).then_inc(s_wn, 1)

                kz = own("kz", [P, 2, 2, 2, 8, S])
                sm = own("sm", [P, 2, H0, S])
                mx = own("mx", [P, 2, H0])
                pT = own("pT", [P, 2, NPAIR, P])
                rden = own("rden", [P, 2, H0])
                av = own("av", [P, 2, H0, HD0])
                s_kz = sem("la_keys_spread")
                s_sc = sem("la_scores_done")
                s_mk = sem("la_scores_masked")
                s_sb = sem("la_max_subtracted")
                s_ex = sem("la_exp_done")
                s_pt = sem("la_probs_transposed")
                s_pc = sem("la_probsT_copied")
                s_av = sem("la_av_done")
                s_nm = sem("la_normalised")
                s_ad = sem("la_added")
                with nc.Block(no_gpsimd_drain=True) as block:
                    def spread(pool, j):
                        u = j % 2
                        wait(pool, s_sc, j - 1)
                        for b in range(2):
                            for h in range(2):
                                ins = nc.gpsimd.tensor_tensor(kz[:, u, b, h, :, :], bc(qkT[:, 2 * h + 1, (2 * j + b) * S:(2 * j + b + 1) * S], 1, 8),
                                                              bc(c_head[:], 2, S), ALU.mult)
                        ins.then_inc(s_kz, 1)

                    @block.gpsimd
                    def _(pool):
                        def residual(j):
                            pool.wait_ge(s_nm, j + 1)
                            nc.gpsimd.tensor_tensor(xt[:, j, :], xt[:, j, :], av[:, j % 2, :, :].rearrange("p h d -> p (h d)"),
                                                    ALU.add).then_inc(s_ad, 1)
                        spread(pool, 0)
                        for j in range(NT):
                            if j + 1 < NT:
                                spread(pool, j + 1)
                            if j >= 1:
                                residual(j - 1)
                        residual(NT - 1)
                        pool.wait_ge(s_ad, NT)

                    @block.tensor
                    def _(pe):
                        def scores(j):
                            u = j % 2
                            pe.wait_ge(s_kz, j + 1)
                            wait(pe, s_mk, j - 1)
                            for h in range(2):
                                for b in range(2):
                                    mm = pe.matmul(ps[64 * b:64 * b + 64, 2 * u + h, :], qkT[:, 2 * h, (2 * j + b) * S:(2 * j + b + 1) * S],
                                                   kz[:, u, b, h, :, :].rearrange("p x k -> p (x k)"), start=True, stop=True)
                            mm.then_inc(s_sc, 1)

                        def turn(j):
                            u = j % 2
                            pe.wait_ge(s_ex, j + 1)
                            for g in range(2):
                                wait(pe, s_pc, 2 * j + g - 1)
                                for i in range(4):
                                    hp = 4 * g + i
                                    mm = pe.transpose(ps[:, 4 + g, i * P:(i + 1) * P],
                                                      sm[:, u, 2 * hp:2 * hp + 2, :].rearrange("p h k -> p (h k)"), ident[:])
                                mm.then_inc(s_pt, 1)

                        def mix(j):
                            u = j % 2
                            pe.wait_ge(s_pc, 2 * j + 2)
                            wait(pe, s_nm, j - 1)
                            for hp in range(NPAIR):
                                for b in range(2):
                                    mm = pe.matmul(ps[64 * b:64 * b + 64, 6 + u, hp * 34:hp * 34 + 34], pT[:, u, hp, 64 * b:64 * b + 64],
                                                   vz[:, 2 * j + b, hp, :], start=True, stop=True)
                            mm.then_inc(s_av, 1)
                        scores(0)
                        for j in range(NT):
                            if j + 1 < NT:
                                scores(j + 1)
                            turn(j)
                            mix(j)

                    @block.vector
                    def _(dve):
                        def soft(j):
                            u = j % 2
                            dve.wait_ge(s_sc, j + 1)
                            wait(dve, s_pt, 2 * (j - 1))
                            nc.vector.scalar_tensor_tensor(sm[:, u, :, :], ps[:, 2 * u:2 * u + 2, :].rearrange("p h (x k) -> p (h x) k", k=S),
                                                           float(HD0) ** -0.5, bc(c_causal[:], 1, H0), ALU.mult, ALU.add).then_inc(s_mk, 1)
                            dve.drain()
                            nc.vector.tensor_reduce(mx[:, u, :], sm[:, u, :, :], AX, ALU.max)
                            dve.drain()
                            nc.vector.tensor_tensor(sm[:, u, :, :], sm[:, u, :, :], bc(mx[:, u, :], 2, S), ALU.subtract).then_inc(s_sb, 1)

                        def norm(j):
                            u = j % 2
                            dve.wait_ge(s_av, j + 1)
                            wait(dve, s_ad, j - 1)
                            o = ps[:, 6 + u, 0:NPAIR * 34].rearrange("p (x d) -> p x d", d=17)
                            nc.vector.reciprocal(rden[:, u, :], o[:, :, 16])
                            dve.drain()
                            nc.vector.tensor_tensor(av[:, u, :, :], o[:, :, 0:HD0], bc(rden[:, u, :], 2, HD0), ALU.mult).then_inc(s_nm, 1)
                        for j in range(NT):
                            soft(j)
                            if j >= 1:
                                norm(j - 1)
                        norm(NT - 1)

                    @block.scalar
                    def _(act):
                        for j in range(NT):
                            u = j % 2
                            act.wait_ge(s_sb, j + 1)
                            nc.scalar.activation(sm[:, u, :, :], sm[:, u, :, :], ACT.Exp).then_inc(s_ex, 1)
                            wait(act, s_av, j - 1)
                            for g in range(2):
                                act.wait_ge(s_pt, 2 * j + g + 1)
                                nc.scalar.copy(pT[:, u, 4 * g:4 * g + 4, :],
                                               ps[:, 4 + g, :].rearrange("p (i t) -> p i t", i=4)).then_inc(s_pc, 1)
                st.close()

            def routed_ffn():
                st = ExitStack()
                xm = sb("ffn_masked", [P, 2, DH, T], F32, own=st)
                s_m = [sem("ffn_masked_dve"), sem("ffn_masked_pool")]
                s_mm = sem("ffn_product")
                s_bias = sem("ffn_bias_added")
                with nc.Block(no_gpsimd_drain=True) as block:
                    def mask(eng, e, h, t):
                        wait(eng, s_mm, t - 1)
                        e.tensor_tensor(xm[:, t % 2, h, :].rearrange("p (b s) -> p b s", s=S), xnT[:, h, :].rearrange("p (b s) -> p b s", s=S),
                                        bc(sel[:, t, :], 1, B), ALU.mult).then_inc(s_m[h], 1)

                    @block.gpsimd
                    def _(pool):
                        for t in range(NTILE):
                            mask(pool, nc.gpsimd, 1, t)
                        for j in range(NT):
                            nc.gpsimd.tensor_tensor(xt[:, j, :], xt[:, j, :], fbias[:], ALU.add).then_inc(s_bias, 1)

                    @block.tensor
                    def _(pe):
                        pe.wait_ge(s_fw, n_fw)
                        for t in range(NTILE):
                            pe.wait_ge(s_m[0], t + 1)
                            pe.wait_ge(s_m[1], t + 1)
                            for j in range(NT):
                                for h in range(DH):
                                    mm = pe.matmul(ps[:, j, 0:D], xm[:, t % 2, h, j * P:(j + 1) * P], wf[:, DH * t + h, :],
                                                   start=t == 0 and h == 0, stop=t == NTILE - 1 and h == 1)
                                if j == NT - 1 or t == NTILE - 1:
                                    mm.then_inc(s_mm, 1)

                    @block.vector
                    def _(dve):
                        for t in range(NTILE):
                            mask(dve, nc.vector, 0, t)
                        for j in range(NT):
                            dve.wait_ge(s_mm, NTILE + j)
                            dve.wait_ge(s_bias, j + 1)
                            nc.vector.tensor_tensor(xt[:, j, :], xt[:, j, :], ps[:, j, 0:D], ALU.add)
                st.close()

            layer_norm(lambda sp: issue(sp, W.loads + WF.loads))
            latent_setup()
            latent_attention()
            layer_norm(lambda sp: None)
            routed_ffn()
            st.close()

        def state_space():
            st = ExitStack()
            own = lambda name, shape, dt=F32: sb("ss_" + name, shape, dt, own=st)
            W = Weights(st, sem("mixer_weights_loaded"))
            win = W.rows("win", "L1_attn_W_inT")
            wdt = W.rows("wdt", "L1_attn_W_dtT")
            wout = W.rows("wout", "L1_attn_W_outT")
            cw = W.plain("cw", "L1_attn_conv")
            cb = W.plain("cb", "L1_attn_conv_b")
            al = W.plain("al", "L1_attn_A_log")
            dcol = W.put("dcol", [P, CI], a["L1_attn_D2"][0].partition_broadcast(P))
            dcol2 = W.put("dcol2", [P, CI], a["L1_attn_D2"][1].partition_broadcast(P))
            dtb = W.on_all("dtb", "L1_attn_dt_bias")
            c_sel = W.plain("c_sel", "c_segments")
            c_lvl = W.plain("c_lvl", "c_levels")
            s_w, n_w = W.s, 16 * len(W.loads)
            layer_norm(lambda sp: issue(sp, W.loads))

            xi = own("xi", [P, CI, B, S + 3])
            xc = own("xc", [P, CI, T])
            sz = own("sz", [P, CI, T])
            bT = own("bT", [P, CI, T])
            cT = own("cT", [P, CI, T])
            dt = own("dt", [P, NT * NH])
            tmp = own("tmp", [P, 8, NT * NH])
            aneg = own("aneg", [P, CI])
            xdt = own("xdt", [P, NT, NH * DS])
            s_pm = sem("ss_projected")
            s_ev = sem("ss_projection_copied")
            s_dtp = sem("ss_dt_product")
            s_dv = sem("ss_dt_vector_step")
            s_da = sem("ss_dt_scalar_step")
            s_a = sem("ss_A_exp")
            s_cv = sem("ss_convolved")
            s_cs = sem("ss_conv_gated")
            s_xt = sem("ss_x_transposed")
            s_xd = sem("ss_x_scaled")
            with nc.Block(no_gpsimd_drain=True) as block:
                def banks(m):
                    return 2 * (m % 4) if m < 3 * CI else 2 * (m % 2)

                @block.tensor
                def _(pe):
                    pe.wait_ge(s_w, n_w)
                    for j in range(NT):
                        for h in range(DH):
                            mm = pe.matmul(ps[:, 6, j * NH:(j + 1) * NH], xnT[:, h, j * P:(j + 1) * P], wdt[:, h, :],
                                           start=h == 0, stop=h == DH - 1)
                    mm.then_inc(s_dtp, 1)
                    for m in range(4 * CI):
                        wait(pe, s_ev, m - 3 if m < 3 * CI + 2 else m - 1)
                        if m == 3:
                            pe.wait_ge(s_dv, 1)
                        for n in range(2):
                            for h in range(DH):
                                mm = pe.matmul(ps[:, banks(m) + n, :], win[:, h, m * P:(m + 1) * P], xnT[:, h, n * 512:(n + 1) * 512],
                                               start=h == 0, stop=h == DH - 1)
                        mm.then_inc(s_pm, 1)
                        if m >= 3 * CI:
                            pe.wait_ge(s_ev, 3 * CI)
                            pe.wait_ge(s_cs, CI)
                            for j in (2 * (m - 3 * CI), 2 * (m - 3 * CI) + 1):
                                wait(pe, s_xd, j - 3)
                                for c in range(CI):
                                    mm = pe.transpose(ps[:, 4 + j % 4, c * P:(c + 1) * P], xc[:, c, j * P:(j + 1) * P], ident[:])
                                mm.then_inc(s_xt, 1)

                @block.scalar
                def _(act):
                    act.wait_ge(s_w, n_w)
                    nc.scalar.activation(aneg[:], al[:], ACT.Exp).then_inc(s_a, 1)
                    act.wait_ge(s_dv, 1)
                    nc.scalar.activation(tmp[:, 2, :], tmp[:, 1, :], ACT.Exp, scale=-1.0).then_inc(s_da, 1)
                    act.wait_ge(s_dv, 2)
                    nc.scalar.activation(tmp[:, 4, :], tmp[:, 3, :], ACT.Ln).then_inc(s_da, 1)
                    for m in range(4 * CI):
                        act.wait_ge(s_pm, m + 1)
                        src = ps[:, banks(m):banks(m) + 2, :].rearrange("p a n -> p (a n)")
                        c = m % CI
                        if m < CI:
                            nc.scalar.copy(xi[:, c, :, 3:S + 3], src.rearrange("p (b s) -> p b s", s=S)).then_inc(s_ev, 1)
                        elif m < 2 * CI:
                            nc.scalar.activation(sz[:, c, :], src, ACT.Silu).then_inc(s_ev, 1)
                        else:
                            nc.scalar.copy((bT if m < 3 * CI else cT)[:, c, :], src).then_inc(s_ev, 1)
                        if 2 * CI <= m < 3 * CI:
                            act.wait_ge(s_cv, c + 1)
                            nc.scalar.activation(xc[:, c, :], xc[:, c, :], ACT.Silu).then_inc(s_cs, 1)

                @block.vector
                def _(dve):
                    nc.vector.memset(xi[:, :, :, 0:3].rearrange("p c b k -> p (c b) k"), 0.0)
                    dve.wait_ge(s_w, n_w)
                    nc.vector.tensor_copy(dcol[64:128, :], dcol2[64:128, :])
                    dve.wait_ge(s_a, 1)
                    nc.vector.tensor_scalar(aneg[:], aneg[:], -1.0, None, ALU.mult)
                    dve.wait_ge(s_dtp, 1)
                    v, av, e, u, lnu, d, z, q = (tmp[:, i, :] for i in range(8))
                    nc.vector.tensor_tensor(v.rearrange("p (j n) -> p j n", n=NH), ps[:, 6, 0:NT * NH].rearrange("p (j n) -> p j n", n=NH),
                                            bc(dtb[:], 1, NT), ALU.add)
                    dve.drain()
                    nc.vector.scalar_tensor_tensor(av, v, -1.0, v, ALU.mult, ALU.max).then_inc(s_dv, 1)
                    dve.wait_ge(s_da, 1)
                    nc.vector.tensor_scalar(u, e, 1.0, None, ALU.add).then_inc(s_dv, 1)
                    dve.drain()
                    nc.vector.tensor_scalar(d, u, -1.0, None, ALU.add)
                    dve.drain()
                    nc.vector.tensor_scalar(z, d, 0.0, None, ALU.is_equal)
                    dve.drain()
                    nc.vector.tensor_tensor(d, d, z, ALU.add)
                    dve.drain()
                    nc.vector.reciprocal(q, d)
                    dve.drain()
                    nc.vector.tensor_tensor(q, q, e, ALU.mult)
                    nc.vector.tensor_tensor(z, z, e, ALU.mult)
                    dve.wait_ge(s_da, 2)
                    dve.drain()
                    nc.vector.tensor_tensor(q, q, lnu, ALU.mult)
                    dve.drain()
                    nc.vector.tensor_tensor(q, q, z, ALU.add)
                    nc.vector.tensor_scalar(v, v, 0.0, None, ALU.max)
                    dve.drain()
                    nc.vector.tensor_tensor(dt[:], q, v, ALU.add)
                    dve.drain()
                    for c in range(CI):
                        dve.wait_ge(s_ev, c + 1)
                        acc = xc[:, c, :].rearrange("p (b s) -> p b s", s=S)
                        nc.vector.tensor_scalar(acc, xi[:, c, :, 3:S + 3], cw[:, 4 * c + 3:4 * c + 4], cb[:, c:c + 1], ALU.mult, ALU.add)
                        for k in range(3):
                            dve.drain()
                            last = nc.vector.scalar_tensor_tensor(acc, xi[:, c, :, k:k + S], cw[:, 4 * c + k:4 * c + k + 1], acc,
                                                                  ALU.mult, ALU.add)
                        last.then_inc(s_cv, 1)
                    for j in range(NT):
                        dve.wait_ge(s_xt, j + 1)
                        nc.vector.tensor_tensor(xdt[:, j, :].rearrange("p (n d) -> p n d", d=DS),
                                                ps[:, 4 + j % 4, :].rearrange("p (n d) -> p n d", d=DS),
                                                bc(dt[:, j * NH:(j + 1) * NH], 2, DS), ALU.mult).then_inc(s_xd, 1)

            dec = own("dec", [P, 2, LV, T])
            pr = own("pr", [P, 2, 2, (LV + 1) * S])
            gm = own("gm", [P, 2, 2, S])
            yT = xi[:].rearrange("p c b s -> p (c b s)")[:, 0:CI * T].rearrange("p (c t) -> p c t", c=CI)
            s_sg = sem("ss_segments_summed")
            s_e = sem("ss_decay_ready")
            s_fl = sem("ss_left_factors")
            s_fr = sem("ss_right_factors")
            s_g = sem("ss_pair_products")
            s_gk = sem("ss_products_masked")
            s_gr = sem("ss_G_ready")
            s_y = sem("ss_y_product")
            s_yd = sem("ss_y_plus_Dx")
            s_yz = sem("ss_y_gated")
            with nc.Block(no_gpsimd_drain=True) as block:
                def seg_banks(c, j):
                    return 2 * (j % 2) if c == 0 else 0

                @block.tensor
                def _(pe):
                    def segments(c, j):
                        wait(pe, s_e, j - 1 if c == 0 else c * NT + j)
                        for a_ in range(2):
                            for par in range(2):
                                n = j * NH + 2 * c + par
                                mm = pe.matmul(ps[64 * par:64 * par + 64, seg_banks(c, j) + a_, 0:3 * P], dt[:, n:n + 1].broadcast_to([P, 64]),
                                               c_sel[:, a_ * 3 * P:(a_ + 1) * 3 * P], start=True, stop=True)
                        mm.then_inc(s_sg, 1)

                    def pairs(c, j):
                        k, u = c * NT + j, j % 2
                        pe.wait_ge(s_fl, LV * (c + 1))
                        pe.wait_ge(s_fr, LV * (c + 1))
                        wait(pe, s_gk, k - 1)
                        for l in range(LV + 1):
                            for b in range(2):
                                t0 = (2 * j + b) * S
                                for par in range(2):
                                    r = slice(64 * par, 64 * par + 64)
                                    f, g = (dec[r, c % 2, l, t0:t0 + S],) * 2 if l < LV else (bT[r, c, t0:t0 + S], cT[r, c, t0:t0 + S])
                                    mm = pe.matmul(ps[64 * b:64 * b + 64, 4 + 2 * u + par, l * S:(l + 1) * S], f, g, start=True, stop=True)
                        mm.then_inc(s_g, 1)

                    def apply(c, j):
                        k, u = c * NT + j, j % 2
                        pe.wait_ge(s_gr, k + 1)
                        wait(pe, s_yd, 2 * c)
                        for b in range(2):
                            for par in range(2):
                                n = 2 * c + par
                                r = slice(64 * b, 64 * b + 64)
                                mm = pe.matmul(ps[64 * par:64 * par + 64, 2 + b, j * S:(j + 1) * S], xdt[r, j, n * DS:(n + 1) * DS],
                                               gm[r, u, par, :], start=True, stop=True)
                        mm.then_inc(s_y, 1)
                    for j in range(NT):
                        segments(0, j)
                    for c in range(CI):
                        for j in range(NT):
                            if c + 1 < CI:
                                segments(c + 1, j)
                            pairs(c, j)
                            if j >= 1:
                                apply(c, j - 1)
                        apply(c, NT - 1)

                @block.scalar
                def _(act):
                    for c in range(CI):
                        for j in range(NT):
                            act.wait_ge(s_sg, c * NT + j + 1)
                            wait(act, s_g, (c - 1) * NT)
                            nc.scalar.activation(dec[:, c % 2, :, j * P:(j + 1) * P].rearrange("p (a l) t -> p a l t", a=2),
                                                 ps[:, seg_banks(c, j):seg_banks(c, j) + 2, 0:3 * P].rearrange("p a (l t) -> p a l t", l=3), ACT.Exp,
                                                 scale=aneg[:, c:c + 1]).then_inc(s_e, 1)

                def factors(eng, e, c, side, src, s, levels=range(LV)):
                    eng.wait_ge(s_e, NT * (c + 1))
                    for l in levels:
                        w = 32 >> l
                        f = dec[:, c % 2, l, :].rearrange("p (k r w) -> p k r w", r=2, w=w)[:, :, side, :]
                        g = src[:, c, :].rearrange("p (k r w) -> p k r w", r=2, w=w)[:, :, side, :]
                        e.tensor_tensor(f, f, g, ALU.mult).then_inc(s, 1)

                @block.gpsimd
                def _(pool):
                    for c in range(CI):
                        factors(pool, nc.gpsimd, c, 1, cT, s_fr, range(LV) if c else range(LV // 2))
                        if c >= 1:
                            pool.wait_ge(s_yd, 2 * c)
                            nc.gpsimd.tensor_tensor(yT[:, c - 1, :], yT[:, c - 1, :], sz[:, c - 1, :], ALU.mult).then_inc(s_yz, 1)
                    pool.wait_ge(s_yd, 2 * CI)
                    nc.gpsimd.tensor_tensor(yT[:, CI - 1, :], yT[:, CI - 1, :], sz[:, CI - 1, :], ALU.mult).then_inc(s_yz, 1)
                    pool.wait_ge(s_yz, CI)

                @block.vector
                def _(dve):
                    factors(dve, nc.vector, 0, 0, bT, s_fl)
                    factors(dve, nc.vector, 0, 1, cT, s_fr, range(LV // 2, LV))
                    for c in range(CI):
                        for j in range(NT):
                            k, u = c * NT + j, j % 2
                            dve.wait_ge(s_g, k + 1)
                            nc.vector.tensor_tensor(pr[:, u, :, :], ps[:, 4 + 2 * u:6 + 2 * u, 0:(LV + 1) * S], bc(c_lvl[:], 1, 2),
                                                    ALU.mult).then_inc(s_gk, 1)
                            wait(dve, s_y, k - 1)
                            dve.drain()
                            nc.vector.tensor_reduce(gm[:, u, :, :], pr[:, u, :, :].rearrange("p r (l t) -> p r t l", t=S), AX,
                                                    ALU.add).then_inc(s_gr, 1)
                        if c + 1 < CI:
                            factors(dve, nc.vector, c + 1, 0, bT, s_fl)
                        dve.wait_ge(s_y, NT * (c + 1))
                        for b in range(2):
                            def half(t):
                                return t.rearrange("p (j b s) -> p j b s", b=2, s=S)[:, :, b, :]
                            nc.vector.scalar_tensor_tensor(half(yT[:, c, :]), half(xc[:, c, :]), dcol[:, c:c + 1],
                                                           ps[:, 2 + b, :].rearrange("p (j s) -> p j s", s=S), ALU.mult, ALU.add
                                                           ).then_inc(s_yd, 1)

            s_o = sem("ss_out_product")
            with nc.Block(no_gpsimd_drain=True) as block:
                @block.tensor
                def _(pe):
                    for j in range(NT):
                        for c in range(CI):
                            mm = pe.matmul(ps[:, j, 0:D], yT[:, c, j * P:(j + 1) * P], wout[:, c, :], start=c == 0, stop=c == CI - 1)
                        mm.then_inc(s_o, 1)

                @block.vector
                def _(dve):
                    for j in range(NT):
                        dve.wait_ge(s_o, j + 1)
                        nc.vector.tensor_tensor(xt[:, j, :], xt[:, j, :], ps[:, j, 0:D], ALU.add)
            st.close()

        def experts():
            st = ExitStack()
            own = lambda name, shape, dt=F32: sb("moe_" + name, shape, dt, own=st)
            W = Weights(st, sem("moe_weights_loaded"))
            gw = W.rows("gw", "L1_ffn_gate_wT")
            gb = W.on_all("gb", "L1_ffn_gate_bias")
            wsgu = W.rows("wsgu", "moe_shared_gu")
            wsd = W.plain("wsd", "L1_ffn_Ws_down")
            c_lt = W.plain("c_lt", "c_lower")
            c_iota = W.plain("c_iota", "c_iota")
            c_first = W.plain("c_first", "c_first")
            c_next = W.plain("c_next", "c_next")
            c_col = W.plain("c_col", "c_col")
            c_before = W.plain("c_before", "c_before")
            c_tok = W.plain("c_tok", "c_tok")
            c_past = W.plain("c_past", "c_past")
            c_spare = W.plain("c_spare", "c_spare")
            s_w, n_w = W.s, 16 * len(W.loads)
            s_rows = sem("moe_rows_stored")
            layer_norm(lambda sp: issue(sp, W.loads))

            sg = own("sg", [P, NT, E])
            sc = own("sc", [P, NT, E])
            hi = own("hi", [P, NT * G, 7])
            lo = own("lo", [P, NT * G, 7])
            losers = own("losers", [P, NT * G, 2])
            gs = own("gs", [P, NT, G])
            cmp = own("cmp", [P, NT, G, G])
            eq = own("eq", [P, NT, G, G])
            gmask = own("gmask", [P, NT * G])
            goff = own("goff", [P, NT * G])
            top = own("top", [P, NT, 8])
            rep = own("rep", [P, NT, E])
            cwt = own("cwt", [P, NT, E])
            tot = own("tot", [P, NT])
            chb = own("chb", [P, NT, E], BF16)
            before = own("before", [P, P], BF16)
            ones = own("ones", [P, P], BF16)
            tok = own("tok", [P, 2, NT, 8], BF16)
            tab = own("tab", [P, NT, E, 4], BF16)
            rest = own("rest", [P, NT, E])
            allone = own("allone", [P, NT * E])
            rank = own("rank", [P, NT, E])
            tiles = own("tiles", [P, E])
            through = own("upto", [P, E])
            first = own("first", [P, E])
            unit = own("unit", [P, E])
            slot1 = own("slot1", [P, NT, E])
            owner = own("owner", [P, 1])
            etab = own("etab", [1, P], I32)
            LEAST, MOST = T * 8 // P // 4, (T * 8 // P + E) // 4
            trip = own("trip", [1, 1], I32)
            tripf = own("tripf", [1, 1])
            hs = own("hs", [P, 2, FE])
            hh = own("hh", [P, 2, FE])
            hT = own("hT", [P, 2, FE])
            up = own("up", [P, 2, FE])
            ysh = own("ysh", [P, 2, D])
            s_gp = sem("moe_gate_product")
            s_gu2, s_si2, s_hh2, s_ht2, s_hc2, s_dn2, s_yc2, s_ya2 = (sem("shared_" + n) for n in (
                "gate_up", "silu", "hidden", "transposed", "copied", "down", "result_copied", "added"))
            s_ge = sem("moe_gate_exp")
            s_ch = sem("moe_chosen")
            s_ct = sem("moe_counted")
            s_ow = sem("moe_owner_ready")
            s_et = sem("moe_owner_turned")
            with nc.Block(no_gpsimd_drain=True) as block:
                @block.sync
                def _(sp):
                    sp.dma_start(xn_rows.rearrange("(j p) d -> p j d", p=P), xn[:]).then_inc(s_rows, 16)

                @block.tensor
                def _(pe):
                    pe.wait_ge(s_w, n_w)
                    for j in range(NT):
                        for h in range(DH):
                            mm = pe.matmul(ps[:, 0, j * E:(j + 1) * E], xnT[:, h, j * P:(j + 1) * P], gw[:, h, :],
                                           start=h == 0, stop=h == DH - 1)
                    mm.then_inc(s_gp, 1)
                    for j in range(NT + 2):
                        if j < NT:
                            wait(pe, s_hh2, j - 1)
                            for h in range(DH):
                                mm = pe.matmul(ps[:, 4 + j % 2, 0:2 * FE], xnT[:, h, j * P:(j + 1) * P], wsgu[:, h, :],
                                               start=h == 0, stop=h == DH - 1)
                            mm.then_inc(s_gu2, 1)
                        if 1 <= j < NT + 1:
                            pe.wait_ge(s_hh2, j)
                            wait(pe, s_hc2, j - 1)
                            pe.transpose(ps[:, 6, 0:P], hh[:, (j - 1) % 2, :], ident[:]).then_inc(s_ht2, 1)
                        if j >= 2:
                            pe.wait_ge(s_hc2, j - 1)
                            wait(pe, s_yc2, j - 2)
                            pe.matmul(ps[:, 7, 0:D], hT[:, j % 2, :], wsd[:], start=True, stop=True).then_inc(s_dn2, 1)
                    pe.wait_ge(s_ch, 1)
                    for j in range(NT + 1):
                        o = ps[:, 1, j * E:(j + 1) * E] if j < NT else ps[:, 2, 0:E]
                        for i in range(min(j + 1, NT)):
                            mm = pe.matmul(o, before[:] if i == j else ones[:], chb[:, i, :], start=i == 0, stop=i == min(j, NT - 1))
                    mm.then_inc(s_ct, 1)
                    pe.wait_ge(s_ow, 1)
                    pe.matmul(ps[0:1, 3, 0:P], owner[:], ident[:], start=True, stop=True).then_inc(s_et, 1)

                @block.scalar
                def _(act):
                    act.wait_ge(s_gp, 1)
                    nc.scalar.activation(sg[:].rearrange("p j e -> p (j e)"), ps[:, 0, :], ACT.Exp, scale=-1.0).then_inc(s_ge, 1)
                    for j in range(NT + 2):
                        if j < NT:
                            act.wait_ge(s_gu2, j + 1)
                            wait(act, s_hh2, j - 1)
                            nc.scalar.copy(up[:, j % 2, :], ps[:, 4 + j % 2, FE:2 * FE])
                            nc.scalar.activation(hs[:, j % 2, :], ps[:, 4 + j % 2, 0:FE], ACT.Silu).then_inc(s_si2, 1)
                        if 1 <= j < NT + 1:
                            act.wait_ge(s_ht2, j)
                            wait(act, s_dn2, j - 2)
                            nc.scalar.copy(hT[:, (j - 1) % 2, :], ps[:, 6, 0:P]).then_inc(s_hc2, 1)
                        if j >= 2:
                            act.wait_ge(s_dn2, j - 1)
                            wait(act, s_ya2, j - 3)
                            nc.scalar.copy(ysh[:, j % 2, :], ps[:, 7, 0:D]).then_inc(s_yc2, 1)

                @block.gpsimd
                def _(pool):
                    for j in range(NT + 1):
                        if j < NT:
                            pool.wait_ge(s_si2, j + 1)
                            wait(pool, s_ht2, j - 1)
                            nc.gpsimd.tensor_tensor(hh[:, j % 2, :], hs[:, j % 2, :], up[:, j % 2, :], ALU.mult).then_inc(s_hh2, 1)
                        if j >= 1:
                            pool.wait_ge(s_yc2, j)
                            nc.gpsimd.tensor_tensor(xt[:, j - 1, :], xt[:, j - 1, :], ysh[:, (j - 1) % 2, :], ALU.add).then_inc(s_ya2, 1)
                    pool.wait_ge(s_ya2, NT)

                @block.vector
                def _(dve):
                    dve.wait_ge(s_w, n_w)
                    nc.vector.tensor_copy(before[:], c_before[:])
                    for u in range(2):
                        nc.vector.tensor_copy(tok[:, u, :, 0:4], c_tok[:].rearrange("p (j x) -> p j x", x=4))
                    nc.vector.memset(allone[:], 1.0)
                    nc.vector.memset(ones[:], 1.0)
                    nc.vector.memset(unit[:], 1.0)
                    dve.wait_ge(s_ge, 1)
                    nc.vector.tensor_scalar(sg[:], sg[:], 1.0, None, ALU.add)
                    dve.drain()
                    nc.vector.reciprocal(sg[:], sg[:])
                    dve.drain()
                    nc.vector.tensor_tensor(sc[:], sg[:], bc(gb[:], 1, NT), ALU.add)
                    dve.drain()
                    x8 = sc[:].rearrange("p j (g x) -> p (j g) x", x=8)
                    nc.vector.tensor_tensor(hi[:, :, 0:4], x8[:, :, 0:4], x8[:, :, 4:8], ALU.max)
                    nc.vector.tensor_tensor(lo[:, :, 0:4], x8[:, :, 0:4], x8[:, :, 4:8], ALU.min)
                    for a_, w in ((0, 2), (4, 1)):
                        l, r_, o = slice(a_, a_ + w), slice(a_ + w, a_ + 2 * w), slice(a_ + 2 * w, a_ + 3 * w)
                        dve.drain()
                        nc.vector.tensor_tensor(hi[:, :, o], hi[:, :, l], hi[:, :, r_], ALU.max)
                        nc.vector.tensor_tensor(lo[:, :, o], hi[:, :, l], hi[:, :, r_], ALU.min)
                        nc.vector.tensor_tensor(losers[:, :, 0:w], lo[:, :, l], lo[:, :, r_], ALU.max)
                        dve.drain()
                        nc.vector.tensor_tensor(lo[:, :, o], lo[:, :, o], losers[:, :, 0:w], ALU.max)
                    dve.drain()
                    nc.vector.tensor_tensor(gs[:].rearrange("p j g -> p (j g)"), hi[:, :, 6], lo[:, :, 6], ALU.add)
                    dve.drain()
                    nc.vector.tensor_tensor(cmp[:], bc(gs[:], 2, G), bc(gs[:], 3, G), ALU.is_gt)
                    nc.vector.tensor_tensor(eq[:], bc(gs[:], 2, G), bc(gs[:], 3, G), ALU.is_equal)
                    dve.drain()
                    nc.vector.tensor_tensor(eq[:].rearrange("p j g h -> p j (g h)"), eq[:].rearrange("p j g h -> p j (g h)"),
                                            bc(c_lt[:], 1, NT), ALU.mult)
                    dve.drain()
                    nc.vector.tensor_tensor(cmp[:], cmp[:], eq[:], ALU.add)
                    dve.drain()
                    nc.vector.tensor_reduce(gmask[:], cmp[:].rearrange("p j g h -> p (j g) h"), AX, ALU.add)
                    dve.drain()
                    nc.vector.tensor_scalar(gmask[:], gmask[:], float(TG), None, ALU.is_lt)
                    dve.drain()
                    nc.vector.tensor_scalar(goff[:], gmask[:], BIG, -BIG, ALU.mult, ALU.add)
                    sc8 = sc[:].rearrange("p j (g x) -> p (j g) x", x=8)
                    nc.vector.tensor_tensor(sc8, sc8, bc(gmask[:], 2, 8), ALU.mult)
                    dve.drain()
                    nc.vector.tensor_tensor(sc8, sc8, bc(goff[:], 2, 8), ALU.add)
                    dve.drain()
                    for j in range(NT):
                        nc.vector.max(top[:, j, :], sc[:, j, :])
                    dve.drain()
                    for j in range(NT):
                        nc.vector.match_replace(out=rep[:, j, :], in_to_replace=top[:, j, :], in_values=sc[:, j, :], imm_value=-3.0 * BIG)
                    dve.drain()
                    nc.vector.tensor_tensor(rep[:], rep[:], sc[:], ALU.not_equal)
                    dve.drain()
                    nc.vector.tensor_copy(chb[:], rep[:]).then_inc(s_ch, 1)
                    nc.vector.tensor_tensor(cwt[:], sg[:], rep[:], ALU.mult)
                    dve.drain()
                    nc.vector.tensor_reduce(tot[:], cwt[:], AX, ALU.add)
                    dve.drain()
                    nc.vector.tensor_scalar(tot[:], tot[:], 1e-20, None, ALU.add)
                    dve.drain()
                    nc.vector.reciprocal(tot[:], tot[:])
                    dve.drain()
                    nc.vector.tensor_scalar(tot[:], tot[:], 2.5, None, ALU.mult)
                    dve.drain()
                    nc.vector.tensor_tensor(cwt[:], cwt[:], bc(tot[:], 2, E), ALU.mult)
                    nc.vector.tensor_tensor_scan(rank[:].rearrange("p j e -> p (j e)"), allone[:],
                                                 rep[:].rearrange("p j e -> p (j e)"), 0.0, ALU.mult, ALU.add)
                    dve.drain()
                    nc.vector.tensor_tensor(tab[:, :, :, 0], rank[:], bc(c_past[:], 2, E), ALU.subtract)
                    nc.vector.tensor_copy(tab[:, :, :, 1], cwt[:])
                    dve.drain()
                    nc.vector.tensor_tensor(rest[:], cwt[:], tab[:, :, :, 1], ALU.subtract)
                    dve.drain()
                    nc.vector.tensor_copy(tab[:, :, :, 2], rest[:])
                    dve.drain()
                    nc.vector.tensor_tensor(rest[:], rest[:], tab[:, :, :, 2], ALU.subtract)
                    dve.drain()
                    nc.vector.tensor_copy(tab[:, :, :, 3], rest[:])
                    dve.wait_ge(s_ct, 1)
                    cnt = cmp[:].rearrange("p j g h -> p (j g) h")
                    nc.vector.tensor_tensor(cnt, bc(ps[:, 2, 0:E], 2, 8), bc(c_first[:, 0:8], 1, E), ALU.is_gt)
                    dve.drain()
                    nc.vector.tensor_reduce(tiles[:], cnt, AX, ALU.add)
                    dve.drain()
                    nc.vector.tensor_tensor_scan(through[:], unit[:], tiles[:], 0.0, ALU.mult, ALU.add)
                    dve.drain()
                    nc.vector.tensor_tensor(first[:], through[:], tiles[:], ALU.subtract)
                    nc.vector.tensor_scalar(unit[:], through[:], c_col[:, 0:1], None, ALU.is_le)
                    nc.vector.tensor_scalar(tripf[:], through[0:1, E - 1:E], float(3 - T * 8 // P), None, ALU.add)
                    dve.drain()
                    nc.vector.tensor_reduce(owner[:], unit[:], AX, ALU.add)
                    nc.vector.tensor_copy(trip[:], tripf[:])
                    nc.vector.tensor_scalar(first[:], first[:], float(P), 1.0, ALU.mult, ALU.add)
                    dve.drain()
                    nc.vector.tensor_scalar(owner[:], owner[:], float(E - 1), None, ALU.min).then_inc(s_ow, 1)
                    nc.vector.tensor_scalar(trip[:], trip[:], 2, None, ALU.arith_shift_right)
                    nc.vector.tensor_tensor(slot1[:], ps[:, 1, :].rearrange("p (j e) -> p j e", e=E), bc(first[:], 1, NT), ALU.add)
                    dve.drain()
                    nc.vector.tensor_tensor(slot1[:], slot1[:], rep[:], ALU.mult)
                    dve.wait_ge(s_et, 1)
                    nc.vector.tensor_copy(etab[:], ps[0:1, 3, 0:P])

            oh = own("oh", [P, 2, NT, P], BF16)
            idx = own("idx", [P, 4], I32)
            held = own("held", [1, 1])
            xg = own("xg", [P, 4, D])
            xgT = own("xgT", [P, 2, DH, P])
            wgu = own("wgu", [P, 4, DH * 2 * FE])
            wdn = own("wdn", [P, 4, D])
            rowf = own("rowf", [P, P])
            wslot = own("wslot", [P, P])
            row = own("row", [P, 4], I32)
            ysb = own("ysb", [P, 4, D])
            s_held = sem("tile_gather_may_start")
            s_oh = sem("tile_onehot")
            s_ix = sem("tile_index_product")
            s_ic = sem("tile_index_ready")
            s_rw = sem("tile_result_rows_ready")
            s_ga = [sem(f"tile_gathered{m}") for m in range(4)]
            s_xt = sem("tile_rows_transposed")
            s_xc = sem("tile_rowsT_copied")
            s_wl = [sem(f"tile_expert_loaded{m}") for m in range(4)]
            s_wd = [sem(f"tile_down_loaded{m}") for m in range(4)]
            s_gu = sem("tile_gate_up")
            s_si = sem("tile_silu")
            s_hh = sem("tile_hidden")
            s_ht = sem("tile_hidden_transposed")
            s_hc = sem("tile_hiddenT_copied")
            s_dn = sem("tile_down")
            s_yc = sem("tile_result_copied")
            s_ys = [sem(f"tile_stored{m}") for m in range(4)]
            PEEL = 12
            LAG = 9

            def run(eng, step):
                fours = LEAST + eng.value_load(trip[0:1, 0:1], min_val=0, max_val=MOST - LEAST)
                for n in range(PEEL):
                    step(n, n % 4, n // 4, lambda k, n=n: n >= k)
                with eng.Fori(PEEL // 4, fours) as g:
                    for m in range(4):
                        step(g * 4 + m, m, g, lambda k: True)
                for r in range(LAG):
                    step(fours * 4 + r, r % 4, fours + r // 4, lambda k, r=r: k > r)

            def slots(m, k):
                return (m - k) % 4, (m - k) % 2

            def round_of(g, m, k):
                return g - (k - m + 3) // 4 if k > m else g

            with nc.Block(no_gpsimd_drain=True) as block:
                @block.tensor
                def _(pe):
                    def step(n, m, g, live):
                        if live(5):
                            k, (a4, a2) = n - 5, slots(m, 5)
                            pe.wait_ge(s_ga[a4], (round_of(g, m, 5) + 1) * 16)
                            for h in range(DH):
                                mm = pe.transpose(ps[:, a2, h * P:(h + 1) * P], xg[:, a4, h * P:(h + 1) * P], ident[:])
                            mm.then_inc(s_xt, 1)
                        if live(6):
                            k, (a4, a2) = n - 6, slots(m, 6)
                            pe.wait_ge(s_xc, k + 1)
                            pe.wait_ge(s_wl[a4], (round_of(g, m, 6) + 1) * 16)
                            for h in range(DH):
                                mm = pe.matmul(ps[:, 2 + a2, 0:2 * FE], xgT[:, a2, h, :], wgu[:, a4, h * 2 * FE:(h + 1) * 2 * FE], start=h == 0, stop=h == DH - 1)
                            mm.then_inc(s_gu, 1)
                        if live(8):
                            k, (a4, a2) = n - 8, slots(m, 8)
                            pe.wait_ge(s_hc, k + 1)
                            pe.wait_ge(s_wd[a4], (round_of(g, m, 8) + 1) * 16)
                            wait(pe, s_yc, k - 1)
                            pe.matmul(ps[:, 5 + a2, 0:D], hT[:, a2, :], wdn[:, a4, :], start=True, stop=True).then_inc(s_dn, 1)
                        if live(7):
                            k, (a4, a2) = n - 7, slots(m, 7)
                            pe.wait_ge(s_hh, k + 1)
                            pe.transpose(ps[:, 4, 0:P], hh[:, a2, :], ident[:]).then_inc(s_ht, 1)
                        if live(1):
                            k, (a4, a2) = n - 1, slots(m, 1)
                            if isinstance(k, int) and k < 2:
                                pe.wait_ge(s_oh, k + 1)
                            wait(pe, s_ic, k)
                            for j in range(NT):
                                mm = pe.matmul(ps[:, 7, 8 * a4:8 * a4 + 8], oh[:, a2, j, :], tok[:, a2, j, :], start=j == 0, stop=j == NT - 1)
                            mm.then_inc(s_ix, 1)
                    run(pe, step)

                @block.vector
                def _(dve):
                    def step(n, m, g, live):
                        if live(8):
                            k, (a4, a2) = n - 8, slots(m, 8)
                            if not (isinstance(k, int) and k < 4):
                                dve.wait_ge(s_ys[a4], round_of(g, m, 8) * 16)
                            nc.vector.tensor_tensor(row[:, a4:a4 + 1], rowf[:, ds(k, 1)], c_spare[:, ds(k, 1)], ALU.max).then_inc(s_rw, 1)
                        if live(2):
                            k, (a4, a2) = n - 2, slots(m, 2)
                            dve.wait_ge(s_ix, k + 1)
                            o = 8 * a4
                            nc.vector.tensor_reduce(wslot[:, ds(k, 1)], ps[:, 7, o + 5:o + 8], AX, ALU.add)
                            nc.vector.tensor_reduce(rowf[:, ds(k, 1)], ps[:, 7, o + 2:o + 5], AX, ALU.add)
                            with nc.allow_low_precision("whole numbers below 1024"):
                                nc.vector.tensor_reduce(idx[:, a4:a4 + 1], ps[:, 7, o:o + 2], AX, ALU.add).then_inc(s_ic, 1)
                        if live(0):
                            e = dve.value_load(etab[0:1, ds(n, 1)], min_val=0, max_val=E - 1)
                            nc.vector.tensor_copy(tok[:, m % 2, :, 4:8].unsqueeze(2), tab[:, :, ds(e, 1), :])
                            nc.vector.scalar_tensor_tensor(oh[:, m % 2, :, :], slot1[:, :, ds(e, 1)].broadcast_to([P, NT, P]),
                                                           c_next[:, ds(n, 1)], bc(c_iota[:], 1, NT), ALU.subtract, ALU.is_equal
                                                           ).then_inc(s_oh, 1)
                        if live(6):
                            k, (a4, a2) = n - 6, slots(m, 6)
                            dve.wait_ge(s_si, k + 1)
                            nc.vector.scalar_tensor_tensor(hh[:, a2, :], hs[:, a2, :], wslot[:, ds(k, 1)], ps[:, 2 + a2, FE:2 * FE],
                                                           ALU.mult, ALU.mult).then_inc(s_hh, 1)
                    run(dve, step)

                @block.scalar
                def _(act):
                    def step(n, m, g, live):
                        if live(5):
                            k, (a4, a2) = n - 5, slots(m, 5)
                            act.wait_ge(s_xt, k + 1)
                            nc.scalar.copy(xgT[:, a2, :, :], ps[:, a2, 0:D].rearrange("p (h t) -> p h t", h=DH)).then_inc(s_xc, 1)
                        if live(6):
                            k, (a4, a2) = n - 6, slots(m, 6)
                            act.wait_ge(s_gu, k + 1)
                            nc.scalar.activation(hs[:, a2, :], ps[:, 2 + a2, 0:FE], ACT.Silu).then_inc(s_si, 1)
                        if live(8):
                            k, (a4, a2) = n - 8, slots(m, 8)
                            act.wait_ge(s_dn, k + 1)
                            if not (isinstance(k, int) and k < 4):
                                act.wait_ge(s_ys[a4], round_of(g, m, 8) * 16)
                            nc.scalar.copy(ysb[:, a4, :], ps[:, 5 + a2, 0:D]).then_inc(s_yc, 1)
                        if live(7):
                            k, (a4, a2) = n - 7, slots(m, 7)
                            act.wait_ge(s_ht, k + 1)
                            nc.scalar.copy(hT[:, a2, :], ps[:, 4, 0:P]).then_inc(s_hc, 1)
                    run(act, step)

                @block.gpsimd
                def _(pool):
                    pool.wait_ge(s_rows, 16)

                    def step(n, m, g, live):
                        if live(2):
                            pool.wait_ge(s_ic, n - 1)
                        if live(9):
                            pool.wait_ge(s_yc, n - 8)
                            pool.wait_ge(s_rw, n - 8)
                        if live(2) or live(9):
                            wait(pool, s_held, n - 2)
                            nc.gpsimd.tensor_tensor(held[:], ident[0:1, 0:1], ident[0:1, 0:1], ALU.mult).then_inc(s_held, 1)
                        if live(2):
                            a4, a2 = slots(m, 2)
                            nc.gpsimd.indirect_dma_start(out=xg[:, a4, :], out_offset=None, in_=xn_rows,
                                                         in_offset=bass.IndirectOffsetOnAxis(ap=idx[:, a4:a4 + 1], axis=0)
                                                         ).then_inc(s_ga[a4], 16)
                        if live(9):
                            a4, a2 = slots(m, 9)
                            nc.gpsimd.indirect_dma_start(out=y_rows, out_offset=bass.IndirectOffsetOnAxis(ap=row[:, a4:a4 + 1], axis=0),
                                                         in_=ysb[:, a4, :], in_offset=None).then_inc(s_ys[a4], 16)
                    run(pool, step)

                @block.sync
                def _(sp):
                    def step(n, m, g, live):
                        if live(0):
                            e = sp.value_load(etab[0:1, ds(n, 1)], min_val=0, max_val=E - 1)
                            wait(sp, s_gu, n - 3)
                            sp.dma_start(wgu[:, m, :], a["moe_gate_up"][ds(e, 1), :, :].rearrange("o p f -> p (o f)")).then_inc(s_wl[m], 16)
                            wait(sp, s_dn, n - 3)
                            sp.dma_start(wdn[:, m, :], a["L1_ffn_We_down"][ds(e, 1), :, :].rearrange("o p f -> p (o f)")).then_inc(s_wd[m], 16)
                    run(sp, step)

            RING = 3
            yg = own("yg", [P, RING, 8 * D])
            ysum = own("ysum", [P, D])
            s_yg = [sem(f"moe_collected{r}") for r in range(RING)]
            s_ya = sem("moe_result_added")
            with nc.Block(no_gpsimd_drain=True) as block:
                @block.sync
                def _(sp):
                    fours = LEAST + sp.value_load(trip[0:1, 0:1], min_val=0, max_val=MOST - LEAST)
                    for m in range(4):
                        sp.wait_ge(s_ys[m], fours * 16)
                    for j in range(NT):
                        wait(sp, s_ya, j - RING + 1)
                        sp.dma_start(yg[:, j % RING, :], y_rows[P * P + j * 8 * P:P * P + (j + 1) * 8 * P, :].rearrange("(p k) d -> p (k d)", k=8)
                                     ).then_inc(s_yg[j % RING], 16)

                @block.scalar
                def _(act):
                    for j in range(NT):
                        act.wait_ge(s_ya, j + 1)
                        act.dma_start(out.rearrange("(j b) s d -> j (b s) d", b=2)[j], xt[:, j, :]).then_inc(s_out, 16)
                    act.wait_ge(s_out, 16 * NT)

                @block.vector
                def _(dve):
                    for j in range(NT):
                        dve.wait_ge(s_yg[j % RING], 16 * (j // RING + 1))
                        nc.vector.tensor_reduce(ysum[:], yg[:, j % RING, :].rearrange("p (k d) -> p d k", k=8), AX, ALU.add)
                        dve.drain()
                        nc.vector.tensor_tensor(xt[:, j, :], xt[:, j, :], ysum[:], ALU.add).then_inc(s_ya, 1)
                        dve.drain()
            st.close()

        with nc.Block(no_gpsimd_drain=True) as block:
            @block.sync
            def _(sp):
                sp.dma_start(xt[:], a["x"].rearrange("(j b) s d -> (b s) j d", b=2)).then_inc(s_x, 16)
                sp.dma_start(ident[:], a["c_ident"]).then_inc(s_const, 16)

            @block.vector
            def _(dve):
                nc.vector.memset(neghalf[:], -0.5)

            @block.tensor
            def _(pe):
                pe.wait_ge(s_const, 16)

        cross_attention("x0", weights_x0, True)
        latent_and_ffn()
        cross_attention("x1", weights_x1, False)
        state_space()
        experts()


def _constants():
    f = np.float32
    c = {"c_ident": np.eye(P, dtype=f)}
    r = np.arange(P)
    c["c_blockdiag"] = (r[:, None] // HD0 == r[None, :] // HD0).astype(f)
    c["c_head"] = (r[:, None] // HD0 == np.arange(8)[None, :]).astype(f)
    c["c_causal"] = np.where(np.arange(S)[None, :] <= (r % S)[:, None], 0.0, -BIG).astype(f)
    pos = np.arange(S, dtype=f)[:, None]
    ang = pos * np.exp(np.arange(0, 32, 2, dtype=f) * f(-math.log(10000.0) / 32))
    table = np.zeros((S, 32), f)
    table[:, 0::2], table[:, 1::2] = np.sin(ang), np.cos(ang)
    same = r[:, None] // S == r[None, :] // S
    tr, tc = (r % S)[:, None], (r % S)[None, :]
    seg, lvl = [], []
    for l in range(LV):
        w = 32 >> l
        mid = tc // (2 * w) * 2 * w + w - 1
        right = tc > mid
        seg.append(same & np.where(right, (tr > mid) & (tr <= tc), (tr > tc) & (tr <= mid)))
        lvl.append((tr // (2 * w) == tc // (2 * w)) & (tr % (2 * w) < w) & (tc % (2 * w) >= w))
    lvl.append(tr == tc)
    c["c_segments"] = np.concatenate(seg, 1).astype(f)
    c["c_levels"] = np.concatenate([v[:, :S] for v in lvl], 1).astype(f)
    c["c_lower"] = np.tile((np.arange(G)[None, :] < np.arange(G)[:, None]).astype(f).reshape(1, -1), (P, 1))
    c["c_iota"] = np.tile(np.arange(P, dtype=f), (P, 1))
    c["c_first"] = np.tile(np.arange(P, dtype=f) * P, (P, 1))
    c["c_next"] = c["c_first"] + f(1)
    c["c_col"] = r.astype(f)[:, None].copy()
    c["c_before"] = (r[:, None] < r[None, :]).astype(f)
    tile, row = np.broadcast_to(np.arange(NT), (P, NT)), np.broadcast_to(r[:, None], (P, NT))
    c["c_tok"] = np.stack([tile * P, row, P * P + tile * P * 8, row * 8], 2).reshape(P, 4 * NT).astype(f)
    c["c_past"] = (tile * 8 + 1).astype(f)
    c["c_spare"] = (np.arange(P)[None, :] * P + r[:, None]).astype(f)
    c["c_positions"] = np.ascontiguousarray(table.T)
    return c


def _arrays(inputs):
    t = {k: np.ascontiguousarray(v) for k, v in inputs.items()}
    lay = {}

    def column(v):
        return np.ascontiguousarray(v.reshape(-1, P).T)

    def T_(name, new):
        lay[new] = np.ascontiguousarray(np.swapaxes(t[name], -1, -2))

    for n in ("x", "ctx_1024", "mask_BxS_ik1", "L0_xattn_Wk", "L0_xattn_bfc"):
        lay[n] = t[n]
    for n in ("L0_xattn_bq", "L0_xattn_bk", "L0_xattn_bv"):
        lay[n] = column(t[n])
    lay["mask_col"] = column(t["mask_BxS_ik1"])
    for n in ("L0_attn_W_QR", "L0_attn_q_norm_w", "L0_attn_k_norm_w", "L0_ffn_b",
              "L1_xattn_Wq", "L1_xattn_Wv", "L1_xattn_bv"):
        lay[n] = t[n]
    T_("L0_ffn_tile_sigs", "L0_ffn_sigsT")
    for n in ("L0_attn_W_DQ", "L0_attn_W_DKV", "L0_attn_W_KR"):
        lay[n + "8"] = np.tile(t[n], (1, 8))
    lay["L0_ffn_WT"] = np.ascontiguousarray(np.swapaxes(t["L0_ffn_W"], 1, 2)).reshape(NTILE * D, D)
    for n in ("L1_xattn_bq", "L1_xattn_bk"):
        lay[n] = column(t[n])
    for n in ("L0_xattn_Wq", "L0_xattn_Wv", "L0_xattn_Wfc", "L0_attn_W_UQ", "L0_attn_W_UKV", "L0_attn_W_O", "L1_xattn_Wk"):
        T_(n, n + "T")
    w_in = t["L1_attn_W_in"].T
    heads = w_in[:, 2 * NH * DS:].reshape(D, NH, 2 * DS + 1)
    lay["L1_attn_W_inT"] = np.ascontiguousarray(np.concatenate(
        [w_in[:, :2 * NH * DS], heads[:, :, :DS].reshape(D, -1), heads[:, :, DS:2 * DS].reshape(D, -1)], 1))
    lay["L1_attn_W_dtT"] = np.ascontiguousarray(heads[:, :, 2 * DS])
    lay["L1_attn_conv"] = np.ascontiguousarray(t["L1_attn_conv_w"].reshape(CI, P, 4).transpose(1, 0, 2)).reshape(P, CI * 4)
    lay["L1_attn_conv_b"] = column(t["L1_attn_conv_b"])
    lay["L1_attn_A_log"] = column(t["L1_attn_A_log"].reshape(-1))
    lay["L1_attn_D2"] = np.ascontiguousarray(t["L1_attn_D"].reshape(CI, 2).T)
    lay["L1_attn_dt_bias"] = t["L1_attn_dt_bias"]
    T_("L1_attn_W_out", "L1_attn_W_outT")
    T_("L1_ffn_gate_w", "L1_ffn_gate_wT")
    lay["L1_ffn_gate_bias"] = t["L1_ffn_gate_bias"]
    gate_up = np.concatenate([t["L1_ffn_We_gate"], t["L1_ffn_We_up"]], 2).reshape(E, DH, P, 2 * FE)
    lay["moe_gate_up"] = np.ascontiguousarray(gate_up.swapaxes(1, 2)).reshape(E, P, DH * 2 * FE)
    lay["L1_ffn_We_down"] = t["L1_ffn_We_down"]
    lay["moe_shared_gu"] = np.concatenate([t["L1_ffn_Ws_gate"], t["L1_ffn_Ws_up"]], 1)
    lay["L1_ffn_Ws_down"] = t["L1_ffn_Ws_down"]
    lay["ctx_T"] = np.ascontiguousarray(np.swapaxes(t["ctx_1024"], 1, 2)).reshape(B * DH, P, NK)
    lay.update(_constants())
    return lay


def kernel(**inputs):
    from concourse import bacc
    from concourse.bass_utils import run_bass_kernel_spmd

    nc = bacc.Bacc("TRN2", target_bir_lowering=False, num_devices=1)
    arrays = _arrays(inputs)
    args = {k: nc.dram_tensor(k, v.shape, mybir.dt.from_np(v.dtype), kind="ExternalInput").ap() for k, v in arrays.items()}
    out = nc.dram_tensor("out", (B, S, D), F32, kind="ExternalOutput").ap()
    perceiver(nc, args, out)
    r = run_bass_kernel_spmd(nc, [arrays], core_ids=[0])
    return r.results[0]["out"]
```
